# Optimizing a Trainium2 kernel written in Bass

```python
import numpy as np
import jax
import jax.numpy as jnp

def _softmax(x, axis=-1):
    return jax.nn.softmax(x, axis=axis)

def _gelu(x):
    return jax.nn.gelu(x, approximate=True)

def _silu(x):
    return jax.nn.silu(x)

def _sigmoid(x):
    return jax.nn.sigmoid(x)

def _layernorm(x, axis=-1, eps=1e-05):
    m = jnp.mean(x, axis=axis, keepdims=True)
    v = jnp.var(x, axis=axis, keepdims=True)
    return (x - m) / jnp.sqrt(v + eps)

def _scatter_add(tgt, idx, src, axis=0):
    return tgt.at[idx].add(src)

def _segment_sum(src, seg, n):
    return jax.ops.segment_sum(src, seg, n)
kernel_name = 'mk_recurrent_d4_jaxref_r8_25fbdb'

def setup_inputs(seed: int=0):
    np.random.seed(seed)
    _w = jnp.asarray

    def _L0_attn_setup():
        import jax, jax.numpy as jnp
        import numpy as np
        N_INPUT = 128
        N_HEAD = 16
        ATT_DIM = N_INPUT // N_HEAD * N_HEAD
        V_DIM = N_INPUT // 2 * N_HEAD
        COMB_DIM = 2 * ATT_DIM + V_DIM
        SCALE = (N_INPUT // N_HEAD) ** 0.5
        key = jax.random.key(seed)
        k1, k2, k3 = jax.random.split(key, 3)
        B, T = (8, 128)
        representations = jax.random.normal(k1, (B, T, N_INPUT), dtype=jnp.float32)
        Wc = jax.random.normal(k2, (COMB_DIM, N_INPUT), dtype=jnp.float32) * (0.1 * np.sqrt(2.0 / (COMB_DIM + N_INPUT)))
        bc = jnp.zeros((COMB_DIM,), dtype=jnp.float32)
        Wo = jax.random.normal(k3, (N_INPUT, V_DIM), dtype=jnp.float32) * (0.1 * np.sqrt(2.0 / (N_INPUT + V_DIM)))
        bo = jnp.zeros((N_INPUT,), dtype=jnp.float32)
        return {'representations': representations, 'Wc': Wc, 'bc': bc, 'Wo': Wo, 'bo': bo}
    _L0_attn_in = _L0_attn_setup()

    def _L0_ffn_setup():
        import jax, jax.numpy as jnp
        import numpy as np
        B, S, D, F, E, K = (2, 256, 128, 256, 8, 2)
        key = jax.random.key(seed)
        ks = jax.random.split(key, 5)
        scale = 0.02
        return {'x': jax.random.normal(ks[0], (B, S, D), dtype=jnp.float32), 'Wg': jax.random.normal(ks[1], (E, D), dtype=jnp.float32) * scale, 'W1': jax.random.normal(ks[2], (E, F, D), dtype=jnp.float32) * scale, 'W2': jax.random.normal(ks[3], (E, F, D), dtype=jnp.float32) * scale, 'W3': jax.random.normal(ks[4], (E, D, F), dtype=jnp.float32) * scale}
    _L0_ffn_in = _L0_ffn_setup()

    def _L1_attn_setup():
        import jax, jax.numpy as jnp
        import numpy as np
        BATCH, SEQ, D_MODEL, STATE_DIM = (8, 256, 128, 128)

        def _cayley_circulant_eigenvalues(a_params, n):
            half_n = n // 2
            a_full = jnp.zeros((n,), dtype=a_params.dtype)
            a_full = a_full.at[1:half_n].set(a_params[:half_n - 1])
            a_full = a_full.at[half_n + 1:].set(-a_params[:half_n - 1][::-1])
            omega = jnp.fft.fft(a_full).imag
            w2 = omega * omega
            denom = 1.0 + w2
            return ((1.0 - w2) / denom + 1j * (-2.0 * omega / denom)).astype(jnp.complex64)
        key = jax.random.key(seed)
        k1, k2, k3, k4 = jax.random.split(key, 4)
        u = jax.random.normal(k1, (BATCH, SEQ, D_MODEL), dtype=jnp.float32)
        a_params = jax.random.normal(k2, (STATE_DIM // 2,), dtype=jnp.float32) * 0.1
        B_w = jax.random.normal(k3, (STATE_DIM, D_MODEL), dtype=jnp.float32) / np.sqrt(D_MODEL).astype(np.float32)
        C_w = jax.random.normal(k4, (D_MODEL, STATE_DIM), dtype=jnp.float32) / np.sqrt(STATE_DIM).astype(np.float32)
        D = jnp.zeros((D_MODEL,), dtype=jnp.float32)
        return {'u': u, 'a_params': a_params, 'B_w': B_w, 'C_w': C_w, 'D': D}
    _L1_attn_in = _L1_attn_setup()

    def _L1_ffn_setup():
        import jax, jax.numpy as jnp
        import numpy as np
        TOP_K = 2
        NUM_EXPERTS = 8
        DIM = 128
        HIDDEN = 352
        BS, SLEN = (2, 128)

        def _grouped_ffn(x, w1, w2, w3, counts):
            num_experts = w1.shape[0]
            ends = jnp.cumsum(counts)
            starts = ends - counts
            t = jnp.arange(x.shape[0])
            out = jnp.zeros((x.shape[0], w2.shape[-1]), x.dtype)
            for e in range(num_experts):
                m = ((t >= starts[e]) & (t < ends[e])).astype(x.dtype)[:, None]
                xe = x * m
                h = jax.nn.silu(xe @ w1[e]) * (xe @ w3[e])
                out = out + h @ w2[e] * m
            return out
        key = jax.random.key(seed)
        k = jax.random.split(key, 5)
        std = 0.02
        return {'x': jax.random.normal(k[0], (BS, SLEN, DIM), jnp.float32), 'gate_w': jax.random.normal(k[1], (NUM_EXPERTS, DIM), jnp.float32) * std, 'expert_bias': jnp.zeros((NUM_EXPERTS,), jnp.float32), 'w1': jax.random.normal(k[2], (NUM_EXPERTS, DIM, HIDDEN), jnp.float32) * std, 'w2': jax.random.normal(k[3], (NUM_EXPERTS, HIDDEN, DIM), jnp.float32) * std, 'w3': jax.random.normal(k[4], (NUM_EXPERTS, DIM, HIDDEN), jnp.float32) * std}
    _L1_ffn_in = _L1_ffn_setup()

    def _L2_attn_setup():
        import jax, jax.numpy as jnp
        import numpy as np
        N_HEADS = 16
        SCALE = 8.0
        key = jax.random.key(seed)
        k1, k2, k3, k4 = jax.random.split(key, 4)
        b, n, d_model, inner = (8, 256, 128, 128)
        x = jax.random.normal(k1, (b, n, d_model), dtype=jnp.float32)
        Wqkv = jax.random.normal(k2, (3 * inner, d_model), dtype=jnp.float32) * (1.0 / np.sqrt(d_model))
        Wproj = jax.random.normal(k3, (d_model, inner), dtype=jnp.float32) * (1.0 / np.sqrt(inner))
        bproj = jax.random.normal(k4, (d_model,), dtype=jnp.float32) * 0.01
        return {'x': x, 'Wqkv': Wqkv, 'Wproj': Wproj, 'bproj': bproj}
    _L2_attn_in = _L2_attn_setup()

    def _L2_ffn_setup():
        import math
        import jax, jax.numpy as jnp
        import numpy as np
        D_CONTENT = 128
        D_POSITION = 32
        NUM_TILES = 8
        BATCH = 8
        SEQ = 256

        def make_pe(seq_len, d_pos):
            pos = jnp.arange(seq_len, dtype=jnp.float32)[:, None]
            div = jnp.exp(jnp.arange(0, d_pos, 2, dtype=jnp.float32) * (-math.log(10000.0) / d_pos))
            ang = pos * div
            pe = jnp.zeros((seq_len, d_pos), dtype=jnp.float32)
            pe = pe.at[:, 0::2].set(jnp.sin(ang))
            pe = pe.at[:, 1::2].set(jnp.cos(ang))
            return pe
        key = jax.random.key(seed)
        k1, k2, k3, k4 = jax.random.split(key, 4)
        x = jax.random.normal(k1, (BATCH, SEQ, D_CONTENT), dtype=jnp.float32)
        tile_sigs = jax.random.normal(k2, (NUM_TILES, D_POSITION), dtype=jnp.float32)
        lim = 1.0 / math.sqrt(D_CONTENT)
        W = jax.random.uniform(k3, (NUM_TILES, D_CONTENT, D_CONTENT), minval=-lim, maxval=lim, dtype=jnp.float32)
        b = jax.random.uniform(k4, (NUM_TILES, D_CONTENT), minval=-lim, maxval=lim, dtype=jnp.float32)
        return {'x': x, 'tile_sigs': tile_sigs, 'W': W, 'b': b}
    _L2_ffn_in = _L2_ffn_setup()

    def _L3_attn_setup():
        import jax, jax.numpy as jnp
        import numpy as np
        GAMMA = 0.96875
        H = 128
        B = 4
        L = 256
        key = jax.random.key(seed)
        k0, k1, k2, k3, k4 = jax.random.split(key, 5)
        x = jax.random.normal(k0, (B, L, H), dtype=jnp.float32)
        weight_q = jax.random.normal(k1, (H, H), dtype=jnp.float32) / H
        weight_k = jax.random.normal(k2, (H, H), dtype=jnp.float32) / H
        weight_v = jax.random.normal(k3, (H, H), dtype=jnp.float32) / H
        theta = jax.random.normal(k4, (H,), dtype=jnp.float32) / H
        return {'x': x, 'weight_q': weight_q, 'weight_k': weight_k, 'weight_v': weight_v, 'theta': theta}
    _L3_attn_in = _L3_attn_setup()

    def _L3_ffn_setup():
        import jax, jax.numpy as jnp
        import numpy as np
        D_MODEL = 128
        D_HIDDEN = 512
        NUM_EXPERTS = 8
        B, T = (2, 256)
        key = jax.random.key(seed)
        ks = jax.random.split(key, 8)
        s = 0.02
        x = jax.random.normal(ks[0], (B, T, D_MODEL), dtype=jnp.float32)
        Wg = jax.random.normal(ks[1], (D_MODEL, NUM_EXPERTS), dtype=jnp.float32) * s
        bg = jnp.zeros((NUM_EXPERTS,), dtype=jnp.float32)
        W1 = jax.random.normal(ks[2], (NUM_EXPERTS, D_MODEL, D_HIDDEN), dtype=jnp.float32) * s
        b1 = jnp.zeros((NUM_EXPERTS, D_HIDDEN), dtype=jnp.float32)
        W2 = jax.random.normal(ks[3], (NUM_EXPERTS, D_HIDDEN, D_MODEL), dtype=jnp.float32) * s
        b2 = jnp.zeros((NUM_EXPERTS, D_MODEL), dtype=jnp.float32)
        return {'x': x, 'Wg': Wg, 'bg': bg, 'W1': W1, 'b1': b1, 'W2': W2, 'b2': b2}
    _L3_ffn_in = _L3_ffn_setup()
    _d = {'L0_attn_representations': _L0_attn_in['representations'], 'L0_attn_Wc': _L0_attn_in['Wc'], 'L0_attn_bc': _L0_attn_in['bc'], 'L0_attn_Wo': _L0_attn_in['Wo'], 'L0_attn_bo': _L0_attn_in['bo'], 'L0_ffn_Wg': _L0_ffn_in['Wg'], 'L0_ffn_W1': _L0_ffn_in['W1'], 'L0_ffn_W2': _L0_ffn_in['W2'], 'L0_ffn_W3': _L0_ffn_in['W3'], 'L1_attn_a_params': _L1_attn_in['a_params'], 'L1_attn_B_w': _L1_attn_in['B_w'], 'L1_attn_C_w': _L1_attn_in['C_w'], 'L1_attn_D': _L1_attn_in['D'], 'L1_ffn_gate_w': _L1_ffn_in['gate_w'], 'L1_ffn_expert_bias': _L1_ffn_in['expert_bias'], 'L1_ffn_w1': _L1_ffn_in['w1'], 'L1_ffn_w2': _L1_ffn_in['w2'], 'L1_ffn_w3': _L1_ffn_in['w3'], 'L2_attn_Wqkv': _L2_attn_in['Wqkv'], 'L2_attn_Wproj': _L2_attn_in['Wproj'], 'L2_attn_bproj': _L2_attn_in['bproj'], 'L2_ffn_tile_sigs': _L2_ffn_in['tile_sigs'], 'L2_ffn_W': _L2_ffn_in['W'], 'L2_ffn_b': _L2_ffn_in['b'], 'L3_attn_weight_q': _L3_attn_in['weight_q'], 'L3_attn_weight_k': _L3_attn_in['weight_k'], 'L3_attn_weight_v': _L3_attn_in['weight_v'], 'L3_attn_theta': _L3_attn_in['theta'], 'L3_ffn_Wg': _L3_ffn_in['Wg'], 'L3_ffn_bg': _L3_ffn_in['bg'], 'L3_ffn_W1': _L3_ffn_in['W1'], 'L3_ffn_b1': _L3_ffn_in['b1'], 'L3_ffn_W2': _L3_ffn_in['W2'], 'L3_ffn_b2': _L3_ffn_in['b2']}
    _x0 = _d['L0_attn_representations']
    _d['L0_attn_representations'] = jax.random.normal(jax.random.fold_in(jax.random.key(seed), 1), (2, 1024, 128), dtype=_x0.dtype)
    del _x0
    return _d

def reference(L0_attn_representations, L0_attn_Wc, L0_attn_bc, L0_attn_Wo, L0_attn_bo, L0_ffn_Wg, L0_ffn_W1, L0_ffn_W2, L0_ffn_W3, L1_attn_a_params, L1_attn_B_w, L1_attn_C_w, L1_attn_D, L1_ffn_gate_w, L1_ffn_expert_bias, L1_ffn_w1, L1_ffn_w2, L1_ffn_w3, L2_attn_Wqkv, L2_attn_Wproj, L2_attn_bproj, L2_ffn_tile_sigs, L2_ffn_W, L2_ffn_b, L3_attn_weight_q, L3_attn_weight_k, L3_attn_weight_v, L3_attn_theta, L3_ffn_Wg, L3_ffn_bg, L3_ffn_W1, L3_ffn_b1, L3_ffn_W2, L3_ffn_b2):

    def _L0_attn_ref(representations, Wc, bc, Wo, bo):
        import jax, jax.numpy as jnp
        import numpy as np
        N_INPUT = 128
        N_HEAD = 16
        ATT_DIM = N_INPUT // N_HEAD * N_HEAD
        V_DIM = N_INPUT // 2 * N_HEAD
        COMB_DIM = 2 * ATT_DIM + V_DIM
        SCALE = (N_INPUT // N_HEAD) ** 0.5
        B, T, D = representations.shape
        H = N_HEAD
        dh = ATT_DIM // H
        dv = V_DIM // H
        cp = jax.nn.leaky_relu(jnp.einsum('btd,cd->btc', representations, Wc) + bc)
        q = cp[..., :ATT_DIM].reshape(B, T, H, dh)
        k = cp[..., ATT_DIM:2 * ATT_DIM].reshape(B, T, H, dh)
        v = cp[..., 2 * ATT_DIM:].reshape(B, T, H, dv)
        scores = jnp.einsum('bqhd,bkhd->bhqk', q, k) / SCALE
        attn = jax.nn.softmax(scores, axis=-1)
        out = jnp.einsum('bhqk,bkhd->bqhd', attn, v).reshape(B, T, V_DIM)
        proj = jax.nn.leaky_relu(jnp.einsum('btv,dv->btd', out, Wo) + bo)
        return representations + proj

    def _L0_ffn_ref(x, Wg, W1, W2, W3):
        import jax, jax.numpy as jnp
        import numpy as np
        B, S, D, F, E, K = (2, 256, 128, 256, 8, 2)
        k = K
        scores = jnp.einsum('bsd,ed->bse', x, Wg)
        topk_scores, topk_idx = jax.lax.top_k(scores, k)
        topk_probs = jax.nn.softmax(topk_scores, axis=-1)
        h1 = jnp.einsum('bsd,efd->bsef', x, W1)
        h2 = jnp.einsum('bsd,efd->bsef', x, W2)
        hidden = jax.nn.silu(h1) * h2
        expert_out = jnp.einsum('bsef,edf->bsed', hidden, W3)
        onehot = jax.nn.one_hot(topk_idx, scores.shape[-1], dtype=x.dtype)
        gating = jnp.einsum('bsk,bske->bse', topk_probs, onehot)
        return jnp.einsum('bse,bsed->bsd', gating, expert_out)

    def _L1_attn_ref(u, a_params, B_w, C_w, D):
        import jax, jax.numpy as jnp
        import numpy as np
        BATCH, SEQ, D_MODEL, STATE_DIM = (8, 256, 128, 128)

        def _cayley_circulant_eigenvalues(a_params, n):
            half_n = n // 2
            a_full = jnp.zeros((n,), dtype=a_params.dtype)
            a_full = a_full.at[1:half_n].set(a_params[:half_n - 1])
            a_full = a_full.at[half_n + 1:].set(-a_params[:half_n - 1][::-1])
            omega = jnp.fft.fft(a_full).imag
            w2 = omega * omega
            denom = 1.0 + w2
            return ((1.0 - w2) / denom + 1j * (-2.0 * omega / denom)).astype(jnp.complex64)
        n = B_w.shape[0]
        lambdas = _cayley_circulant_eigenvalues(a_params, n)
        Bu = jnp.einsum('bsd,nd->bsn', u, B_w)

        def step(h, bu_t):
            Wh = jnp.fft.ifft(lambdas * jnp.fft.fft(h.astype(jnp.float32))).real.astype(h.dtype)
            h_new = Wh + bu_t
            return (h_new, h_new)
        h0 = jnp.zeros((u.shape[0], n), dtype=u.dtype)
        _, hs = jax.lax.scan(step, h0, jnp.swapaxes(Bu, 0, 1))
        y = jnp.einsum('sbn,dn->bsd', hs, C_w) + D * u
        return y

    def _L1_ffn_ref(x, gate_w, expert_bias, w1, w2, w3):
        import jax, jax.numpy as jnp
        import numpy as np
        TOP_K = 2
        NUM_EXPERTS = 8
        DIM = 128
        HIDDEN = 352
        BS, SLEN = (2, 128)

        def _grouped_ffn(x, w1, w2, w3, counts):
            num_experts = w1.shape[0]
            ends = jnp.cumsum(counts)
            starts = ends - counts
            t = jnp.arange(x.shape[0])
            out = jnp.zeros((x.shape[0], w2.shape[-1]), x.dtype)
            for e in range(num_experts):
                m = ((t >= starts[e]) & (t < ends[e])).astype(x.dtype)[:, None]
                xe = x * m
                h = jax.nn.silu(xe @ w1[e]) * (xe @ w3[e])
                out = out + h @ w2[e] * m
            return out
        bs, slen, dim = x.shape
        num_experts = gate_w.shape[0]
        xf = x.reshape(bs * slen, dim)
        scores = jax.nn.softmax((xf @ gate_w.T).astype(jnp.float32), axis=-1)
        _, sel = jax.lax.top_k(scores + expert_bias, TOP_K)
        top_scores = jnp.take_along_axis(scores, sel, axis=1).reshape(-1)
        sel_flat = sel.reshape(-1)
        counts = jnp.zeros((num_experts,), jnp.int32).at[sel_flat].add(1)
        order = jnp.argsort(sel_flat, stable=True)
        top_scores_sorted = top_scores[order]
        token_idx = order // TOP_K
        routed = xf[token_idx] * top_scores_sorted[:, None].astype(xf.dtype)
        routed_out = _grouped_ffn(routed, w1, w2, w3, counts)
        out = jnp.zeros_like(xf).at[token_idx].add(routed_out)
        return out.reshape(bs, slen, dim)

    def _L2_attn_ref(x, Wqkv, Wproj, bproj):
        import jax, jax.numpy as jnp
        import numpy as np
        N_HEADS = 16
        SCALE = 8.0
        b, n, _ = x.shape
        qkv = jnp.einsum('bnm,fm->bnf', x, Wqkv)
        qkv = qkv.reshape(b, n, N_HEADS, -1)
        dh = qkv.shape[3] // 3
        q, k, v = (qkv[..., :dh], qkv[..., dh:2 * dh], qkv[..., 2 * dh:])
        scores = jnp.einsum('bnhd,bngd->bnhg', q, k) / SCALE
        attn = jax.nn.softmax(scores, axis=-1)
        out = jnp.einsum('bnhg,bngd->bnhd', attn, v)
        out = out.reshape(b, n, -1)
        return jnp.einsum('bni,mi->bnm', out, Wproj) + bproj

    def _L2_ffn_ref(x, tile_sigs, W, b):
        import math
        import jax, jax.numpy as jnp
        import numpy as np
        D_CONTENT = 128
        D_POSITION = 32
        NUM_TILES = 8
        BATCH = 8
        SEQ = 256

        def make_pe(seq_len, d_pos):
            pos = jnp.arange(seq_len, dtype=jnp.float32)[:, None]
            div = jnp.exp(jnp.arange(0, d_pos, 2, dtype=jnp.float32) * (-math.log(10000.0) / d_pos))
            ang = pos * div
            pe = jnp.zeros((seq_len, d_pos), dtype=jnp.float32)
            pe = pe.at[:, 0::2].set(jnp.sin(ang))
            pe = pe.at[:, 1::2].set(jnp.cos(ang))
            return pe
        B, S, D = x.shape
        P = tile_sigs.shape[1]
        pe = make_pe(S, P)
        scores = jnp.einsum('sp,tp->st', pe, jnp.sign(tile_sigs))
        idx = jnp.argmax(scores, axis=-1)
        y_all = jnp.einsum('bsd,tod->bsto', x, W) + b
        idx4 = jnp.broadcast_to(idx[None, :, None, None], (B, S, 1, D))
        out = jnp.take_along_axis(y_all, idx4, axis=2)[:, :, 0]
        return out

    def _L3_attn_ref(x, weight_q, weight_k, weight_v, theta):
        import jax, jax.numpy as jnp
        import numpy as np
        GAMMA = 0.96875
        H = 128
        B = 4
        L = 256
        Bb, Ll, Hh = x.shape
        dt = x.dtype
        seq = jnp.arange(1, Ll + 1, dtype=dt)
        zero = jnp.asarray(0.0, dtype=dt)
        thetas = jnp.exp(zero * seq[:, None] * theta[None, :])
        theta_conj = thetas
        q = jnp.matmul(x, weight_q) * thetas[None]
        k = jnp.matmul(x, weight_k) * theta_conj[None]
        v = jnp.matmul(x, weight_v)
        n = jnp.arange(Ll)
        diff = n[:, None] - n[None, :]
        D = jnp.where(diff >= 0, jnp.asarray(GAMMA, dt) ** diff.astype(dt), jnp.zeros((), dt))
        scores = jnp.einsum('bid,bjd->bij', q, k) * D[None]
        return jnp.einsum('bij,bjd->bid', scores, v)

    def _L3_ffn_ref(x, Wg, bg, W1, b1, W2, b2):
        import jax, jax.numpy as jnp
        import numpy as np
        D_MODEL = 128
        D_HIDDEN = 512
        NUM_EXPERTS = 8
        B, T = (2, 256)
        gate_logits = jnp.einsum('btd,de->bte', x, Wg) + bg
        gate_scores = jax.nn.softmax(gate_logits, axis=-1)
        top1_idx = jnp.argmax(gate_scores, axis=-1)
        top1_mask = jax.nn.one_hot(top1_idx, NUM_EXPERTS, dtype=x.dtype)
        top1_weight = jnp.sum(gate_scores * top1_mask, axis=-1, keepdims=True)
        h = jax.nn.silu(jnp.einsum('btd,edh->bteh', x, W1) + b1)
        o = jnp.einsum('bteh,ehd->bted', h, W2) + b2
        y = jnp.sum(o * top1_mask[..., None], axis=2) * top1_weight
        return y
    x = L0_attn_representations
    xn = _layernorm(x, axis=-1)
    s = _L0_attn_ref(xn, L0_attn_Wc, L0_attn_bc, L0_attn_Wo, L0_attn_bo)
    g = _silu(_L0_ffn_ref(xn, L0_ffn_Wg, L0_ffn_W1, L0_ffn_W2, L0_ffn_W3))
    x = x + s * g
    xn = _layernorm(x, axis=-1)
    s = _L1_attn_ref(xn, L1_attn_a_params, L1_attn_B_w, L1_attn_C_w, L1_attn_D)
    g = _silu(_L1_ffn_ref(xn, L1_ffn_gate_w, L1_ffn_expert_bias, L1_ffn_w1, L1_ffn_w2, L1_ffn_w3))
    x = x + s * g
    xn = _layernorm(x, axis=-1)
    s = _L2_attn_ref(xn, L2_attn_Wqkv, L2_attn_Wproj, L2_attn_bproj)
    g = _silu(_L2_ffn_ref(xn, L2_ffn_tile_sigs, L2_ffn_W, L2_ffn_b))
    x = x + s * g
    xn = _layernorm(x, axis=-1)
    s = _L3_attn_ref(xn, L3_attn_weight_q, L3_attn_weight_k, L3_attn_weight_v, L3_attn_theta)
    g = _silu(_L3_ffn_ref(xn, L3_ffn_Wg, L3_ffn_bg, L3_ffn_W1, L3_ffn_b1, L3_ffn_W2, L3_ffn_b2))
    x = x + s * g
    return x

_drawn_inputs = setup_inputs


def setup_inputs(seed=0):
    import zlib

    import numpy as np

    out = dict(_drawn_inputs(seed))
    spreads = {'L0_attn_bc': (0.0, 0.1),
     'L0_attn_bo': (0.0, 0.1),
     'L1_attn_D': (0.0, 0.1),
     'L1_ffn_expert_bias': (0.0, 0.1),
     'L3_ffn_bg': (0.0, 0.1),
     'L3_ffn_b1': (0.0, 0.1),
     'L3_ffn_b2': (0.0, 0.1)}
    factors = {}
    for name, (base, spread) in spreads.items():
        noise = np.random.default_rng([zlib.crc32(name.encode()), seed]).standard_normal(out[name].shape)
        drawn = base * np.exp(spread * noise) if base else spread * noise
        out[name] = jnp.asarray(drawn.astype(out[name].dtype))
    for name, factor in factors.items():
        out[name] = (out[name] * factor).astype(out[name].dtype)
    return out
```

```python
from contextlib import ExitStack

import numpy as np

import concourse.bass as bass
from concourse import mybir

ALU = mybir.AluOpType
ACT = mybir.ActivationFunctionType
AX = mybir.AxisListType
F32 = mybir.dt.float32
BF16 = mybir.dt.bfloat16

T = 2048
NT = T // 128
NC = 4
CW = 512
NE = 8
EPS = 1e-5
BIG = -3.0e38

CF_COLS = {}
_off = 0
for _name, _n in (("ident", 128), ("ft", 128), ("jft", 128), ("fi", 128), ("fij", 128), ("sm", 128),
                  ("pe", 1024), ("dt", 1024), ("w8", 8)):
    CF_COLS[_name] = (_off, _n)
    _off += _n
CF_N = _off
CB_N = 128 + NE * 128


class Stream:

    def __init__(self, queues, key, sem):
        self.q, self.key, self.sem, self.n = queues[key], key, sem, 0

    def _put(self, f, after, inc):
        for t in after:
            if t is not None:
                self.q.append(("wait", t[0], t[1]))
        self.q.append(("do", f, inc))

    def __call__(self, f, *after):
        self.n += 1
        self._put(f, after, (self.sem, 1))
        return (self.sem, self.n)

    def quiet(self, f, *after):
        self._put(f, after, None)

    def last(self):
        return (self.sem, self.n) if self.n else None


class Dma:

    def __init__(self, queues, sem, key="sync"):
        self.q, self.sem, self.n = queues[key], sem, 0

    def __call__(self, out, in_, *after):
        for t in after:
            if t is not None:
                self.q.append(("wait", t[0], t[1]))
        self.n += 16
        self.q.append(("do", lambda e: e.dma_start(out, in_), (self.sem, 16)))
        return (self.sem, self.n)


def emit(eng, queue):
    seen = {}
    for item in queue:
        if item[0] == "wait":
            _, sem, value = item
            if seen.get(id(sem), 0) < value:
                eng.wait_ge(sem, value)
                seen[id(sem)] = value
        else:
            _, f, inc = item
            ins = f(eng)
            if inc is not None:
                ins.then_inc(*inc)


def program(nc, A, out):
    ctx = ExitStack()
    with ctx:
        _program(nc, A, out, ctx)


def _program(nc, A, out, ctx):
    queues = {k: [] for k in ("sync", "tensor", "vector", "scalar", "gpsimd")}

    def sem(name):
        return ctx.enter_context(nc.semaphore(name))

    def sb(name, shape, dt=F32):
        return ctx.enter_context(nc.sbuf_tensor(name, shape, dt))

    class Phase:
        def __init__(self, name):
            self.pe = Stream(queues, "tensor", sem(name + "_pe"))
            self.dve = Stream(queues, "vector", sem(name + "_dve"))
            self.act = Stream(queues, "scalar", sem(name + "_act"))
            self.pool = Stream(queues, "gpsimd", sem(name + "_pool"))

        def ends(self):
            return [s.last() for s in (self.pe, self.dve, self.act, self.pool)]

    def finish(t_out):
        queues["sync"].append(("wait", *t_out))
        with nc.Block() as block:
            @block.sync
            def _(e):
                emit(e, queues["sync"])

            @block.tensor
            def _(e):
                emit(e, queues["tensor"])

            @block.vector
            def _(e):
                emit(e, queues["vector"])

            @block.scalar
            def _(e):
                emit(e, queues["scalar"])

            @block.gpsimd
            def _(e):
                emit(e, queues["gpsimd"])

    ps = ctx.enter_context(nc.psum_tensor("ps", [128, 8, CW], F32))
    cf = sb("cf", [128, CF_N])
    cb = sb("cb", [128, CB_N], BF16)
    xs = sb("xs", [128, NT, 128])
    xnT = sb("xnT", [128, T])
    gT = sb("gT", [128, T])
    small = sb("small", [128, 2048])
    AR = 31000
    ar = sb("ar", [128, AR])

    def C(name):
        o, n = CF_COLS[name]
        return cf[:, o:o + n]

    ident = C("ident")
    identb = cb[:, 0:128]

    def area(off, n):
        assert off + n <= AR, (off, n)
        return ar[:, off:off + n]

    d_c = Dma(queues, sem("d_const"))
    d_x = [Dma(queues, sem(f"d_x{c}")) for c in range(NC)]
    xv = A["x"].rearrange("b (t p) d -> p (b t) d", p=128)
    t_x = [d_x[c](xs[:, 4 * c:4 * c + 4, :], xv[:, 4 * c:4 * c + 4, :]) for c in range(NC)]
    d_c(cf[:, :], A["cf"])
    t_c = d_c(cb[:, :], A["cb"].bitcast(BF16))

    SM = [0]

    def sm(n):
        o = SM[0]
        SM[0] += n
        assert SM[0] <= 2048
        return small[:, o:o + n]

    mu, var, rstd = sm(16), sm(16), sm(16)
    gs, g1, g2, g3, oh1, oh2, gate = (sm(128) for _ in range(7))
    r1, r2, r3, r4 = sm(16), sm(16), sm(16), sm(16)
    scn = small[:, SM[0]:SM[0] + 64]
    sm(64)
    nm = sm(64)
    gsp = sm(192).bitcast(BF16)
    nsp = sm(96).bitcast(BF16)
    b8 = sm(32)

    def v3(ap, k):
        return ap.rearrange("p (t k) -> p t k", k=k)

    def layernorm(ph, ready, tmp):
        done = []
        for c in range(NC):
            x4 = xs[:, 4 * c:4 * c + 4, :]
            m4, v4, s4 = mu[:, 4 * c:4 * c + 4], var[:, 4 * c:4 * c + 4], rstd[:, 4 * c:4 * c + 4]
            xc = v3(tmp[:, 1024 * c:1024 * c + 512], 128)
            sq = v3(tmp[:, 1024 * c + 512:1024 * c + 1024], 128)
            t = ph.dve(lambda e, m4=m4, x4=x4: e.tensor_reduce(m4, x4, AX.X, ALU.add), *ready[c])
            t = ph.dve(lambda e, m4=m4: e.tensor_scalar(m4, m4, -1.0 / 128, None, ALU.mult), t)
            t = ph.dve(lambda e, m4=m4, x4=x4, xc=xc: e.tensor_tensor(
                xc, x4, m4.unsqueeze(2).to_broadcast([128, 4, 128]), ALU.add), t)
            ta = ph.act(lambda e, xc=xc, sq=sq: e.activation(sq, xc, ACT.Square), t)
            t = ph.dve(lambda e, v4=v4, sq=sq: e.tensor_reduce(v4, sq, AX.X, ALU.add), ta)
            t = ph.dve(lambda e, v4=v4: e.tensor_scalar(v4, v4, 1.0 / 128, EPS, ALU.mult, ALU.add), t)
            ta = ph.act(lambda e, v4=v4, s4=s4: e.activation(s4, v4, ACT.Sqrt), t)
            t = ph.dve(lambda e, s4=s4: e.reciprocal(s4, s4), ta)
            t = ph.dve(lambda e, s4=s4, xc=xc: e.tensor_tensor(
                xc, xc, s4.unsqueeze(2).to_broadcast([128, 4, 128]), ALU.mult), t)
            for j in range(4):
                f = lambda e, c=c, j=j, xc=xc: e.transpose(ps[:, c, 128 * j:128 * j + 128], xc[:, j, :], ident)
                tp = ph.pe(f, t, t_c)
            done.append(ph.act(lambda e, c=c: e.copy(xnT[:, CW * c:CW * c + CW], ps[:, c, :]), tp))
        return done

    def bc8(ap):
        return ap.unsqueeze(2).to_broadcast([128, ap.shape[1], 8])

    def pick_first(ph, s, oh, m, t, n):
        w8 = C("w8").unsqueeze(1).to_broadcast([128, n, 8])
        g = v3(g3[:, 0:8 * n], 8)
        t = ph.dve(lambda e: e.tensor_reduce(m, s, AX.X, ALU.max), t)
        t = ph.dve(lambda e: e.tensor_tensor(g, s, bc8(m), ALU.is_equal), t)
        t = ph.dve(lambda e: e.tensor_tensor(g, g, w8, ALU.mult), t)
        t = ph.dve(lambda e: e.tensor_reduce(r4[:, 0:n], g, AX.X, ALU.max), t)
        return ph.dve(lambda e: e.tensor_tensor(oh, g, bc8(r4[:, 0:n]), ALU.is_equal), t)

    def softmax8(ph, s, t):
        t = ph.dve(lambda e: e.tensor_reduce(r1, s, AX.X, ALU.max, negate=True), t)
        t = ph.dve(lambda e: e.tensor_tensor(s, s, bc8(r1), ALU.add), t)
        t = ph.act(lambda e: e.activation(s, s, ACT.Exp), t)
        t = ph.dve(lambda e: e.tensor_reduce(r2, s, AX.X, ALU.add), t)
        t = ph.dve(lambda e: e.reciprocal(r2, r2), t)
        return ph.dve(lambda e: e.tensor_tensor(s, s, bc8(r2), ALU.mult), t)

    def logits(ph, w, t_w, t_xn, lhs=None, n=NT, k=128):
        for i in range(n):
            l = (xnT[:, 128 * i:128 * i + 128] if lhs is None else lhs[:, 128 * i:128 * i + 128])
            tp = ph.pe(lambda e, i=i, l=l: e.matmul(ps[:, 6, 8 * i:8 * i + 8], l, w, start=True, stop=True),
                       t_w, *t_xn)
        return ph.dve(lambda e: e.tensor_copy(gs[:, 0:8 * n], ps[:, 6, 0:8 * n]), tp)

    def split3(ph, src, parts, tmp, t, eng=None):
        eng = eng or ph.dve
        t1 = eng(lambda e: e.tensor_copy(parts[0], src), t)
        t1 = eng(lambda e: e.tensor_tensor(tmp, src, parts[0], ALU.subtract), t1)
        t2 = eng(lambda e: e.tensor_copy(parts[1], tmp), t1)
        t2 = eng(lambda e: e.tensor_tensor(tmp, tmp, parts[1], ALU.subtract), t2)
        return eng(lambda e: e.tensor_copy(parts[2], tmp), t2)

    def gates_T(ph, src, gTT, n, t):
        g24 = v3(gsp, 24)[:, 0:n, :]
        parts = [g24[:, :, 8 * k:8 * k + 8] for k in range(3)]
        t = split3(ph, src, parts, v3(g3[:, 0:8 * n], 8), t)
        for c in range(n // 8):
            pb = ps[:, 6 + c, :].bitcast(BF16)
            for j in range(8):
                tp = ph.pe(lambda e, c=c, j=j, pb=pb: e.transpose(pb[0:24, 128 * j:128 * j + 128],
                                                                g24[:, 8 * c + j, :], identb), t, t_c)
            td = ph.dve(lambda e, c=c, pb=pb: e.tensor_copy(gTT[0:24, 1024 * c:1024 * c + 1024], pb[0:24, :]), tp)
        return td

    def spread(ph, gTT, e8, c0, bank, *after):
        return ph.pe(lambda e: e.matmul(ps[:, bank, :], cb[0:24, 128 + 128 * e8:256 + 128 * e8],
                                        gTT[0:24, c0:c0 + CW], start=True, stop=True), *after)

    def combine(ph, c, prod, t_prod, bank, t_bank):
        for j in range(4):
            tp = ph.pe(lambda e, j=j: e.transpose(ps[:, bank, 128 * j:128 * j + 128],
                                                  prod[:, 128 * j:128 * j + 128], ident), t_prod, t_bank)
        x4 = xs[:, 4 * c:4 * c + 4, :]
        return ph.dve(lambda e: e.tensor_tensor(x4, x4, v3(ps[:, bank, :], 128), ALU.add), tp)

    O_FW = 0
    w0 = {"w1": area(0, 2048), "w2": area(2048, 2048), "w3": area(4096, 2048)}
    lnt = area(6144, 4096)
    o = 10240
    gTT = area(o, 1024).bitcast(BF16)
    sbufs = [area(o + 1024 + 512 * i, 512) for i in range(8)]
    bbufs = [area(o + 5120 + 512 * i, 512) for i in range(2)]
    wgs = area(o + 6144, 8)
    d_w0 = Dma(queues, sem("d_w0"))
    d_w0(wgs, A["L0_Wg"])
    for k in ("w1", "w2", "w3"):
        t_w0 = d_w0(w0[k], A["L0_" + k])

    p = Phase("l0f")
    t_xn = layernorm(p, [[t_x[c]] for c in range(NC)], lnt)

    def top2(ph, s, t):
        t = pick_first(ph, s, v3(oh1, 8), r1, t, NT)
        t = ph.dve(lambda e: e.scalar_tensor_tensor(out=v3(g2, 8), in0=v3(oh1, 8), scalar=BIG, in1=s,
                                                    op0=ALU.mult, op1=ALU.add), t)
        return pick_first(ph, v3(g2, 8), v3(oh2, 8), r2, t, NT)

    s3 = v3(gs, 8)
    t = logits(p, wgs, t_w0, t_xn)
    t = top2(p, s3, t)
    t = p.dve(lambda e: e.tensor_tensor(r3, r2, r1, ALU.subtract), t)
    t = p.act(lambda e: e.activation(r3, r3, ACT.Exp), t)
    t = p.dve(lambda e: e.tensor_scalar(r1, r3, 1.0, None, ALU.add), t)
    t = p.dve(lambda e: e.reciprocal(r1, r1), t)
    t = p.dve(lambda e: e.tensor_tensor(r2, r3, r1, ALU.mult), t)
    t = p.dve(lambda e: e.tensor_tensor(v3(oh1, 8), v3(oh1, 8), bc8(r1), ALU.mult), t)
    t = p.dve(lambda e: e.tensor_tensor(v3(oh2, 8), v3(oh2, 8), bc8(r2), ALU.mult), t)
    t = p.dve(lambda e: e.tensor_tensor(gate, oh1, oh2, ALU.add), t)
    t_g = gates_T(p, v3(gate, 8), gTT, NT, t)

    def experts(ph, fs, fw, up, mid, down, b_sb, x_of, t_w, t_g, fin):
        free = {b: None for b in range(8)}
        sbfree = {}
        n = 0
        ne = 0
        pend = []

        def flush():
            f = pend.pop(0)
            f()

        for c in range(NC):
            acc = 4 + c % 2
            for e8 in range(NE):
                gb = 6 + ne % 2
                tsp = spread(ph, gTT, e8, CW * c if gTT_n == NT else CW * (c % 2), gb, t_g, free[gb])
                tgt = bbufs[ne % 2]
                if x_of:
                    tb = ph.dve(lambda e, gb=gb, tgt=tgt, c=c: e.tensor_tensor(
                        tgt, xnT[:, CW * c:CW * c + CW], ps[:, gb, :], ALU.mult), tsp, sbfree.get(("b", ne % 2)))
                else:
                    tb = ph.act(lambda e, gb=gb, tgt=tgt: e.copy(tgt, ps[:, gb, :]), tsp,
                                sbfree.get(("b", ne % 2)))
                free[gb] = tb
                for f in range(len(fs)):
                    up(ph, c, e8, f, n, tgt, tb, free, sbfree, pend, acc, ne)
                    n += 1
                    if len(pend) > 1:
                        flush()
                ne += 1
            while pend:
                flush()
            fin(ph, c, acc, free)
        return

    gTT_n = NT

    def gated_up(w1, w2, w3, fs, fw, fwo, x_scaled):
        def up(ph, c, e8, f, n, tgt, tb, free, sbfree, pend, acc, ne):
            m = fs[f]
            ba, bb = (0, 1) if n % 2 == 0 else (2, 3)
            xin = tgt if x_scaled else xnT[:, CW * c:CW * c + CW]
            o1 = e8 * fw + 128 * f
            ta = ph.pe(lambda e: e.matmul(ps[0:m, ba, :], w1[:, o1:o1 + m], xin, start=True, stop=True),
                       tb if x_scaled else None, t_wcur[0], free[ba])
            tc_ = ph.pe(lambda e: e.matmul(ps[0:m, bb, :], w2[:, o1:o1 + m], xin, start=True, stop=True), free[bb])
            if x_scaled:
                sbfree[("b", ne % 2)] = tc_
            s1, u = sbufs[2 * (n % 2)], sbufs[2 * (n % 2) + 1]
            h = sbufs[4 + n % 4]
            ts = ph.act(lambda e: e.activation(s1[0:m, :], ps[0:m, ba, :], ACT.Silu), ta, sbfree.get(("s", n % 2)))
            free[ba] = ts
            if x_scaled:
                th = ph.dve(lambda e: e.tensor_tensor(h[0:m, :], s1[0:m, :], ps[0:m, bb, :], ALU.mult),
                            ts, tc_, sbfree.get(("h", n % 4)))
                free[bb] = th
                sbfree[("s", n % 2)] = th
            else:
                td = ph.dve(lambda e: e.tensor_tensor(u[0:m, :], s1[0:m, :], ps[0:m, bb, :], ALU.mult),
                            ts, tc_, sbfree.get(("u", n % 2)))
                free[bb] = td
                sbfree[("s", n % 2)] = td
                th = ph.dve(lambda e: e.tensor_tensor(h[0:m, :], u[0:m, :], tgt[0:m, :], ALU.mult),
                            td, tb, sbfree.get(("h", n % 4)))
                sbfree[("u", n % 2)] = th
                sbfree[("b", ne % 2)] = th
            k = (e8 * len(fs) + f)
            first, lastm = k == 0, (k == NE * len(fs) - 1)
            o3 = k * 128

            def down():
                t3 = ph.pe(lambda e: e.matmul(ps[:, acc, :], w3[0:m, o3:o3 + 128], h[0:m, :],
                                              start=first, stop=lastm), th, free[acc] if first else None)
                sbfree[("h", n % 4)] = t3
                free["acc"] = t3
            pend.append(down)
        return up

    def fin_silu(ph, c, acc, free):
        t = ph.act(lambda e: e.activation(gT[:, CW * c:CW * c + CW], ps[:, acc, :], ACT.Silu), free["acc"])
        free[acc] = t

    t_wcur = [t_w0]
    experts(p, [128, 128], 256, gated_up(w0["w1"], w0["w2"], w0["w3"], [128, 128], 256, 128, False),
            None, None, True, False, t_w0, t_g, fin_silu)
    end0 = p.ends()

    scr = [nc.dram_tensor(f"scr{i}", [2, 7, 128, T], BF16).ap() for i in range(2)]
    oscr = nc.dram_tensor("oscr", [4, 128, T], F32).ap()
    d_ld = [[Dma(queues, sem(f"d_ld{l}{i}")) for i in range(3)] for l in range(2)]
    d_mr = [Dma(queues, sem(f"d_mr{l}")) for l in range(2)]
    QORD = (0, 0, 0, 1, 1, 2)
    KORD = (0, 1, 2, 0, 1, 0)

    VOFF = 0
    QOFF = 16384
    KOFF = QOFF + 3 * 2048
    POFF = KOFF + 3 * 1024
    RES = POFF + 4 * 1024
    assert RES + 352 <= AR
    acc_sb = sb("acc_sb", [128, T])
    psum_sb = sb("psum_sb", [128, 2048])
    on_sb = sb("on_sb", [128, 1024])
    rec_sb = sb("rec_sb", [128, 512])
    mT = sb("mT", [16, 2 * 1024], BF16)
    wA = sb("wA", [128, 1280 + 1024])
    V0 = area(VOFF, 16384)
    Qs = area(QOFF, 3 * 2048).bitcast(BF16).rearrange("p (s h t) -> p s h t", s=3, h=4)
    Ks = area(KOFF, 3 * 1024).bitcast(BF16).rearrange("p (s h t) -> p s h t", s=3, h=2)
    Ps = area(POFF, 4 * 1024).rearrange("p (s t) -> p s t", s=4)
    parts = area(POFF, 4096)
    onesf = sb("onesf", [128, 64])
    t_one = None
    bias_qk = sb("bias_qk", [128, 2])
    bv = psum_sb[:, 0:1024]
    d_wa = Dma(queues, sem("d_wa0"))
    bo = sb("bo", [128, 1])
    d_wa(wA[:, 0:1280], A["L0_WcT"])
    d_wa(wA[:, 1280:2304], A["L0_WoT"])
    d_wa(bias_qk[:, :], A["L0_bqk"])
    d_wa(bo[:, :], A["L0_bo"])
    t_wa0 = d_wa(bv, A["L0_bv"].partition_broadcast(128))

    def prepare(ph, lay, before, t_w, t_xn, leaky, fill_v):
        tz = ph.pool(lambda e: e.memset(Qs, 0.0), *before)
        tz = ph.pool(lambda e: e.memset(Ks, 1.0), *before)
        t1 = ph.pool(lambda e: e.memset(onesf[:, :], 1.0), *before)
        dd = [Dma(queues, sem(f"d_scr{lay}{i}")) for i in range(2)]
        wr = []
        last = {}
        k = 0
        for c in range(NC):
            for ty in range(2):
                bank = k % 2
                d = dd[bank]
                f0 = parts[:, 2048 * (k % 2):2048 * (k % 2) + 512]
                f1 = parts[:, 2048 * (k % 2) + 512:2048 * (k % 2) + 1024]
                pt = [parts[:, 2048 * (k % 2) + 1024 + 256 * i:2048 * (k % 2) + 1280 + 256 * i].bitcast(BF16)
                      for i in range(3)]
                lf, ld = last.get(k % 2, (None, None))
                tp = ph.pe(lambda e, ty=ty, c=c, bank=bank: e.matmul(
                    ps[:, bank, :], wA[:, 128 * ty:128 * ty + 128], xnT[:, CW * c:CW * c + CW],
                    start=True, stop=True), t_w, *t_xn, *before, lf)
                if leaky:
                    t = ph.dve(lambda e, ty=ty, bank=bank, f1=f1: e.tensor_scalar(
                        f1, ps[:, bank, :], bias_qk[:, ty:ty + 1], None, ALU.add), tp)
                    t = ph.dve(lambda e, f0=f0, f1=f1: e.scalar_tensor_tensor(
                        out=f0, in0=f1, scalar=0.01, in1=f1, op0=ALU.mult, op1=ALU.max), t)
                else:
                    t = ph.dve(lambda e, f0=f0, bank=bank: e.tensor_copy(f0, ps[:, bank, :]), tp)
                lf = t
                t = ph.dve(lambda e, f0=f0, pt=pt: e.tensor_copy(pt[0], f0), t, ld)
                t = ph.dve(lambda e, f0=f0, f1=f1, pt=pt: e.tensor_tensor(f1, f0, pt[0], ALU.subtract), t)
                t = ph.dve(lambda e, f1=f1, pt=pt: e.tensor_copy(pt[1], f1), t)
                t = ph.dve(lambda e, f1=f1, pt=pt: e.tensor_tensor(f1, f1, pt[1], ALU.subtract), t)
                t = ph.dve(lambda e, f1=f1, pt=pt: e.tensor_copy(pt[2], f1), t)
                for g, which in enumerate((QORD, KORD)[ty]):
                    td = d(scr[lay][ty, g, :, CW * c:CW * c + CW], pt[which], t)
                if ty == 0:
                    for g in (6,):
                        td = d(scr[lay][ty, g, :, CW * c:CW * c + CW], zero_b, t_zero)
                last[k % 2] = (lf, td)
                k += 1
            wr.append([last[0][1], last[1][1]])
        tv = fill_v(ph, before, t_w, t_xn)
        return wr, tv, [tz, t1], last

    zero_b = sb("zero_b", [128, CW], BF16)[:, :]
    t_zero = Phase("z").pool(lambda e: e.memset(zero_b, 0.0))

    def fill_v0(ph, before, t_w, t_xn):
        free = [None, None]
        tv = None
        for i in range(NT):
            for hf in range(2):
                k = (2 * i + hf) % 2
                tp = ph.pe(lambda e, i=i, hf=hf, k=k: e.matmul(
                    ps[:, 2 + k, :], xnT[:, 128 * i:128 * i + 128], wA[:, 256 + 512 * hf:768 + 512 * hf],
                    start=True, stop=True), t_w, *t_xn, *before, free[k])
                dst = V0[:, 1024 * i + 512 * hf:1024 * i + 512 * hf + 512]
                tmp = on_sb[:, 512 * k:512 * k + 512]
                t = ph.dve(lambda e, k=k, hf=hf, tmp=tmp: e.tensor_tensor(
                    tmp, ps[:, 2 + k, :], bv[:, 512 * hf:512 * hf + 512], ALU.add), tp)
                free[k] = t
                tv = ph.dve(lambda e, tmp=tmp, dst=dst: e.scalar_tensor_tensor(
                    out=dst, in0=tmp, scalar=0.01, in1=tmp, op0=ALU.mult, op1=ALU.max), t)
        return tv

    def softmax_heads(ph, lay, prep, wide, scale, unit_done):
        wr, tv, tcst, last = prep
        nq = 8
        slot_free = [[], [], []]
        ld_tok = {}
        mrow = {}
        start_all = [tv] + tcst

        def load(g):
            b, q, s = g // 4, g % 4, g % 3
            d = d_ld[lay][s]
            w = wr[2 * b + 1]
            for h in range(4):
                hh = 4 * q + h
                r0 = 64 * (h % 2)
                tok = d(Qs[r0:r0 + 56, s, h, :],
                        scr[lay][0, :, 8 * hh:8 * hh + 8, 1024 * b:1024 * b + 1024], *w, *slot_free[s], *tcst)
                tok = d(Ks[r0:r0 + 48, s, h // 2, :],
                        scr[lay][1, 0:6, 8 * hh:8 * hh + 8, 1024 * b:1024 * b + 1024])
            ld_tok[g] = tok

        negm = [nm[:, 0:32], nm[:, 32:64]]
        slots = {"mx": {0: tv, 1: tv, 2: tv, 3: tv}}
        slots_n = [0]
        bank_free = {b: [x for x in ph.ends()] for b in range(8)}
        negm_free = [None, None]
        mT_free = [[], []]

        def max_tile(g, j, sl):
            s = g % 3
            h, qt = j // 8, j % 8
            b0 = 2 * sl
            for hf in range(2):
                tp = ph.pe(lambda e, hf=hf: e.matmul(
                    ps[:, b0 + hf, :], Qs[:, s, h, 128 * qt:128 * qt + 128],
                    Ks[:, s, h // 2, 512 * hf:512 * hf + 512], start=True, stop=True),
                    ld_tok[g], *bank_free[b0], *bank_free[b0 + 1])
            t = ph.dve(lambda e: e.tensor_reduce(negm[g % 2][:, j:j + 1],
                                                 ps[:, b0:b0 + 2, :].rearrange("p a t -> p (a t)"),
                                                 AX.X, ALU.max, negate=True), tp, negm_free[g % 2])
            bank_free[b0] = bank_free[b0 + 1] = [t]
            return t

        def max_rows(g, t):
            s = g % 3
            k = g % 2
            sp = nsp[:, 96 * k:96 * k + 96].rearrange("p (q h r) -> p h q r", q=8, h=4)
            src = negm[k].rearrange("p (h q) -> p h q", h=4)
            tmp = g1[:, 0:32].rearrange("p (h q) -> p h q", h=4)
            t = split3(ph, src, [sp[:, :, :, r] for r in range(3)], tmp, t)
            negm_free[k] = t
            pb = ps[:, 4, :].bitcast(BF16)
            for qt in range(8):
                tp = ph.pe(lambda e, qt=qt: e.transpose(pb[0:12, 128 * qt:128 * qt + 128],
                                                        nsp[:, 96 * k + 12 * qt:96 * k + 12 * qt + 12], identb),
                           t, *bank_free[4])
            t = ph.dve(lambda e: e.tensor_copy(mT[0:12, 1024 * k:1024 * k + 1024], pb[0:12, :]), tp, *mT_free[k])
            bank_free[4] = [t]
            for h in range(4):
                r0 = 64 * (h % 2) + 48
                tok = d_mr[lay](Qs[r0:r0 + 3, s, h, :], mT[3 * h:3 * h + 3, 1024 * k:1024 * k + 1024], t)
            mT_free[k] = [tok]
            mrow[g] = tok

        load(0)
        load(1)
        for j in range(32):
            t = max_tile(0, j, j % 4)
        max_rows(0, t)

        exp_tok, st_tok, pv_tok, add_tok = {}, {}, {}, {}
        pending = []
        i = 0
        sched = []
        for g in range(nq):
            for hf in range(2):
                if wide:
                    sched += [(g, hf, pr, kt) for pr in range(2) for kt in range(8)]
                else:
                    sched += [(g, hf, pr, kt) for kt in range(8) for pr in range(2)]
        tail = {}
        U = 8 if wide else 16

        def pv(i):
            g, hf, pr, kt = sched[i]
            b = g // 4
            u = i // U
            bank = 6 + u % 2
            pbuf = Ps[:, i % 4, :]
            tile = 8 * b + kt
            for a in range(2):
                h = 4 * (g % 4) + 2 * pr + a
                if wide:
                    o_ap = ps[64 * a:64 * a + 64, bank, :]
                    w_ap = V0[:, 1024 * tile + 64 * h:1024 * tile + 64 * h + 64]
                else:
                    jj = 2 * pr + a
                    o_ap = ps[32 * jj:32 * jj + 32, bank, :]
                    w_ap = V0[:, 512 * tile + 32 * h:512 * tile + 32 * h + 32]
                pv_tok[i] = ph.pe(lambda e, o_ap=o_ap, w_ap=w_ap, a=a: e.matmul(
                    o_ap, w_ap, pbuf[:, 512 * a:512 * a + 512], start=(kt == 0), stop=(kt == 7),
                    skip_group_check=not wide),
                    exp_tok[i], tv, *(bank_free[bank] if kt == 0 else []))

        for i, (g, hf, pr, kt) in enumerate(sched):
            s = g % 3
            loc = i % 32
            if loc == 0 and g + 2 < nq:
                load(g + 2)
            b0 = 2 * (i % 2)
            for a in range(2):
                st_tok[i] = ph.pe(lambda e, a=a, b0=b0, s=s, pr=pr, kt=kt, hf=hf: e.matmul(
                    ps[:, b0 + a, :], Ks[:, s, pr, 128 * kt:128 * kt + 128],
                    Qs[:, s, 2 * pr + a, 512 * hf:512 * hf + 512], start=True, stop=True),
                    mrow[g], *bank_free[b0], *bank_free[b0 + 1])
            ex = ph.act(lambda e, b0=b0, i=i: e.activation(
                Ps[:, i % 4, :], ps[:, b0:b0 + 2, :].rearrange("p a t -> p (a t)"), ACT.Exp, scale=scale),
                st_tok[i], pv_tok.get(i - 4), add_tok.get(i - 4), last[0][1], last[1][1])
            exp_tok[i] = ex
            bank_free[b0] = bank_free[b0 + 1] = [ex]
            if wide:
                u, k = i // 8, i % 8
                sb_ = psum_sb[:, 1024 * (u % 2):1024 * (u % 2) + 1024]
                if k == 0:
                    add_tok[i] = None
                elif k == 1:
                    add_tok[i] = ph.pool(lambda e, i=i, sb_=sb_: e.tensor_tensor(
                        sb_, Ps[:, (i - 1) % 4, :], Ps[:, i % 4, :], ALU.add), ex, tail.get(("sum", u - 2)))
                    add_tok[i - 1] = add_tok[i]
                else:
                    add_tok[i] = ph.pool(lambda e, i=i, sb_=sb_: e.tensor_tensor(
                        sb_, sb_, Ps[:, i % 4, :], ALU.add), ex, add_tok[i - 1])
            if g + 1 < nq and loc < 27:
                for j in range(loc * 32 // 27, (loc + 1) * 32 // 27):
                    tmx = max_tile(g + 1, j, 2)
            if i >= 1:
                pv(i - 1)
            if g + 1 < nq and loc == 27:
                max_rows(g + 1, tmx)
            if loc == 31:
                slot_free[s] = [st_tok[i]]
            unit_done(ph, i, sched, pv_tok, add_tok, bank_free, tail)
        pv(i)
        for x in range(i + 1, i + 8):
            unit_done(ph, x, sched, pv_tok, add_tok, bank_free, tail)
        return tail

    d_fin = Dma(queues, sem("d_fin"))

    def unit_done0(ph, i, sched, pv_tok, add_tok, bank_free, tail):
        u, k = i // 8 - 1, i % 8
        if u < 0:
            return
        g, hf, pr, _ = sched[8 * u]
        b = g // 4
        bank = 6 + u % 2
        c0 = 1024 * b + 512 * hf
        on = on_sb[:, 512 * (u % 2):512 * (u % 2) + 512]
        if k == 2:
            sb_ = psum_sb[:, 1024 * (u % 2):1024 * (u % 2) + 1024]
            for a in range(2):
                t = ph.pe(lambda e, a=a: e.matmul(ps[64 * a:64 * a + 64, 4, :], onesf[:, :],
                                                  sb_[:, 512 * a:512 * a + 512], start=True, stop=True),
                          add_tok[8 * u + 7], *bank_free[4], *bank_free[5])
            tail[("sum", u)] = t
            t = ph.dve(lambda e: e.reciprocal(rec_sb[:, :], ps[:, 4, :]), t, tail.get(("on", u - 1)))
            bank_free[4] = [t]
            t = ph.dve(lambda e: e.tensor_tensor(on, ps[:, bank, :], rec_sb[:, :], ALU.mult),
                       t, pv_tok[8 * u + 7], tail.get(("pr", u - 2)))
            tail[("on", u)] = t
        if k == 4:
            pi = 2 * (g % 4) + pr
            t = ph.pe(lambda e: e.matmul(ps[:, bank, :], wA[:, 1280 + 128 * pi:1408 + 128 * pi], on,
                                         start=True, stop=True), tail[("on", u)])
            tail[("pr", u)] = t
            dst = acc_sb[:, c0:c0 + CW]
            if pi == 0:
                t = ph.dve(lambda e: e.tensor_copy(dst, ps[:, bank, :]), t)
            else:
                t = ph.dve(lambda e: e.tensor_tensor(dst, dst, ps[:, bank, :], ALU.add), t, tail[("acc", c0)])
            tail[("acc", c0)] = t
            bank_free[bank] = [t]

    p = Phase("l0a")
    prep = prepare(p, 0, end0, t_wa0, t_xn, True, fill_v0)
    tail = softmax_heads(p, 0, prep, True, float(1.0 / np.sqrt(8.0)), unit_done0)
    t_x1 = []
    bank_t = p.ends()
    for c in range(NC):
        a = acc_sb[:, CW * c:CW * c + CW]
        tm = on_sb[:, 512 * (c % 2):512 * (c % 2) + 512]
        t = p.dve(lambda e, a=a: e.tensor_scalar(a, a, bo[:, 0:1], None, ALU.add), tail[("acc", CW * c)])
        t = p.dve(lambda e, a=a: e.scalar_tensor_tensor(out=a, in0=a, scalar=0.01, in1=a,
                                                        op0=ALU.mult, op1=ALU.max), t)
        t = p.dve(lambda e, a=a, c=c: e.tensor_tensor(a, a, xnT[:, CW * c:CW * c + CW], ALU.add), t)
        t = p.dve(lambda e, a=a, c=c: e.tensor_tensor(a, a, gT[:, CW * c:CW * c + CW], ALU.mult), t)
        t_x1.append(combine(p, c, a, t, c, p.act.last()))
    end = p.ends()

    w1 = {"w1": area(0, 2816), "w3": area(2816, 2816), "w2": area(5632, 3072)}
    o = 8704
    lnt = area(o, 4096)
    gTT = area(o + 4096, 1024).bitcast(BF16)
    sbufs = [area(o + 5120 + 512 * i, 512) for i in range(8)]
    bbufs = [area(o + 9216 + 512 * i, 512) for i in range(2)]
    wgs = area(o + 10240, 8)
    L1 = o + 10300
    d_w1 = Dma(queues, sem("d_w1"))
    d_w1(wgs, A["L1_Wg"], *end)
    d_w1(b8[:, 0:8], A["L1_eb"].partition_broadcast(128))
    for k in ("w1", "w3", "w2"):
        t_w1 = d_w1(w1[k], A["L1_" + k])
    d_s1 = Dma(queues, sem("d_s1"))
    bw, cw, asc, dcol = (area(L1, 128), area(L1 + 128, 128), area(L1 + 256, 1), area(L1 + 257, 1))
    for dst, k in ((bw, "L1_Bw"), (cw, "L1_CwT"), (asc[0:64, :], "L1_a"), (dcol, "L1_D")):
        t_s1 = d_s1(dst, A[k])

    p = Phase("l1f")
    t_xn = layernorm(p, [[t_x1[c]] for c in range(NC)], lnt)
    t = logits(p, wgs, t_w1, t_xn)
    t = softmax8(p, v3(gs, 8), t)
    t = p.dve(lambda e: e.tensor_tensor(v3(g1, 8), v3(gs, 8), b8[:, 0:8].unsqueeze(1).to_broadcast([128, NT, 8]),
                                        ALU.add), t)
    t = top2(p, v3(g1, 8), t)
    t = p.dve(lambda e: e.tensor_tensor(oh1, oh1, oh2, ALU.add), t)
    t = p.dve(lambda e: e.tensor_tensor(gate, oh1, gs, ALU.mult), t)
    t_g = gates_T(p, v3(gate, 8), gTT, NT, t)
    t_wcur[0] = t_w1
    fs = [128, 128, 96]
    experts(p, fs, 352, gated_up(w1["w1"], w1["w3"], w1["w2"], fs, 352, 128, True),
            None, None, False, True, t_w1, t_g, fin_silu)
    end = p.ends()

    p = Phase("l1a")
    wt, wjt, gt_, gjt = (area(L1 + 260 + 128 * i, 128) for i in range(4))
    tabc = area(0, 1024)
    tabs = area(1024, 1024)
    tmpt = area(2048, 1024)
    bb_, bj_ = area(3072, 2048), area(5120, 2048)
    zz = area(7168, 2048)
    q = 0
    for dst, l, r in ((wt, bw, C("ft")), (wjt, bw, C("jft")), (gt_, C("fi"), cw), (gjt, C("fij"), cw)):
        tp = p.pe(lambda e, l=l, r=r, q=q: e.matmul(ps[:, q, 0:128], l, r, start=True, stop=True), t_s1, *end)
        t_m = p.dve(lambda e, dst=dst, q=q: e.tensor_copy(dst, ps[:, q, 0:128]), tp)
        q += 1
    tp = p.pe(lambda e: e.matmul(ps[:, 4, 0:1], C("sm")[0:64, :], asc[0:64, :], start=True, stop=True), *end)
    om, w2_, dn, rd, cr, ci, u1, u2 = (scn[:, i:i + 1] for i in range(8))
    t = p.dve(lambda e: e.tensor_copy(om, ps[:, 4, 0:1]), tp)
    t = p.dve(lambda e: e.tensor_tensor(w2_, om, om, ALU.mult), t)
    t = p.dve(lambda e: e.tensor_scalar(dn, w2_, 1.0, None, ALU.add), t)
    t = p.dve(lambda e: e.reciprocal(rd, dn), t)
    t = p.dve(lambda e: e.tensor_scalar(cr, w2_, -1.0, 1.0, ALU.mult, ALU.add), t)
    t = p.dve(lambda e: e.tensor_tensor(cr, cr, rd, ALU.mult), t)
    t = p.dve(lambda e: e.tensor_scalar(ci, om, -2.0, None, ALU.mult), t)
    t = p.dve(lambda e: e.tensor_tensor(ci, ci, rd, ALU.mult), t)
    p.dve.quiet(lambda e: e.memset(tabs[:, 0:1], 0.0))
    t = p.dve(lambda e: e.memset(tabc[:, 0:1], 1.0), t)
    m = 1
    while m < 1024:
        t = p.dve(lambda e, m=m: e.tensor_scalar(tmpt[:, 0:m], tabs[:, 0:m], ci, None, ALU.mult), t)
        t = p.dve(lambda e, m=m: e.scalar_tensor_tensor(out=tabc[:, m:2 * m], in0=tabc[:, 0:m], scalar=cr,
                                                        in1=tmpt[:, 0:m], op0=ALU.mult, op1=ALU.subtract), t)
        t = p.dve(lambda e, m=m: e.tensor_scalar(tmpt[:, 0:m], tabc[:, 0:m], ci, None, ALU.mult), t)
        t = p.dve(lambda e, m=m: e.scalar_tensor_tensor(out=tabs[:, m:2 * m], in0=tabs[:, 0:m], scalar=cr,
                                                        in1=tmpt[:, 0:m], op0=ALU.mult, op1=ALU.add), t)
        m *= 2
        if m < 1024:
            t = p.dve(lambda e: e.tensor_tensor(u1, ci, ci, ALU.mult), t)
            t = p.dve(lambda e: e.tensor_tensor(u2, cr, ci, ALU.mult), t)
            t = p.dve(lambda e: e.scalar_tensor_tensor(out=cr, in0=cr, scalar=cr, in1=u1, op0=ALU.mult,
                                                       op1=ALU.subtract), t)
            t = p.dve(lambda e: e.tensor_scalar(ci, u2, 2.0, None, ALU.mult), t)
    t_tab = t
    t_z, t_b = [], []
    for c in range(NC):
        tc0 = 512 * (c % 2)
        ta = p.pe(lambda e, c=c: e.matmul(ps[:, 2 * (c % 2), :], wt, xnT[:, CW * c:CW * c + CW], start=True, stop=True),
                  t_m, t_b[c - 2] if c >= 2 else None)
        tb = p.pe(lambda e, c=c: e.matmul(ps[:, 2 * (c % 2) + 1, :], wjt, xnT[:, CW * c:CW * c + CW],
                                          start=True, stop=True))
        t1 = p.dve(lambda e, c=c, tc0=tc0: e.tensor_tensor(
            bb_[:, CW * c:CW * c + CW], tabc[:, tc0:tc0 + 512], ps[:, 2 * (c % 2), :], ALU.mult), ta, t_tab)
        t2 = p.dve(lambda e, c=c, tc0=tc0: e.tensor_tensor(
            bj_[:, CW * c:CW * c + CW], tabs[:, tc0:tc0 + 512], ps[:, 2 * (c % 2) + 1, :], ALU.mult), tb)
        t_b.append(t2)
        t3 = p.dve(lambda e, c=c: e.tensor_tensor(bb_[:, CW * c:CW * c + CW], bb_[:, CW * c:CW * c + CW],
                                                  bj_[:, CW * c:CW * c + CW], ALU.add), t2)
        init = 0.0 if c % 2 == 0 else zz[:, CW * c - 1:CW * c]
        t4 = p.dve(lambda e, c=c, init=init: e.tensor_tensor_scan(
            zz[:, CW * c:CW * c + CW], bb_[:, CW * c:CW * c + CW], bb_[:, CW * c:CW * c + CW], init,
            ALU.add, ALU.bypass), t3)
        t_z.append(t4)
    t_x2 = []
    for c in range(NC):
        tc0 = 512 * (c % 2)
        r = slice(CW * c, CW * c + CW)
        t1 = p.dve(lambda e, r=r, tc0=tc0: e.tensor_tensor(bb_[:, r], tabc[:, tc0:tc0 + 512], zz[:, r], ALU.mult), t_z[c])
        t2 = p.dve(lambda e, r=r, tc0=tc0: e.tensor_tensor(bj_[:, r], tabs[:, tc0:tc0 + 512], zz[:, r], ALU.mult))
        bank = 4 + c % 2
        p.pe.quiet(lambda e, r=r, bank=bank: e.matmul(ps[:, bank, :], gt_, bb_[:, r], start=True, stop=False),
                   t2, t_x2[c - 2] if c >= 2 else None)
        tp = p.pe(lambda e, r=r, bank=bank: e.matmul(ps[:, bank, :], gjt, bj_[:, r], start=False, stop=True))
        t = p.dve(lambda e, r=r, bank=bank: e.scalar_tensor_tensor(
            out=zz[:, r], in0=xnT[:, r], scalar=dcol[:, 0:1], in1=ps[:, bank, :], op0=ALU.mult, op1=ALU.add), tp)
        t = p.dve(lambda e, r=r: e.tensor_tensor(zz[:, r], zz[:, r], gT[:, r], ALU.mult), t)
        t_x2.append(combine(p, c, zz[:, r], t, 6 + c % 2, t_x2[c - 2] if c >= 2 else None))
    end = p.ends()

    w2l = area(0, 1024)
    lnt = area(12288, 4096)
    gTT = area(5120, 1024).bitcast(BF16)
    bbufs = [area(6144 + 512 * i, 512) for i in range(4)]
    sg = area(8192, 8)
    b2t = area(8200, 128)
    ohT = area(8400, 1024)
    d_w2 = Dma(queues, sem("d_w2"))
    d_w2(w2l, A["L2_W"], *end)
    d_w2(sg[0:32, :], A["L2_sig"])
    d_w2(wA[:, 0:512], A["L2_Wqkvp"])
    d_w2(bo[:, :], A["L2_bp"])
    t_w2 = d_w2(b2t[0:8, :], A["L2_b"])
    p = Phase("l2f")
    t_xn = layernorm(p, [[t_x2[c]] for c in range(NC)], lnt)
    t = p.dve(lambda e: e.tensor_scalar(b8[0:32, 0:8], sg[0:32, :], 0.0, None, ALU.is_gt), t_w2)
    t = p.dve(lambda e: e.tensor_scalar(b8[0:32, 8:16], sg[0:32, :], 0.0, None, ALU.is_lt), t)
    t = p.dve(lambda e: e.tensor_tensor(b8[0:32, 0:8], b8[0:32, 0:8], b8[0:32, 8:16], ALU.subtract), t)
    t = logits(p, b8[0:32, 0:8], t, t_xn, lhs=C("pe")[0:32, :], n=8)
    t = pick_first(p, v3(gs[:, 0:64], 8), v3(gate[:, 0:64], 8), r1[:, 0:8], t, 8)
    t_g = gates_T(p, v3(gate[:, 0:64], 8), gTT, 8, t)
    oh_src = gTT[0:8, 0:1024]
    t_oh = p.dve(lambda e: e.tensor_copy(ohT[0:8, :], oh_src), t_g)
    free = {}
    k = 0
    for c in range(NC):
        c0 = CW * (c % 2)
        acc = 4 + c % 2
        for e8 in range(NE):
            tb = bbufs[k % 4]
            ts = spread(p, gTT, e8, c0, k % 2, t_g, free.get(("g", k % 2)))
            td = p.dve(lambda e, tb=tb, k=k, c=c: e.tensor_tensor(tb, xnT[:, CW * c:CW * c + CW], ps[:, k % 2, :],
                                                                  ALU.mult), ts, free.get(("x", k % 4)))
            free[("g", k % 2)] = td
            free[("x", k % 4)] = p.pe(lambda e, tb=tb, e8=e8, acc=acc: e.matmul(
                ps[:, acc, :], w2l[:, 128 * e8:128 * e8 + 128], tb, start=(e8 == 0), stop=False), td,
                free.get(("a", acc)))
            k += 1
        tp = p.pe(lambda e, acc=acc, c0=c0: e.matmul(ps[:, acc, :], b2t[0:8, :], ohT[0:8, c0:c0 + CW],
                                                     start=False, stop=True), t_oh)
        free[("a", acc)] = p.act(lambda e, c=c, acc=acc: e.activation(gT[:, CW * c:CW * c + CW], ps[:, acc, :],
                                                                      ACT.Silu), tp)
    end = p.ends()

    p = Phase("l2a")
    qkv = [area(384 * k, 384) for k in range(2)]
    pr1 = [area(1024 + 2048 * k, 2048) for k in range(2)]
    pr2 = [area(5120 + 2048 * k, 2048) for k in range(2)]
    sc2 = [area(9216 + 256 * k, 256) for k in range(2)]
    ot2 = [area(9728 + 128 * k, 128) for k in range(2)]
    st2 = [area(9984 + 64 * k, 64) for k in range(2)]
    oT2 = area(10240, 2048)
    t_x3 = []
    HD = 8
    fin_ = {}

    def h4(ap, spec, **kw):
        return ap.rearrange(spec, **kw)

    def tile_a(i):
        k = i % 2
        tp = p.pe(lambda e: e.matmul(ps[:, k, 0:384], xnT[:, 128 * i:128 * i + 128], wA[:, 0:384],
                                     start=True, stop=True), *end, fin_.get(("qkv", i - 2)))
        ta = p.act(lambda e: e.copy(qkv[k], ps[:, k, 0:384]), tp, *end, fin_.get(("p2", i - 2)),
                   fin_.get(("p2g", i - 2)))
        fin_[("qkv", i)] = ta
        q4 = qkv[k][:, 0:128].rearrange("p (h d) -> p h d", d=8).unsqueeze(2).to_broadcast([128, 16, 16, 8])
        k4 = qkv[k][:, 128:256].rearrange("p (g d) -> p g d", d=8).unsqueeze(1).to_broadcast([128, 16, 16, 8])
        fin_[("p1", i)] = p.pool(lambda e: e.tensor_tensor(
            pr1[k].rearrange("p (h g d) -> p h g d", h=16, g=16), q4, k4, ALU.mult), ta, fin_.get(("r1", i - 2)))

    def tile_b(i):
        k = i % 2
        s = sc2[k]
        s3_ = s.rearrange("p (h g) -> p h g", g=16)
        mx, ls = st2[k][:, 0:16], st2[k][:, 16:32]
        t = p.dve(lambda e: e.tensor_reduce(s, pr1[k].rearrange("p (a d) -> p a d", d=8), AX.X, ALU.add),
                  fin_[("p1", i)], fin_.get(("p2", i - 2)), fin_.get(("p2g", i - 2)))
        fin_[("r1", i)] = t
        t = p.dve(lambda e: e.tensor_reduce(mx, s3_, AX.X, ALU.max, negate=True), t)
        t = p.dve(lambda e: e.tensor_tensor(s3_, s3_, mx.unsqueeze(2).to_broadcast([128, 16, 16]), ALU.add), t)
        t = p.act(lambda e: e.activation(s, s, ACT.Exp, scale=0.125), t)
        v4 = qkv[k][:, 256:384].rearrange("p (g d) -> p d g", d=8).unsqueeze(1)
        s4 = s3_.unsqueeze(2)
        o4 = pr2[k].rearrange("p (h d g) -> p h d g", h=16, d=8)
        n1, n2 = HD, 16 - HD
        fin_[("p2g", i)] = p.pool(lambda e: e.tensor_tensor(
            o4[:, n1:16, :, :], s4[:, n1:16, :, :].to_broadcast([128, n2, 8, 16]),
            v4.to_broadcast([128, n2, 8, 16]), ALU.mult), t, fin_.get(("r2", i - 2)))
        p.dve.quiet(lambda e: e.tensor_reduce(ls, s3_, AX.X, ALU.add), t)
        fin_[("p2", i)] = p.dve(lambda e: e.tensor_tensor(
            o4[:, 0:n1, :, :], s4[:, 0:n1, :, :].to_broadcast([128, n1, 8, 16]),
            v4.to_broadcast([128, n1, 8, 16]), ALU.mult), t, fin_.get(("r2", i - 2)))

    def tile_c(i):
        k = i % 2
        ls = st2[k][:, 16:32]
        t0 = p.dve(lambda e: e.reciprocal(ls, ls), fin_[("p2", i)])
        t = p.dve(lambda e: e.tensor_reduce(ot2[k], pr2[k].rearrange("p (a g) -> p a g", g=16), AX.X, ALU.add),
                  fin_[("p2", i)], fin_[("p2g", i)], fin_.get(("tr", i - 2)))
        fin_[("r2", i)] = t
        t = p.dve(lambda e: e.tensor_tensor(v3(ot2[k], 8), v3(ot2[k], 8), bc8(ls), ALU.mult), t, t0)
        c = i // 4
        tp = p.pe(lambda e: e.transpose(ps[:, 2 + c % 2, 128 * (i % 4):128 * (i % 4) + 128], ot2[k], ident), t,
                  fin_.get(("ev", c - 2)))
        fin_[("tr", i)] = tp
        if i % 4 == 3:
            r = slice(CW * c, CW * c + CW)
            ta = p.act(lambda e: e.copy(oT2[:, r], ps[:, 2 + c % 2, :]), tp)
            fin_[("ev", c)] = ta
            tp = p.pe(lambda e: e.matmul(ps[:, 4 + c % 2, :], wA[:, 384:512], oT2[:, r], start=True, stop=True), ta,
                      t_x3[c - 2] if c >= 2 else None)
            a = acc_sb[:, r]
            t = p.dve(lambda e: e.scalar_tensor_tensor(out=a, in0=ps[:, 4 + c % 2, :], scalar=bo[:, 0:1],
                                                       in1=gT[:, r], op0=ALU.add, op1=ALU.mult), tp)
            t_x3.append(combine(p, c, a, t, 6 + c % 2, t_x3[c - 2] if c >= 2 else None))

    for i in range(NT + 2):
        if i < NT:
            tile_a(i)
        if 1 <= i <= NT:
            tile_b(i - 1)
        if i >= 2:
            tile_c(i - 2)
    end = p.ends()

    w3 = {"w1": area(0, 4096), "w2": area(4096, 4096)}
    lnt = area(16384, 4096)
    o = 12288
    gTT = area(o, 1024).bitcast(BF16)
    gTf = area(o + 1024, 2048)
    sbufs = [area(o + 3072 + 512 * i, 512) for i in range(8)]
    bbufs = [area(o + 7168 + 512 * i, 512) for i in range(2)]
    wgs = area(o + 8192, 8)
    b1c = area(o + 8200, 32)
    b2r = area(o + 8232, 128)
    L3 = o + 8400
    d_w3 = Dma(queues, sem("d_w3"))
    d_w3(wgs, A["L3_Wg"], *end)
    d_w3(b8[:, 0:8], A["L3_bg"].partition_broadcast(128))
    d_w3(b1c, A["L3_b1"])
    d_w3(b2r[0:8, :], A["L3_b2"])
    for k in ("w1", "w2"):
        t_w3 = d_w3(w3[k], A["L3_" + k])
    wq3, wk3, wv3, th = area(L3, 128), area(L3 + 128, 128), area(L3 + 256, 128), area(L3 + 384, 1)
    d_s3 = Dma(queues, sem("d_s3"))
    for dst, k in ((wq3, "L3_wq"), (wk3, "L3_wk"), (wv3, "L3_wv"), (th, "L3_th")):
        t_s3 = d_s3(dst, A[k])
    p = Phase("l3f")
    t_xn = layernorm(p, [[t_x3[c]] for c in range(NC)], lnt)
    t = logits(p, wgs, t_w3, t_xn)
    t = p.dve(lambda e: e.tensor_tensor(v3(gs, 8), v3(gs, 8), b8[:, 0:8].unsqueeze(1).to_broadcast([128, NT, 8]),
                                        ALU.add), t)
    t = softmax8(p, v3(gs, 8), t)
    t = pick_first(p, v3(gs, 8), v3(oh1, 8), r1, t, NT)
    t = p.dve(lambda e: e.tensor_tensor(gate, oh1, gs, ALU.mult), t)
    for c in range(NC):
        for j in range(4):
            tp = p.pe(lambda e, c=c, j=j: e.transpose(ps[0:8, c, 128 * j:128 * j + 128],
                                                      v3(gate, 8)[:, 4 * c + j, :], ident), t)
        tf = p.dve(lambda e, c=c: e.tensor_copy(gTf[0:8, CW * c:CW * c + CW], ps[0:8, c, :]), tp)
    t_g = gates_T(p, v3(gate, 8), gTT, NT, t)

    def up3(ph, c, e8, f, n, tgt, tb, free, sbfree, pend, acc, ne):
        bk = n % 4
        o1 = e8 * 512 + 128 * f
        ta = ph.pe(lambda e: e.matmul(ps[:, bk, :], w3["w1"][:, o1:o1 + 128], xnT[:, CW * c:CW * c + CW],
                                      start=True, stop=True), t_w3, free[bk])
        s1 = sbufs[n % 2]
        h = sbufs[4 + n % 4]
        k = 4 * e8 + f
        ts = ph.act(lambda e: e.activation(s1, ps[:, bk, :], ACT.Silu, bias=b1c[:, k:k + 1]), ta,
                    sbfree.get(("s", n % 2)))
        free[bk] = ts
        t_h = ph.dve(lambda e: e.tensor_tensor(h, s1, tgt, ALU.mult), ts, tb, sbfree.get(("h", n % 4)))
        sbfree[("s", n % 2)] = t_h
        sbfree[("b", ne % 2)] = t_h

        def down():
            t3 = ph.pe(lambda e: e.matmul(ps[:, acc, :], w3["w2"][:, 128 * k:128 * k + 128], h,
                                          start=(k == 0), stop=False), t_h, free[acc] if k == 0 else None)
            sbfree[("h", n % 4)] = t3
        pend.append(down)

    def fin3(ph, c, acc, free):
        t = ph.pe(lambda e: e.matmul(ps[:, acc, :], b2r[0:8, :], gTf[0:8, CW * c:CW * c + CW],
                                     start=False, stop=True), tf)
        free[acc] = ph.act(lambda e: e.activation(gT[:, CW * c:CW * c + CW], ps[:, acc, :], ACT.Silu), t)

    experts(p, [128] * 4, 512, up3, None, None, True, False, t_w3, t_g, fin3)
    end = p.ends()

    p = Phase("l3a")
    qT, kT, vv, sc = area(0, 2048), area(2048, 2048), area(4096, 2048), area(6144, 8192)
    ex = scn[:, 0:1]
    t = p.dve(lambda e: e.tensor_scalar(ex, th, 0.0, None, ALU.mult), t_s3, *end)
    t_th = p.act(lambda e: e.activation(ex, ex, ACT.Exp), t)
    k = 0
    bf = {b: None for b in range(8)}
    t_q = {}
    for c in range(NC):
        for w_, dst in ((wq3, qT), (wk3, kT)):
            bank = k % 4
            tp = p.pe(lambda e, w_=w_, c=c, bank=bank: e.matmul(ps[:, bank, :], w_, xnT[:, CW * c:CW * c + CW],
                                                                start=True, stop=True), t_s3, *end, bf[bank])
            t_q[c] = bf[bank] = p.dve(lambda e, dst=dst, c=c, bank=bank: e.tensor_scalar(
                dst[:, CW * c:CW * c + CW], ps[:, bank, :], ex, None, ALU.mult), tp, t_th)
            k += 1
    for i in range(NT):
        bank = 4 + (i // 4) % 2
        tp = p.pe(lambda e, i=i, bank=bank: e.matmul(ps[:, bank, 128 * (i % 4):128 * (i % 4) + 128],
                                                     xnT[:, 128 * i:128 * i + 128], wv3, start=True, stop=True),
                  *end, bf[bank])
        if i % 4 == 3:
            t_v = bf[bank] = p.act(lambda e, i=i, bank=bank: e.copy(vv[:, 128 * (i - 3):128 * (i + 1)],
                                                                    ps[:, bank, :]), tp)
    d_out = Dma(queues, sem("d_out"))
    ov = out.rearrange("b (t p) d -> p (b t) d", p=128)
    k = 0
    for b in range(2):
        scb = {}
        for jb in range(8):
            w = 1024 - 128 * jb
            o1 = 0
            dst = sc[:, 1024 * jb:1024 * jb + w]
            while o1 < w:
                wd = min(512, w - o1)
                bank = k % 4
                k += 1
                i0 = 1024 * b + 128 * jb + o1
                tp = p.pe(lambda e, bank=bank, i0=i0, jb=jb, wd=wd, b=b: e.matmul(
                    ps[:, bank, 0:wd], kT[:, 1024 * b + 128 * jb:1024 * b + 128 * jb + 128],
                    qT[:, i0:i0 + wd], start=True, stop=True), t_q[3], bf[bank])
                bf[bank] = p.dve(lambda e, bank=bank, dst=dst, o1=o1, wd=wd: e.tensor_tensor(
                    dst[:, o1:o1 + wd], ps[:, bank, 0:wd], C("dt")[:, o1:o1 + wd], ALU.mult), tp,
                    scfree if b else None)
                o1 += wd
            scb[jb] = bf[bank]
        for hf in range(2):
            bank = 4 + (2 * b + hf) % 4
            for jb in range(4 * (hf + 1)):
                i0 = max(0, 128 * jb - 512 * hf)
                s0 = 1024 * jb + 512 * hf + i0 - 128 * jb
                tp = p.pe(lambda e, bank=bank, i0=i0, s0=s0, jb=jb, b=b, hf=hf: e.matmul(
                    ps[:, bank, i0:512], vv[:, 1024 * b + 128 * jb:1024 * b + 128 * jb + 128],
                    sc[:, s0:s0 + 512 - i0], start=(jb == 0), stop=(jb == 4 * hf + 3)), scb[jb], t_v, bf[bank])
            scfree = tp
            c = 2 * b + hf
            a = acc_sb[:, CW * c:CW * c + CW]
            t = p.dve(lambda e, bank=bank, a=a, c=c: e.tensor_tensor(a, ps[:, bank, :], gT[:, CW * c:CW * c + CW],
                                                                     ALU.mult), tp)
            t = combine(p, c, a, t, bank, t)
            bf[bank] = t
            t_out = d_out(ov[:, 4 * c:4 * c + 4, :], xs[:, 4 * c:4 * c + 4, :], t)
    finish(t_out)


def constants():
    f = np.zeros((128, CF_N), np.float64)

    def put(name, a):
        o, _ = CF_COLS[name]
        f[:a.shape[0], o:o + a.shape[1]] = a

    put("ident", np.eye(128))
    n = np.arange(128)[:, None]
    k = np.arange(64)[None, :]
    w = 2 * np.pi * n * k / 128
    F = np.concatenate([np.cos(w), -np.sin(w)], 1)
    F[:, 64] = (-1.0) ** np.arange(128)
    J = np.zeros((128, 128))
    for i in range(1, 64):
        J[i, 64 + i] = 1
        J[64 + i, i] = -1
    Fi = np.concatenate([2 * np.cos(w), -2 * np.sin(w)], 1) / 128
    Fi[:, 0] = 1 / 128
    Fi[:, 64] = (-1.0) ** np.arange(128) / 128
    put("ft", F)
    put("jft", F @ J.T)
    put("fi", Fi)
    put("fij", -(Fi @ J))
    j = np.arange(1, 65)[:, None]
    s = -2 * np.sin(2 * np.pi * j * k / 128)
    s[63] = 0
    S = np.concatenate([s, s], 1)
    put("sm", S)
    pos = np.arange(1024, dtype=np.float32)[:, None]
    div = np.exp(np.arange(0, 32, 2, dtype=np.float32) * np.float32(-np.log(10000.0) / 32)).astype(np.float32)
    ang = (pos * div).astype(np.float32)
    pe = np.zeros((1024, 32), np.float32)
    pe[:, 0::2] = np.sin(ang)
    pe[:, 1::2] = np.cos(ang)
    put("pe", pe.T)
    i = np.arange(1024)[None, :] - np.arange(128)[:, None]
    put("dt", np.where(i >= 0, 0.96875 ** np.maximum(i, 0).astype(np.float64), 0.0))
    put("w8", np.tile(8.0 - np.arange(8), (128, 1)))
    one = 0x3F80
    b = np.zeros((128, CB_N), np.uint16)
    b[:, 0:128] = one * np.eye(128, dtype=np.uint16)
    for e in range(NE):
        for r in range(3):
            b[8 * r + e, 128 + 128 * e:256 + 128 * e] = one
    return f.astype(np.float32), b


def layouts(a):
    def blocks(w, k):
        return np.ascontiguousarray(w.reshape(-1, k, w.shape[-1]).transpose(1, 0, 2).reshape(k, -1))

    d = {"x": a["L0_attn_representations"]}
    Wc = a["L0_attn_Wc"]
    d["L0_WcT"] = Wc.T
    d["L0_WoT"] = blocks(a["L0_attn_Wo"].T, 128)
    d["L0_bqk"] = a["L0_attn_bc"][:256].reshape(2, 128).T
    d["L0_bv"] = a["L0_attn_bc"][256:]
    d["L0_bo"] = a["L0_attn_bo"][:, None]
    d["L0_Wg"] = a["L0_ffn_Wg"].T
    d["L0_w1"] = a["L0_ffn_W1"].reshape(2048, 128).T
    d["L0_w2"] = a["L0_ffn_W2"].reshape(2048, 128).T
    d["L0_w3"] = blocks(a["L0_ffn_W3"].transpose(0, 2, 1).reshape(2048, 128), 128)
    d["L1_Wg"] = a["L1_ffn_gate_w"].T
    d["L1_eb"] = a["L1_ffn_expert_bias"]
    d["L1_w1"] = a["L1_ffn_w1"].transpose(1, 0, 2).reshape(128, -1)
    d["L1_w3"] = a["L1_ffn_w3"].transpose(1, 0, 2).reshape(128, -1)
    w2 = np.zeros((8, 384, 128), np.float32)
    w2[:, :352] = a["L1_ffn_w2"]
    d["L1_w2"] = blocks(w2.reshape(-1, 128), 128)
    d["L1_Bw"] = a["L1_attn_B_w"]
    d["L1_CwT"] = a["L1_attn_C_w"].T
    d["L1_a"] = a["L1_attn_a_params"][:, None]
    d["L1_D"] = a["L1_attn_D"][:, None]
    d["L2_W"] = a["L2_ffn_W"].transpose(2, 0, 1).reshape(128, -1)
    d["L2_sig"] = a["L2_ffn_tile_sigs"].T
    d["L2_b"] = a["L2_ffn_b"]
    w = a["L2_attn_Wqkv"].reshape(16, 3, 8, 128).transpose(1, 0, 2, 3).reshape(384, 128)
    d["L2_Wqkvp"] = np.concatenate([w, a["L2_attn_Wproj"].T.T], 0)
    d["L2_Wqkvp"] = np.concatenate([w.T, a["L2_attn_Wproj"].T], 1)
    d["L2_bp"] = a["L2_attn_bproj"][:, None]
    d["L3_Wg"] = a["L3_ffn_Wg"]
    d["L3_bg"] = a["L3_ffn_bg"]
    d["L3_w1"] = a["L3_ffn_W1"].transpose(1, 0, 2).reshape(128, -1)
    d["L3_b1"] = a["L3_ffn_b1"].reshape(32, 128).T
    d["L3_w2"] = blocks(a["L3_ffn_W2"].reshape(-1, 128), 128)
    d["L3_b2"] = a["L3_ffn_b2"]
    d["L3_wq"] = a["L3_attn_weight_q"]
    d["L3_wk"] = a["L3_attn_weight_k"]
    d["L3_wv"] = a["L3_attn_weight_v"]
    d["L3_th"] = a["L3_attn_theta"][:, None]
    return {k: np.ascontiguousarray(v) for k, v in d.items()}


def kernel(**inputs):
    import concourse.bacc as bacc
    from concourse.bass_utils import run_bass_kernel_spmd

    a = layouts({k: np.asarray(v) for k, v in inputs.items()})
    a["cf"], a["cb"] = constants()
    nc = bacc.Bacc("TRN2", target_bir_lowering=False, num_devices=1)
    arrays, aps = {}, {}
    for name, v in a.items():
        arrays["in_" + name] = v
        aps[name] = nc.dram_tensor("in_" + name, v.shape, mybir.dt.from_np(v.dtype), kind="ExternalInput").ap()
    out = nc.dram_tensor("out_0", (2, 1024, 128), F32, kind="ExternalOutput").ap()
    program(nc, aps, out)
    r = run_bass_kernel_spmd(nc, [arrays], core_ids=[0])
    return r.results[0]["out_0"]
```

```python
from contextlib import ExitStack

import numpy as np

import concourse.bass as bass
from concourse import mybir

ALU = mybir.AluOpType
ACT = mybir.ActivationFunctionType
AX = mybir.AxisListType
F32 = mybir.dt.float32
BF16 = mybir.dt.bfloat16

T = 2048
NT = T // 128
NC = 4
CW = 512
NE = 8
EPS = 1e-5
BIG = -3.0e38

CF_COLS = {}
_off = 0
for _name, _n in (("ident", 128), ("ft", 128), ("jft", 128), ("fi", 128), ("fij", 128), ("sm", 128),
                  ("w8", 8), ("pe", 1024), ("dt", 1024)):
    CF_COLS[_name] = (_off, _n)
    _off += _n
CF_N = _off
CF_KEPT = CF_COLS["pe"][0]
CB_N = 128 + NE * 128

MISC_COLS = {}
_off = 0
for _name, _n in (("wqkvp", 512), ("wq", 128), ("wk", 128), ("wv", 128), ("bw", 128), ("cw", 128), ("wg1", 8),
                  ("wg3", 8), ("b1c", 32), ("th", 1), ("asc", 1), ("dcol", 1), ("bp", 1), ("eb", 8), ("bg", 8),
                  ("sig", 8), ("b2", 128), ("b3", 128)):
    MISC_COLS[_name] = (_off, _n)
    _off += _n
MISC_N = _off
HD = 4
SPH = 2


class Stream:

    def __init__(self, queues, key, sem):
        self.q, self.key, self.sem, self.n = queues[key], key, sem, 0

    def _put(self, f, after, inc):
        for t in after:
            if t is not None:
                self.q.append(("wait", t[0], t[1]))
        self.q.append(("do", f, inc))

    def __call__(self, f, *after):
        self.n += 1
        self._put(f, after, (self.sem, 1))
        return (self.sem, self.n)

    def quiet(self, f, *after):
        self._put(f, after, None)

    def last(self):
        return (self.sem, self.n) if self.n else None


class Dma:

    def __init__(self, queues, sem, key="sync"):
        self.q, self.sem, self.n = queues[key], sem, 0

    def __call__(self, out, in_, *after):
        for t in after:
            if t is not None:
                self.q.append(("wait", t[0], t[1]))
        self.n += 16
        self.q.append(("do", lambda e: e.dma_start(out, in_), (self.sem, 16)))
        return (self.sem, self.n)


def emit(eng, queue):
    seen = {}
    for item in queue:
        if item[0] == "wait":
            _, sem, value = item
            if seen.get(id(sem), 0) < value:
                eng.wait_ge(sem, value)
                seen[id(sem)] = value
        else:
            _, f, inc = item
            ins = f(eng)
            if inc is not None:
                ins.then_inc(*inc)


def program(nc, A, out):
    ctx = ExitStack()
    with ctx:
        _program(nc, A, out, ctx)


def _program(nc, A, out, ctx):
    queues = {k: [] for k in ("sync", "tensor", "vector", "scalar", "gpsimd")}

    def sem(name):
        return ctx.enter_context(nc.semaphore(name))

    def sb(name, shape, dt=F32):
        return ctx.enter_context(nc.sbuf_tensor(name, shape, dt))

    class Phase:
        def __init__(self, name):
            self.pe = Stream(queues, "tensor", sem(name + "_pe"))
            self.dve = Stream(queues, "vector", sem(name + "_dve"))
            self.act = Stream(queues, "scalar", sem(name + "_act"))
            self.pool = Stream(queues, "gpsimd", sem(name + "_pool"))

        def ends(self):
            return [s.last() for s in (self.pe, self.dve, self.act, self.pool)]

    def finish(t_out):
        queues["sync"].append(("wait", *t_out))
        with nc.Block() as block:
            @block.sync
            def _(e):
                emit(e, queues["sync"])

            @block.tensor
            def _(e):
                emit(e, queues["tensor"])

            @block.vector
            def _(e):
                emit(e, queues["vector"])

            @block.scalar
            def _(e):
                emit(e, queues["scalar"])

            @block.gpsimd
            def _(e):
                emit(e, queues["gpsimd"])

    ps = ctx.enter_context(nc.psum_tensor("ps", [128, 8, CW], F32))
    cf = sb("cf", [128, CF_KEPT])
    cb = sb("cb", [128, CB_N], BF16)
    xs = sb("xs", [128, NT, 128])
    xnT = sb("xnT", [128, T])
    gT = sb("gT", [128, T])
    small = sb("small", [128, 2048])
    AR = 30100
    ar = sb("ar", [128, AR])

    def C(name):
        o, n = CF_COLS[name]
        return cf[:, o:o + n]

    ident = C("ident")
    identb = cb[:, 0:128]

    def area(off, n):
        assert off + n <= AR, (off, n)
        return ar[:, off:off + n]

    d_c = Dma(queues, sem("d_const"))
    d_x = [Dma(queues, sem(f"d_x{c}")) for c in range(NC)]
    xv = A["x"].rearrange("b (t p) d -> p (b t) d", p=128)
    t_x = [d_x[c](xs[:, 4 * c:4 * c + 4, :], xv[:, 4 * c:4 * c + 4, :]) for c in range(NC)]
    d_c(cf[:, :], A["cf"][:, 0:CF_KEPT])
    t_c = d_c(cb[:, :], A["cb"].bitcast(BF16))

    SM = [0]

    def sm(n):
        o = SM[0]
        SM[0] += n
        assert SM[0] <= 2048
        return small[:, o:o + n]

    mu, var, rstd = sm(16), sm(16), sm(16)
    gs, g1, g2, g3, oh1, oh2, gate = (sm(128) for _ in range(7))
    r1, r2, r3, r4 = sm(16), sm(16), sm(16), sm(16)
    scn = small[:, SM[0]:SM[0] + 64]
    sm(64)
    nm = sm(128)
    gsp = sm(192).bitcast(BF16)
    nsp = sm(96).bitcast(BF16)
    b8 = sm(32)

    def v3(ap, k):
        return ap.rearrange("p (t k) -> p t k", k=k)

    def layernorm(ph, ready, tmp):
        done = []
        for c in range(NC):
            x4 = xs[:, 4 * c:4 * c + 4, :]
            m4, v4, s4 = mu[:, 4 * c:4 * c + 4], var[:, 4 * c:4 * c + 4], rstd[:, 4 * c:4 * c + 4]
            xc = v3(tmp[:, 1024 * c:1024 * c + 512], 128)
            sq = v3(tmp[:, 1024 * c + 512:1024 * c + 1024], 128)
            t = ph.dve(lambda e, m4=m4, x4=x4: e.tensor_reduce(m4, x4, AX.X, ALU.add), *ready[c])
            t = ph.dve(lambda e, m4=m4: e.tensor_scalar(m4, m4, -1.0 / 128, None, ALU.mult), t)
            t = ph.dve(lambda e, m4=m4, x4=x4, xc=xc: e.tensor_tensor(
                xc, x4, m4.unsqueeze(2).to_broadcast([128, 4, 128]), ALU.add), t)
            ta = ph.act(lambda e, xc=xc, sq=sq: e.activation(sq, xc, ACT.Square), t)
            t = ph.dve(lambda e, v4=v4, sq=sq: e.tensor_reduce(v4, sq, AX.X, ALU.add), ta)
            t = ph.dve(lambda e, v4=v4: e.tensor_scalar(v4, v4, 1.0 / 128, EPS, ALU.mult, ALU.add), t)
            ta = ph.act(lambda e, v4=v4, s4=s4: e.activation(s4, v4, ACT.Sqrt), t)
            t = ph.dve(lambda e, s4=s4: e.reciprocal(s4, s4), ta)
            t = ph.dve(lambda e, s4=s4, xc=xc: e.tensor_tensor(
                xc, xc, s4.unsqueeze(2).to_broadcast([128, 4, 128]), ALU.mult), t)
            for j in range(4):
                f = lambda e, c=c, j=j, xc=xc: e.transpose(ps[:, c, 128 * j:128 * j + 128], xc[:, j, :], ident)
                tp = ph.pe(f, t, t_c)
            done.append(ph.act(lambda e, c=c: e.copy(xnT[:, CW * c:CW * c + CW], ps[:, c, :]), tp))
        return done

    def bc8(ap):
        return ap.unsqueeze(2).to_broadcast([128, ap.shape[1], 8])

    def pick_first(ph, s, oh, m, t, n):
        w8 = C("w8").unsqueeze(1).to_broadcast([128, n, 8])
        g = v3(g3[:, 0:8 * n], 8)
        t = ph.dve(lambda e: e.tensor_reduce(m, s, AX.X, ALU.max), t)
        t = ph.dve(lambda e: e.tensor_tensor(g, s, bc8(m), ALU.is_equal), t)
        t = ph.dve(lambda e: e.tensor_tensor(g, g, w8, ALU.mult), t)
        t = ph.dve(lambda e: e.tensor_reduce(r4[:, 0:n], g, AX.X, ALU.max), t)
        return ph.dve(lambda e: e.tensor_tensor(oh, g, bc8(r4[:, 0:n]), ALU.is_equal), t)

    def softmax8(ph, s, t):
        t = ph.dve(lambda e: e.tensor_reduce(r1, s, AX.X, ALU.max, negate=True), t)
        t = ph.dve(lambda e: e.tensor_tensor(s, s, bc8(r1), ALU.add), t)
        t = ph.act(lambda e: e.activation(s, s, ACT.Exp), t)
        t = ph.dve(lambda e: e.tensor_reduce(r2, s, AX.X, ALU.add), t)
        t = ph.dve(lambda e: e.reciprocal(r2, r2), t)
        return ph.dve(lambda e: e.tensor_tensor(s, s, bc8(r2), ALU.mult), t)

    def logits(ph, w, t_w, t_xn, lhs=None, n=NT, k=128):
        for i in range(n):
            l = (xnT[:, 128 * i:128 * i + 128] if lhs is None else lhs[:, 128 * i:128 * i + 128])
            tp = ph.pe(lambda e, i=i, l=l: e.matmul(ps[:, 6, 8 * i:8 * i + 8], l, w, start=True, stop=True),
                       t_w, *t_xn)
        return ph.dve(lambda e: e.tensor_copy(gs[:, 0:8 * n], ps[:, 6, 0:8 * n]), tp)

    def split3(ph, src, parts, tmp, t, eng=None):
        eng = eng or ph.dve
        t1 = eng(lambda e: e.tensor_copy(parts[0], src), t)
        t1 = eng(lambda e: e.tensor_tensor(tmp, src, parts[0], ALU.subtract), t1)
        t2 = eng(lambda e: e.tensor_copy(parts[1], tmp), t1)
        t2 = eng(lambda e: e.tensor_tensor(tmp, tmp, parts[1], ALU.subtract), t2)
        return eng(lambda e: e.tensor_copy(parts[2], tmp), t2)

    def gates_T(ph, src, gTT, n, t):
        g24 = v3(gsp, 24)[:, 0:n, :]
        parts = [g24[:, :, 8 * k:8 * k + 8] for k in range(3)]
        t = split3(ph, src, parts, v3(g3[:, 0:8 * n], 8), t)
        for c in range(n // 8):
            pb = ps[:, 6 + c, :].bitcast(BF16)
            for j in range(8):
                tp = ph.pe(lambda e, c=c, j=j, pb=pb: e.transpose(pb[0:24, 128 * j:128 * j + 128],
                                                                g24[:, 8 * c + j, :], identb), t, t_c)
            td = ph.dve(lambda e, c=c, pb=pb: e.tensor_copy(gTT[0:24, 1024 * c:1024 * c + 1024], pb[0:24, :]), tp)
        return td

    def spread(ph, gTT, e8, c0, bank, *after):
        return ph.pe(lambda e: e.matmul(ps[:, bank, :], cb[0:24, 128 + 128 * e8:256 + 128 * e8],
                                        gTT[0:24, c0:c0 + CW], start=True, stop=True), *after)

    def combine(ph, c, prod, t_prod, bank, t_bank):
        for j in range(4):
            tp = ph.pe(lambda e, j=j: e.transpose(ps[:, bank, 128 * j:128 * j + 128],
                                                  prod[:, 128 * j:128 * j + 128], ident), t_prod, t_bank)
        x4 = xs[:, 4 * c:4 * c + 4, :]
        return ph.dve(lambda e: e.tensor_tensor(x4, x4, v3(ps[:, bank, :], 128), ALU.add), tp)

    O_FW = 0
    w0 = {"w1": area(0, 2048), "w2": area(2048, 2048), "w3": area(4096, 2048)}
    lnt = area(6144, 4096)
    o = 10240
    gTT = area(o, 1024).bitcast(BF16)
    sbufs = [area(o + 1024 + 512 * i, 512) for i in range(8)]
    bbufs = [area(o + 5120 + 512 * i, 512) for i in range(2)]
    wgs = area(o + 6144, 8)
    d_w0 = Dma(queues, sem("d_w0"))
    d_w0(wgs, A["L0_Wg"])
    for k in ("w1", "w2", "w3"):
        t_w0 = d_w0(w0[k], A["L0_" + k])

    p = Phase("l0f")
    t_xn = layernorm(p, [[t_x[c]] for c in range(NC)], lnt)

    def top2(ph, s, t):
        t = pick_first(ph, s, v3(oh1, 8), r1, t, NT)
        t = ph.dve(lambda e: e.scalar_tensor_tensor(out=v3(g2, 8), in0=v3(oh1, 8), scalar=BIG, in1=s,
                                                    op0=ALU.mult, op1=ALU.add), t)
        return pick_first(ph, v3(g2, 8), v3(oh2, 8), r2, t, NT)

    s3 = v3(gs, 8)
    t = logits(p, wgs, t_w0, t_xn)
    t = top2(p, s3, t)
    t = p.dve(lambda e: e.tensor_tensor(r3, r2, r1, ALU.subtract), t)
    t = p.act(lambda e: e.activation(r3, r3, ACT.Exp), t)
    t = p.dve(lambda e: e.tensor_scalar(r1, r3, 1.0, None, ALU.add), t)
    t = p.dve(lambda e: e.reciprocal(r1, r1), t)
    t = p.dve(lambda e: e.tensor_tensor(r2, r3, r1, ALU.mult), t)
    t = p.dve(lambda e: e.tensor_tensor(v3(oh1, 8), v3(oh1, 8), bc8(r1), ALU.mult), t)
    t = p.dve(lambda e: e.tensor_tensor(v3(oh2, 8), v3(oh2, 8), bc8(r2), ALU.mult), t)
    t = p.dve(lambda e: e.tensor_tensor(gate, oh1, oh2, ALU.add), t)
    t_g = gates_T(p, v3(gate, 8), gTT, NT, t)

    def experts(ph, fs, fw, up, mid, down, b_sb, x_of, t_w, t_g, fin):
        free = {b: None for b in range(8)}
        sbfree = {}
        n = 0
        ne = 0
        pend = []

        def flush():
            f = pend.pop(0)
            f()

        for c in range(NC):
            acc = 4 + c % 2
            for e8 in range(NE):
                gb = 6 + ne % 2
                tsp = spread(ph, gTT, e8, CW * c if gTT_n == NT else CW * (c % 2), gb, t_g, free[gb])
                tgt = bbufs[ne % 2]
                if x_of:
                    tb = ph.dve(lambda e, gb=gb, tgt=tgt, c=c: e.tensor_tensor(
                        tgt, xnT[:, CW * c:CW * c + CW], ps[:, gb, :], ALU.mult), tsp, sbfree.get(("b", ne % 2)))
                else:
                    tb = ph.act(lambda e, gb=gb, tgt=tgt: e.copy(tgt, ps[:, gb, :]), tsp,
                                sbfree.get(("b", ne % 2)))
                free[gb] = tb
                for f in range(len(fs)):
                    up(ph, c, e8, f, n, tgt, tb, free, sbfree, pend, acc, ne)
                    n += 1
                    if len(pend) > 1:
                        flush()
                ne += 1
            while pend:
                flush()
            fin(ph, c, acc, free)
        return

    gTT_n = NT

    def gated_up(w1, w2, w3, fs, fw, fwo, x_scaled):
        def up(ph, c, e8, f, n, tgt, tb, free, sbfree, pend, acc, ne):
            m = fs[f]
            ba, bb = (0, 1) if n % 2 == 0 else (2, 3)
            xin = tgt if x_scaled else xnT[:, CW * c:CW * c + CW]
            o1 = e8 * fw + 128 * f
            ta = ph.pe(lambda e: e.matmul(ps[0:m, ba, :], w1[:, o1:o1 + m], xin, start=True, stop=True),
                       tb if x_scaled else None, t_wcur[0], free[ba])
            tc_ = ph.pe(lambda e: e.matmul(ps[0:m, bb, :], w2[:, o1:o1 + m], xin, start=True, stop=True), free[bb])
            if x_scaled:
                sbfree[("b", ne % 2)] = tc_
            s1, u = sbufs[2 * (n % 2)], sbufs[2 * (n % 2) + 1]
            h = sbufs[4 + n % 4]
            ts = ph.act(lambda e: e.activation(s1[0:m, :], ps[0:m, ba, :], ACT.Silu), ta, sbfree.get(("s", n % 2)))
            free[ba] = ts
            if x_scaled:
                th = ph.dve(lambda e: e.tensor_tensor(h[0:m, :], s1[0:m, :], ps[0:m, bb, :], ALU.mult),
                            ts, tc_, sbfree.get(("h", n % 4)))
                free[bb] = th
                sbfree[("s", n % 2)] = th
            else:
                td = ph.dve(lambda e: e.tensor_tensor(u[0:m, :], s1[0:m, :], ps[0:m, bb, :], ALU.mult),
                            ts, tc_, sbfree.get(("u", n % 2)))
                free[bb] = td
                sbfree[("s", n % 2)] = td
                th = ph.dve(lambda e: e.tensor_tensor(h[0:m, :], u[0:m, :], tgt[0:m, :], ALU.mult),
                            td, tb, sbfree.get(("h", n % 4)))
                sbfree[("u", n % 2)] = th
                sbfree[("b", ne % 2)] = th
            k = (e8 * len(fs) + f)
            first, lastm = k == 0, (k == NE * len(fs) - 1)
            o3 = k * 128

            def down():
                t3 = ph.pe(lambda e: e.matmul(ps[:, acc, :], w3[0:m, o3:o3 + 128], h[0:m, :],
                                              start=first, stop=lastm), th, free[acc] if first else None)
                sbfree[("h", n % 4)] = t3
                free["acc"] = t3
            pend.append(down)
        return up

    def fin_silu(ph, c, acc, free):
        t = ph.act(lambda e: e.activation(gT[:, CW * c:CW * c + CW], ps[:, acc, :], ACT.Silu), free["acc"])
        free[acc] = t

    t_wcur = [t_w0]
    experts(p, [128, 128], 256, gated_up(w0["w1"], w0["w2"], w0["w3"], [128, 128], 256, 128, False),
            None, None, True, False, t_w0, t_g, fin_silu)
    end0 = p.ends()

    scr = nc.dram_tensor("scr", [2, 7, 128, T], BF16).ap()
    lscr = nc.dram_tensor("lscr", [2, 2, 512], F32).ap()
    d_ld = [Dma(queues, sem(f"d_ld{i}")) for i in range(3)]
    d_mr = Dma(queues, sem("d_mr"))
    d_lc = [Dma(queues, sem(f"d_lc{i}")) for i in range(4)]
    NP = 4
    QORD = (0, 0, 0, 1, 1, 2)
    KORD = (0, 1, 2, 0, 1, 0)

    VOFF = 0
    QOFF = 16384
    KOFF = QOFF + 3 * 2048
    POFF = KOFF + 3 * 1024
    RES = POFF + 4 * 1024
    assert RES <= AR
    acc_sb = sb("acc_sb", [128, T])
    psum_sb = sb("psum_sb", [128, 2048])
    on_sb = sb("on_sb", [128, 1024])
    osb_ = sb("osb", [128, 1024])
    rec_sb = sb("rec_sb", [128, 1024])
    lrow = sb("lrow", [64, 512])
    lcol = sb("lcol", [128, 8])
    ps2_sb = sb("ps2_sb", [128, 1024])
    mT = sb("mT", [16, 2 * 1024], BF16)
    wA = sb("wA", [128, 1280 + 1024])
    V0 = area(VOFF, 16384)
    Qs = area(QOFF, 3 * 2048).bitcast(BF16).rearrange("p (s h t) -> p s h t", s=3, h=4)
    Ks = area(KOFF, 3 * 1024).bitcast(BF16).rearrange("p (s h t) -> p s h t", s=3, h=2)
    Ps = area(POFF, 4 * 1024).rearrange("p (s t) -> p s t", s=4)
    parts = area(POFF, 4096)
    onesf = sb("onesf", [128, 64])
    t_one = None
    bias_qk = sb("bias_qk", [128, 2])
    bv = psum_sb[:, 0:1024]
    d_wa = Dma(queues, sem("d_wa0"))
    bo = sb("bo", [128, 1])
    d_wa(wA[:, 0:1280], A["L0_WcT"])
    d_wa(wA[:, 1280:2304], A["L0_WoT"])
    d_wa(bias_qk[:, :], A["L0_bqk"])
    d_wa(bo[:, :], A["L0_bo"])
    t_wa0 = d_wa(bv, A["L0_bv"].partition_broadcast(128))

    def prepare(ph, before, t_w, t_xn, leaky, fill_v):
        tz = ph.pool(lambda e: e.memset(Qs, 0.0), *before)
        tz = ph.pool(lambda e: e.memset(Ks, 1.0), *before)
        t1 = ph.pool(lambda e: e.memset(onesf[:, :], 1.0), *before)
        dd = [Dma(queues, sem(f"d_scr{i}")) for i in range(2)]
        wr = []
        last = {}
        k = 0
        for c in range(NC):
            for ty in range(2):
                bank = k % 2
                d = dd[bank]
                f0 = parts[:, 2048 * (k % 2):2048 * (k % 2) + 512]
                f1 = parts[:, 2048 * (k % 2) + 512:2048 * (k % 2) + 1024]
                pt = [parts[:, 2048 * (k % 2) + 1024 + 256 * i:2048 * (k % 2) + 1280 + 256 * i].bitcast(BF16)
                      for i in range(3)]
                lf, ld = last.get(k % 2, (None, None))
                tp = ph.pe(lambda e, ty=ty, c=c, bank=bank: e.matmul(
                    ps[:, bank, :], wA[:, 128 * ty:128 * ty + 128], xnT[:, CW * c:CW * c + CW],
                    start=True, stop=True), t_w, *t_xn, *before, lf)
                if leaky:
                    t = ph.dve(lambda e, ty=ty, bank=bank, f1=f1: e.tensor_scalar(
                        f1, ps[:, bank, :], bias_qk[:, ty:ty + 1], None, ALU.add), tp)
                    t = ph.dve(lambda e, f0=f0, f1=f1: e.scalar_tensor_tensor(
                        out=f0, in0=f1, scalar=0.01, in1=f1, op0=ALU.mult, op1=ALU.max), t)
                else:
                    t = ph.dve(lambda e, f0=f0, bank=bank: e.tensor_copy(f0, ps[:, bank, :]), tp)
                lf = t
                t = ph.dve(lambda e, f0=f0, pt=pt: e.tensor_copy(pt[0], f0), t, ld)
                t = ph.dve(lambda e, f0=f0, f1=f1, pt=pt: e.tensor_tensor(f1, f0, pt[0], ALU.subtract), t)
                t = ph.dve(lambda e, f1=f1, pt=pt: e.tensor_copy(pt[1], f1), t)
                t = ph.dve(lambda e, f1=f1, pt=pt: e.tensor_tensor(f1, f1, pt[1], ALU.subtract), t)
                t = ph.dve(lambda e, f1=f1, pt=pt: e.tensor_copy(pt[2], f1), t)
                for g, which in enumerate((QORD, KORD)[ty]):
                    td = d(scr[ty, g, :, CW * c:CW * c + CW], pt[which], t)
                if ty == 0:
                    for g in (6,):
                        td = d(scr[ty, g, :, CW * c:CW * c + CW], zero_b, t_zero)
                last[k % 2] = (lf, td)
                k += 1
            wr.append([last[0][1], last[1][1]])
        tv = fill_v(ph, before, t_w, t_xn)
        return wr, tv, [tz, t1], last

    zero_b = sb("zero_b", [128, CW], BF16)[:, :]
    t_zero = Phase("z").pool(lambda e: e.memset(zero_b, 0.0))

    def fill_v0(ph, before, t_w, t_xn):
        free = [None, None]
        tv = None
        for i in range(NT):
            for hf in range(2):
                k = (2 * i + hf) % 2
                tp = ph.pe(lambda e, i=i, hf=hf, k=k: e.matmul(
                    ps[:, 2 + k, :], xnT[:, 128 * i:128 * i + 128], wA[:, 256 + 512 * hf:768 + 512 * hf],
                    start=True, stop=True), t_w, *t_xn, *before, free[k])
                dst = V0[:, 1024 * i + 512 * hf:1024 * i + 512 * hf + 512]
                tmp = on_sb[:, 512 * k:512 * k + 512]
                t = ph.dve(lambda e, k=k, hf=hf, tmp=tmp: e.tensor_tensor(
                    tmp, ps[:, 2 + k, :], bv[:, 512 * hf:512 * hf + 512], ALU.add), tp)
                free[k] = t
                tv = ph.dve(lambda e, tmp=tmp, dst=dst: e.scalar_tensor_tensor(
                    out=dst, in0=tmp, scalar=0.01, in1=tmp, op0=ALU.mult, op1=ALU.max), t)
        return tv

    d_w1a, t_w1a = Dma(queues, sem("d_w1a")), []

    def softmax_heads(ph, prep, scale):
        wr, tv, tcst, last = prep
        NQ = 8
        slot_free = [[], [], []]
        ld_tok, mrow = {}, {}

        def load(g):
            b, q, s = g // 4, g % 4, g % 3
            d = d_ld[s]
            for h in range(4):
                hh = 4 * q + h
                r0 = 64 * (h % 2)
                tok = d(Qs[r0:r0 + 56, s, h, :], scr[0, :, 8 * hh:8 * hh + 8, 1024 * b:1024 * b + 1024],
                        *wr[2 * b + 1], *slot_free[s], *tcst)
                tok = d(Ks[r0:r0 + 48, s, h // 2, :], scr[1, 0:6, 8 * hh:8 * hh + 8, 1024 * b:1024 * b + 1024])
            ld_tok[g] = tok

        negm = [nm[:, 0:64], nm[:, 64:128]]
        bank_free = {b: [x for x in ph.ends()] for b in range(8)}
        negm_free = [None, None]
        mT_free = [None, None]

        def max_half(g, j, bank):
            s = g % 3
            h, qt, hf = j // 16, (j // 2) % 8, j % 2
            tp = ph.pe(lambda e: e.matmul(
                ps[:, bank, :], Qs[:, s, h, 128 * qt:128 * qt + 128],
                Ks[:, s, h // 2, 512 * hf:512 * hf + 512], start=True, stop=True),
                ld_tok[g], *bank_free[bank])
            t = ph.dve(lambda e: e.tensor_reduce(negm[g % 2][:, j:j + 1], ps[:, bank, :],
                                                 AX.X, ALU.max, negate=True), tp, negm_free[g % 2])
            bank_free[bank] = [t]
            return t

        def max_rows(g, t):
            s, k = g % 3, g % 2
            nv = negm[k].rearrange("p (a f) -> p a f", f=2)
            mn = g2[:, 0:32]
            t = ph.dve(lambda e: e.tensor_reduce(mn, nv, AX.X, ALU.min), t)
            negm_free[k] = t
            sp = nsp[:, 96 * k:96 * k + 96].rearrange("p (q h r) -> p h q r", q=8, h=4)
            src = mn.rearrange("p (h q) -> p h q", h=4)
            tmp = g1[:, 0:32].rearrange("p (h q) -> p h q", h=4)
            t = split3(ph, src, [sp[:, :, :, r] for r in range(3)], tmp, t)
            pb = ps[:, 4, :].bitcast(BF16)
            for qt in range(8):
                tp = ph.pe(lambda e, qt=qt: e.transpose(pb[0:12, 128 * qt:128 * qt + 128],
                                                        nsp[:, 96 * k + 12 * qt:96 * k + 12 * qt + 12], identb),
                           t, *bank_free[4])
            t = ph.dve(lambda e: e.tensor_copy(mT[0:12, 1024 * k:1024 * k + 1024], pb[0:12, :]), tp, mT_free[k])
            bank_free[4] = [t]
            for h in range(4):
                r0 = 64 * (h % 2) + 48
                tok = d_mr(Qs[r0:r0 + 3, s, h, :], mT[3 * h:3 * h + 3, 1024 * k:1024 * k + 1024], t)
            mT_free[k] = tok
            mrow[g] = tok

        load(0)
        load(1)
        for j in range(64):
            t = max_half(0, j, j % 8)
        max_rows(0, t)

        exp_tok, st_tok, pv_tok, add_tok = {}, {}, {}, {}
        tail = {}
        sched = [(g, hf, pr, kt) for g in range(NQ) for hf in range(2) for pr in range(2) for kt in range(8)]

        def pv(i):
            g, hf, pr, kt = sched[i]
            bank = 6 + (i // 8) % 2
            pbuf = Ps[:, i % NP, :]
            tile = 8 * (g // 4) + kt
            for a in range(2):
                h = 4 * (g % 4) + 2 * pr + a
                o_ap = ps[64 * a:64 * a + 64, bank, :]
                w_ap = V0[:, 1024 * tile + 64 * h:1024 * tile + 64 * h + 64]
                pv_tok[i] = ph.pe(lambda e, o_ap=o_ap, w_ap=w_ap, a=a: e.matmul(
                    o_ap, w_ap, pbuf[:, 512 * a:512 * a + 512], start=(kt == 0), stop=(kt == 7)),
                    exp_tok[i], tv, *(bank_free[bank] if kt == 0 else []))

        def adds(i):
            u, k = i // 8, i % 8
            a_, b_ = psum_sb[:, 1024 * (u % 2):1024 * (u % 2) + 1024], ps2_sb[:, :]
            if k == 1:
                add_tok[i] = add_tok[i - 1] = ph.pool(lambda e: e.tensor_tensor(
                    a_, Ps[:, (i - 1) % NP, :], Ps[:, i % NP, :], ALU.add), exp_tok[i], tail.get(("sum", u - 2)))
            elif 2 <= k <= 5:
                add_tok[i] = ph.pool(lambda e: e.tensor_tensor(a_, a_, Ps[:, i % NP, :], ALU.add),
                                     exp_tok[i], add_tok[i - 1])
                if k == 5:
                    tail[("pool", u)] = add_tok[i]
            elif k == 7:
                add_tok[i] = add_tok[i - 1] = ph.dve(lambda e: e.tensor_tensor(
                    b_, Ps[:, (i - 1) % NP, :], Ps[:, i % NP, :], ALU.add), exp_tok[i])
                tail[("dve", u)] = add_tok[i]

        def unit_tail(u, k):
            if u < 0 or u >= 32:
                return
            g, hf, pr, _ = sched[8 * u]
            b = g // 4
            bank = 6 + u % 2
            c0 = 1024 * b + 512 * hf
            m = u % 2
            on = on_sb[:, 512 * m:512 * m + 512]
            osb = osb_[:, 512 * m:512 * m + 512]
            a_ = psum_sb[:, 1024 * m:1024 * m + 1024]
            if k == 1:
                t = ph.act(lambda e: e.copy(osb, ps[:, bank, :]), pv_tok[8 * u + 7], tail.get(("on", u - 2)))
                tail[("osb", u)] = t
                bank_free[bank] = [t]
            if k == 1:
                tail[("tot", u)] = ph.dve(lambda e: e.tensor_tensor(a_, a_, ps2_sb[:, :], ALU.add),
                                          tail[("pool", u)], tail[("dve", u)])
            if k == 2:
                for a in range(2):
                    t = ph.pe(lambda e, a=a: e.matmul(ps[32 * a:32 * a + 32, 5, :], onesf[:, 0:32],
                                                      a_[:, 512 * a:512 * a + 512], start=True, stop=True),
                              tail[("tot", u)], *bank_free[5])
                tail[("sum", u)] = t
                t = ph.act(lambda e: e.copy(lrow[0:64, :], ps[0:64, 5, :]), t, tail.get(("lc", u - 1)))
                bank_free[5] = [t]
                tl = d_lc[0](lcol[:, :], lrow[0:64:32, :], t, tail.get(("ld", u - 1)))
                tail[("lc", u)] = tl
            if k == 4:
                t = ph.dve(lambda e: e.reciprocal(lcol[:, :], lcol[:, :]), tail[("lc", u)])
                tl = d_lc[1](lscr[m], lcol[:, :], t, tail.get(("rec", u - 2)))
                tail[("ld", u)] = tl
                for a in range(2):
                    tl = d_lc[2 + m](rec_sb[64 * a:64 * a + 64, 512 * m:512 * m + 512],
                                     lscr[m, a].partition_broadcast(64), tail[("ld", u)], tail.get(("on", u - 2)))
                tail[("rec", u)] = tl
            if k == 8:
                tail[("on", u)] = ph.dve(lambda e: e.tensor_tensor(on, osb, rec_sb[:, 512 * m:512 * m + 512],
                                                                   ALU.mult),
                                         tail[("rec", u)], tail[("osb", u)], tail.get(("pr", u - 2)))
            if k == 9:
                pi = 2 * (g % 4) + pr
                t = ph.pe(lambda e: e.matmul(ps[:, 5, :], wA[:, 1280 + 128 * pi:1408 + 128 * pi], on,
                                             start=True, stop=True), tail[("on", u)], *bank_free[5])
                tail[("pr", u)] = t
                dst = acc_sb[:, c0:c0 + CW]
                if pi == 0:
                    t = ph.dve(lambda e: e.tensor_copy(dst, ps[:, 5, :]), t)
                else:
                    t = ph.dve(lambda e: e.tensor_tensor(dst, dst, ps[:, 5, :], ALU.add), t, tail[("acc", c0)])
                tail[("acc", c0)] = t
                bank_free[5] = [t]

        MS = 27
        for i, (g, hf, pr, kt) in enumerate(sched):
            s = g % 3
            loc = i % 32
            if loc == 0 and g + 2 < NQ:
                load(g + 2)
            if loc == 8 and g == NQ - 3:
                for e8 in range(NE - 1):
                    t_w1a.append(d_w1a(ar[:, 1088 * e8:1088 * e8 + 1088],
                                       A["L1_w"][:, 1088 * e8:1088 * e8 + 1088], pv_tok[127]))
            b0 = 2 * (i % 2)
            for a in range(2):
                st_tok[i] = ph.pe(lambda e, a=a, b0=b0, s=s, pr=pr, kt=kt, hf=hf: e.matmul(
                    ps[:, b0 + a, :], Ks[:, s, pr, 128 * kt:128 * kt + 128],
                    Qs[:, s, 2 * pr + a, 512 * hf:512 * hf + 512], start=True, stop=True),
                    mrow[g], *bank_free[b0], *bank_free[b0 + 1])
            ex = ph.act(lambda e, b0=b0, i=i: e.activation(
                Ps[:, i % NP, :], ps[:, b0:b0 + 2, :].rearrange("p a t -> p (a t)"), ACT.Exp, scale=scale),
                st_tok[i], pv_tok.get(i - NP), add_tok.get(i - NP), last[0][1], last[1][1])
            exp_tok[i] = ex
            bank_free[b0] = bank_free[b0 + 1] = [ex]
            js = list(range(loc * 64 // MS, (loc + 1) * 64 // MS)) if g + 1 < NQ and loc < MS else []
            for j in js[:1]:
                tmx = max_half(g + 1, j, 4 + j % 2)
            unit_tail(i // 8 - 1, i % 8)
            unit_tail(i // 8 - 2, i % 8 + 8)
            if i >= 1:
                pv(i - 1)
            for j in js[1:]:
                tmx = max_half(g + 1, j, 4 + j % 2)
            adds(i)
            if g + 1 < NQ and loc == MS:
                max_rows(g + 1, tmx)
            if loc == 31:
                slot_free[s] = [st_tok[i]]
        pv(i)
        for x in range(256, 256 + 16):
            unit_tail(x // 8 - 1, x % 8)
            unit_tail(x // 8 - 2, x % 8 + 8)
        return tail

    p = Phase("l0a")
    prep = prepare(p, end0, t_wa0, t_xn, True, fill_v0)
    tail = softmax_heads(p, prep, float(1.0 / np.sqrt(8.0)))
    t_x1 = []
    bank_t = p.ends()
    for c in range(NC):
        a = acc_sb[:, CW * c:CW * c + CW]
        tm = on_sb[:, 512 * (c % 2):512 * (c % 2) + 512]
        t = p.dve(lambda e, a=a: e.tensor_scalar(a, a, bo[:, 0:1], None, ALU.add), tail[("acc", CW * c)])
        t = p.dve(lambda e, a=a: e.scalar_tensor_tensor(out=a, in0=a, scalar=0.01, in1=a,
                                                        op0=ALU.mult, op1=ALU.max), t)
        t = p.dve(lambda e, a=a, c=c: e.tensor_tensor(a, a, xnT[:, CW * c:CW * c + CW], ALU.add), t)
        t = p.dve(lambda e, a=a, c=c: e.tensor_tensor(a, a, gT[:, CW * c:CW * c + CW], ALU.mult), t)
        t_x1.append(combine(p, c, a, t, c, p.act.last()))
    end = p.ends()

    tk = {}
    free = {b: list(end) for b in range(8)}
    p = Phase("l123")
    pe, dve, act, pool = p.pe, p.dve, p.act, p.pool

    def mm(o_, l, r, *w, start=True, stop=True):
        return pe(lambda e: e.matmul(o_, l, r, start=start, stop=stop), *w)

    def tr(o_, i_, idn, *w):
        return pe(lambda e: e.transpose(o_, i_, idn), *w)

    def tt(eng, o_, a, b, op, *w):
        return eng(lambda e: e.tensor_tensor(o_, a, b, op), *w)

    def ts(o_, a, s0, s1, op0, op1, *w):
        if op1 is None:
            return dve(lambda e: e.tensor_scalar(o_, a, s0, None, op0), *w)
        return dve(lambda e: e.tensor_scalar(o_, a, s0, s1, op0, op1), *w)

    def stt(o_, a, s, b, op0, op1, *w):
        return dve(lambda e: e.scalar_tensor_tensor(out=o_, in0=a, scalar=s, in1=b, op0=op0, op1=op1), *w)

    def red(o_, a, op, *w, negate=False):
        if negate:
            return dve(lambda e: e.tensor_reduce(o_, a, AX.X, op, negate=True), *w)
        return dve(lambda e: e.tensor_reduce(o_, a, AX.X, op), *w)

    def cp(eng, o_, a, *w):
        return eng(lambda e: e.tensor_copy(o_, a), *w)

    def acp(o_, a, *w):
        return act(lambda e: e.copy(o_, a), *w)

    def af(o_, a, fn, *w, **kw):
        return act(lambda e: e.activation(o_, a, fn, **kw), *w)

    W = [area(1088 * e8, 1088) for e8 in range(NE)]
    R = 8704
    FB = 16304
    s_buf = [area(FB + 512 * i, 512) for i in range(2)]
    h_buf = [area(FB + 1024 + 512 * i, 512) for i in range(4)]
    tg_buf = [area(FB + 3072 + 512 * i, 512) for i in range(2)]
    pr1 = [area(20400 + 2048 * k, 2048) for k in range(2)]
    pr2 = [area(24496 + 2048 * k, 2048) for k in range(2)]
    pe_sb = pr1[0][0:32, 0:1024]
    qkv = [area(28592 + 384 * k, 384) for k in range(2)]
    sc2 = [area(29360 + 256 * k, 256) for k in range(2)]
    st2 = [area(29872 + 64 * k, 64) for k in range(2)]
    gTT1 = psum_sb[:, 0:1024].bitcast(BF16)
    gTT3 = psum_sb[:, 1024:2048].bitcast(BF16)
    gTT2 = osb_[:, 0:512].bitcast(BF16)
    ot2 = [osb_[:, 512 + 128 * k:640 + 128 * k] for k in range(2)]
    b2sp = osb_[:, 768:1024]
    w2l = on_sb[:, :]
    lt = [rec_sb[:, 0:512], rec_sb[:, 512:1024]]
    oT2 = [ps2_sb[:, 0:512], ps2_sb[:, 512:1024]]

    def M(name):
        o_, n_ = MISC_COLS[name]
        return wA[:, o_:o_ + n_]

    d_ml = Dma(queues, sem("d_ml"))
    t_ml = d_ml(wA[:, 0:MISC_N], A["misc"], *end)
    d_w1b = Dma(queues, sem("d_w1b"))
    t_w1b = d_w1b(W[7], A["L1_w"][:, 7 * 1088:8 * 1088], *end)
    d_w2 = Dma(queues, sem("d_w2"))
    d_w2(pe_sb, A["cf"][0:32, CF_KEPT:CF_KEPT + 1024])
    t_w2 = d_w2(w2l, A["L2_W"])
    d_w3 = [Dma(queues, sem(f"d_w3_{e8}")) for e8 in range(NE)]

    mi = [0]

    def take():
        mi[0] += 1
        return 6 + mi[0] % 2

    def until(*keys):
        while any(k not in tk for k in keys):
            yield "blocked"

    def g_ln(layer, c, buf):
        yield from until(("x", layer, c))
        x4 = xs[:, 4 * c:4 * c + 4, :]
        sl = slice(4 * c, 4 * c + 4)
        m4, v4, s4 = mu[:, sl], var[:, sl], rstd[:, sl]
        dst = xnT[:, CW * c:CW * c + CW]
        xc, sq = v3(buf, 128), v3(dst, 128)
        t = red(m4, x4, ALU.add, tk["x", layer, c])
        t = ts(m4, m4, -1.0 / 128, None, ALU.mult, None, t)
        t = tt(dve, xc, x4, m4.unsqueeze(2).to_broadcast([128, 4, 128]), ALU.add, t)
        t = af(sq, xc, ACT.Square, t)
        yield
        t = red(v4, sq, ALU.add, t)
        t = ts(v4, v4, 1.0 / 128, EPS, ALU.mult, ALU.add, t)
        t = af(s4, v4, ACT.Sqrt, t)
        yield
        t = dve(lambda e: e.reciprocal(s4, s4), t)
        t = tt(dve, xc, xc, s4.unsqueeze(2).to_broadcast([128, 4, 128]), ALU.mult, t)
        yield
        b = take()
        for j in range(4):
            t1 = tr(ps[:, b, 128 * j:128 * j + 128], xc[:, j, :], ident, t, *free[b])
        t = acp(dst, ps[:, b, :], t1)
        free[b] = [t]
        tk["xn", layer, c] = t
        yield

    def first_of(s, oh, m, g, q, t):
        n = s.shape[1]
        t = red(m, s, ALU.max, t)
        t = tt(dve, g, s, bc8(m), ALU.is_equal, t)
        t = tt(dve, g, g, C("w8").unsqueeze(1).to_broadcast([128, n, 8]), ALU.mult, t)
        t = red(q, g, ALU.max, t)
        return tt(dve, oh, g, bc8(q), ALU.is_equal, t)

    def g_split_T(src, n, gT_, c0, key, t):
        tmp = v3(g3, 8)[:, c0 // 128:c0 // 128 + n, :]
        g24 = v3(gsp, 24)[:, c0 // 128:c0 // 128 + n, :]
        t = cp(dve, g24[:, :, 0:8], src, t)
        t = tt(dve, tmp, src, g24[:, :, 0:8], ALU.subtract, t)
        t = cp(dve, g24[:, :, 8:16], tmp, t)
        t = tt(dve, tmp, tmp, g24[:, :, 8:16], ALU.subtract, t)
        t = cp(dve, g24[:, :, 16:24], tmp, t)
        yield
        b = take()
        pb = ps[:, b, :].bitcast(BF16)
        for j in range(n):
            tp = tr(pb[0:24, 128 * j:128 * j + 128], g24[:, j, :], identb, t, *free[b])
        t = cp(dve, gT_[0:24, c0:c0 + 128 * n], pb[0:24, 0:128 * n], tp)
        free[b] = [t]
        tk[key] = t
        yield

    def g_gates(layer, c):
        yield from until(("xn", layer, c))
        sl, wd = slice(32 * c, 32 * c + 32), slice(4 * c, 4 * c + 4)
        w_ = M("wg1" if layer == 1 else "wg3")
        s, a, g, o1, o2, gt = (v3(x[:, sl], 8) for x in (gs, g1, g3, oh1, oh2, gate))
        m, q = r1[:, wd], r2[:, wd]
        b = take()
        for j in range(4):
            i0 = CW * c + 128 * j
            tp = mm(ps[:, b, 8 * j:8 * j + 8], xnT[:, i0:i0 + 128], w_, tk["xn", layer, c], t_ml, *free[b])
        pv_ = v3(ps[:, b, 0:32], 8)
        if layer == 1:
            t = cp(dve, s, pv_, tp)
        else:
            t = tt(dve, s, pv_, M("bg").unsqueeze(1).to_broadcast([128, 4, 8]), ALU.add, tp)
        free[b] = [t]
        t = red(m, s, ALU.max, t, negate=True)
        t = tt(dve, s, s, bc8(m), ALU.add, t)
        t = af(s, s, ACT.Exp, t)
        yield
        t = red(m, s, ALU.add, t)
        t = dve(lambda e: e.reciprocal(m, m), t)
        t = tt(dve, s, s, bc8(m), ALU.mult, t)
        if layer == 1:
            t = tt(dve, a, s, M("eb").unsqueeze(1).to_broadcast([128, 4, 8]), ALU.add, t)
            t = first_of(a, o1, m, g, q, t)
            t = stt(a, o1, BIG, a, ALU.mult, ALU.add, t)
            yield
            t = first_of(a, o2, m, g, q, t)
            t = tt(dve, o1, o1, o2, ALU.add, t)
        else:
            t = first_of(s, o1, m, g, q, t)
        t = tt(dve, gt, o1, s, ALU.mult, t)
        yield
        yield from g_split_T(gt, 4, gTT1 if layer == 1 else gTT3, CW * c, ("g", layer, c), t)

    def g_bias(name, dst, key):
        b_ = M(name)[0:24, :]
        tmp = wA[0:24, MISC_N:MISC_N + 128]
        t = cp(dve, dst[0], b_, t_ml)
        t = tt(dve, tmp, b_, dst[0], ALU.subtract, t)
        t = cp(dve, dst[1], tmp, t)
        t = tt(dve, tmp, tmp, dst[1], ALU.subtract, t)
        tk[key] = cp(dve, dst[2], tmp, t)
        yield

    bp2 = [wA[0:24, MISC_N + 128 + 64 * i:MISC_N + 192 + 64 * i].bitcast(BF16) for i in range(3)]
    bp3 = [wA[0:24, MISC_N + 320 + 64 * i:MISC_N + 384 + 64 * i].bitcast(BF16) for i in range(3)]

    def g_position():
        yield from until(("g", 1, 0), ("g", 1, 1))
        sg = M("sig")[0:32, :]
        t = ts(b8[0:32, 0:8], sg, 0.0, None, ALU.is_gt, None, t_ml)
        t = ts(b8[0:32, 8:16], sg, 0.0, None, ALU.is_lt, None, t)
        t = tt(dve, b8[0:32, 0:8], b8[0:32, 0:8], b8[0:32, 8:16], ALU.subtract, t)
        yield
        b = take()
        for j in range(8):
            tp = mm(ps[:, b, 8 * j:8 * j + 8], pe_sb[:, 128 * j:128 * j + 128], b8[0:32, 0:8], t, t_w2, *free[b])
        s, g, q = v3(gs[:, 0:64], 8), v3(oh2[:, 0:64], 8), v3(oh1[:, 0:64], 8)
        t = cp(dve, s, v3(ps[:, b, 0:64], 8), tp)
        free[b] = [t]
        tk["pe_read"] = tp
        t = first_of(s, q, r1[:, 0:8], g, r2[:, 0:8], t)
        yield
        yield from g_split_T(q, 8, gTT2, 0, "pos", t)

    wt, wjt, gt_, gjt = (area(R + 128 * i, 128) for i in range(4))
    tabc, tabs, tmpt = area(R + 512, 1024), area(R + 1536, 1024), area(R + 2560, 512)
    bb_ = [area(R + 3072 + 512 * i, 512) for i in range(2)]
    bj_ = [area(R + 4096 + 512 * i, 512) for i in range(2)]
    zz = area(R + 5120, 2048)

    def g_tables():
        tm_ = None
        for dst, l, r in ((wt, M("bw"), C("ft")), (wjt, M("bw"), C("jft")), (gt_, C("fi"), M("cw")),
                          (gjt, C("fij"), M("cw"))):
            b = take()
            tp = mm(ps[:, b, 0:128], l, r, t_ml, *free[b])
            tm_ = cp(dve, dst, ps[:, b, 0:128], tp)
            free[b] = [tm_]
            yield
        tk["mats"] = tm_
        b = take()
        tp = mm(ps[:, b, 0:1], C("sm")[0:64, :], M("asc")[0:64, :], t_ml, *free[b])
        om, w2_, dn, rd, cr, ci, u1, u2 = (scn[:, i:i + 1] for i in range(8))
        t = cp(dve, om, ps[:, b, 0:1], tp)
        free[b] = [t]
        t = tt(dve, w2_, om, om, ALU.mult, t)
        t = ts(dn, w2_, 1.0, None, ALU.add, None, t)
        t = dve(lambda e: e.reciprocal(rd, dn), t)
        t = ts(cr, w2_, -1.0, 1.0, ALU.mult, ALU.add, t)
        t = tt(dve, cr, cr, rd, ALU.mult, t)
        t = ts(ci, om, -2.0, None, ALU.mult, None, t)
        t = tt(dve, ci, ci, rd, ALU.mult, t)
        dve.quiet(lambda e: e.memset(tabs[:, 0:1], 0.0))
        t = dve(lambda e: e.memset(tabc[:, 0:1], 1.0), t)
        m = 1
        while m < 1024:
            t = ts(tmpt[:, 0:m], tabs[:, 0:m], ci, None, ALU.mult, None, t)
            t = stt(tabc[:, m:2 * m], tabc[:, 0:m], cr, tmpt[:, 0:m], ALU.mult, ALU.subtract, t)
            t = ts(tmpt[:, 0:m], tabc[:, 0:m], ci, None, ALU.mult, None, t)
            t = stt(tabs[:, m:2 * m], tabs[:, 0:m], cr, tmpt[:, 0:m], ALU.mult, ALU.add, t)
            m *= 2
            if m < 1024:
                t = tt(dve, u1, ci, ci, ALU.mult, t)
                t = tt(dve, u2, cr, ci, ALU.mult, t)
                t = stt(cr, cr, cr, u1, ALU.mult, ALU.subtract, t)
                t = ts(ci, u2, 2.0, None, ALU.mult, None, t)
            yield
        tk["tab"] = t

    def g_rec(c):
        yield from until(("xn", 1, c), "tab", "mats", *([("recout", c - 2)] if c > 1 else []))
        x_ = xnT[:, CW * c:CW * c + CW]
        k0 = 512 * (c % 2)
        tc_, tn_ = tabc[:, k0:k0 + 512], tabs[:, k0:k0 + 512]
        bb, bj, z = bb_[c % 2], bj_[c % 2], zz[:, CW * c:CW * c + CW]
        b = take()
        tp = mm(ps[:, b, :], wt, x_, tk["mats"], tk["xn", 1, c], *free[b])
        t1 = tt(dve, bb, tc_, ps[:, b, :], ALU.mult, tp, tk["tab"], tk.get(("recout", c - 2)))
        free[b] = [t1]
        yield
        b = take()
        tp = mm(ps[:, b, :], wjt, x_, *free[b])
        t1 = tt(dve, bj, tn_, ps[:, b, :], ALU.mult, tp)
        free[b] = [t1]
        yield
        t = tt(dve, bb, bb, bj, ALU.add, t1)
        init = 0.0 if c % 2 == 0 else zz[:, CW * c - 1:CW * c]
        t = dve(lambda e: e.tensor_tensor_scan(z, bb, bb, init, ALU.add, ALU.bypass), t)
        yield
        t = tt(dve, bb, tc_, z, ALU.mult, t)
        t = tt(dve, bj, tn_, z, ALU.mult, t)
        yield
        b = take()
        mm(ps[:, b, :], gt_, bb, t, *free[b], stop=False)
        tp = mm(ps[:, b, :], gjt, bj, start=False)
        t = stt(bb, x_, M("dcol"), ps[:, b, :], ALU.mult, ALU.add, tp)
        free[b] = [t]
        tk["s", 1, c] = t
        yield

    def g_combine(layer, c, a, key, t):
        b = take()
        for j in range(4):
            tp = tr(ps[:, b, 128 * j:128 * j + 128], a[:, 128 * j:128 * j + 128], ident, t, *free[b])
        x4 = xs[:, 4 * c:4 * c + 4, :]
        t = tt(dve, x4, x4, v3(ps[:, b, :], 128), ALU.add, tp)
        free[b] = [t]
        tk["tr", layer, c] = tp
        tk["x", layer + 1, c] = t
        yield

    def g_end1(c):
        yield from until(("s", 1, c), ("gT", 1, c))
        bb = bb_[c % 2]
        t = tt(dve, bb, bb, gT[:, CW * c:CW * c + CW], ALU.mult, tk["s", 1, c], tk["gT", 1, c])
        yield
        yield from g_combine(1, c, bb, None, t)
        tk["recout", c] = tk["tr", 1, c]

    def g_ffn2(c):
        yield from until(("xn", 2, c), "pos", "b2")
        while tk.get("bank5"):
            yield "blocked"
        tk["bank5"] = True
        x_ = xnT[:, CW * c:CW * c + CW]
        c0 = CW * (c % 2)
        for e8 in range(NE):
            b = take()
            sp = mm(ps[:, b, :], cb[0:24, 128 + 128 * e8:256 + 128 * e8], gTT2[0:24, c0:c0 + CW],
                    tk["pos"], *free[b])
            xb = acc_sb[:, 512 * (e8 % 2):512 * (e8 % 2) + 512]
            t = tt(dve, xb, x_, ps[:, b, :], ALU.mult, sp, tk["xn", 2, c], tk.get(("xb", e8 % 2)))
            free[b] = [t]
            yield
            tk["xb", e8 % 2] = mm(ps[:, 5, :], w2l[:, 128 * e8:128 * e8 + 128], xb, t, t_w2,
                                  *(free[5] if e8 == 0 else []), start=(e8 == 0), stop=False)
        for i in range(3):
            tp = mm(ps[:, 5, :], bp2[i], gTT2[0:24, c0:c0 + CW], tk["b2"], start=False, stop=(i == 2))
        t = af(gT[:, CW * c:CW * c + CW], ps[:, 5, :], ACT.Silu, tp)
        free[5] = [t]
        tk["bank5"] = False
        tk["gT", 2, c] = t
        yield

    def g_tile(i):
        k, c = i % 2, i // 4
        yield from until(("xn", 2, c), "pos")
        q_, s, ls = qkv[k], sc2[k], st2[k][:, 16:32]
        mx = st2[k][:, 0:16]
        s3_ = s.rearrange("p (h g) -> p h g", g=16)
        b = take()
        tp = mm(ps[:, b, 0:384], xnT[:, 128 * i:128 * i + 128], wA[:, 0:384], tk["xn", 2, c], t_ml, *free[b])
        t = acp(q_, ps[:, b, 0:384], tp, tk.get(("p2", k)), tk.get(("p2g", k)))
        free[b] = [t]
        q4 = q_[:, 0:128].rearrange("p (h d) -> p h d", d=8).unsqueeze(2).to_broadcast([128, 16, 16, 8])
        k4 = q_[:, 128:256].rearrange("p (g d) -> p g d", d=8).unsqueeze(1).to_broadcast([128, 16, 16, 8])
        t = tt(pool, pr1[k].rearrange("p (h g d) -> p h g d", h=16, g=16), q4, k4, ALU.mult, t,
               tk.get(("r1", k)), tk["pe_read"])
        yield
        yield
        p1 = pr1[k].rearrange("p (a d) -> p a d", d=8)
        t1 = red(s[:, 0:128], p1[:, 0:128, :], ALU.add, t)
        yield
        t = red(s[:, 128:256], p1[:, 128:256, :], ALU.add, t1)
        tk["r1", k] = t
        t = red(mx, s3_, ALU.max, t, negate=True)
        t = tt(dve, s3_, s3_, mx.unsqueeze(2).to_broadcast([128, 16, 16]), ALU.add, t)
        t = af(s, s, ACT.Exp, t, scale=0.125)
        yield
        v4 = q_[:, 256:384].rearrange("p (g d) -> p d g", d=8).unsqueeze(1)
        s4 = s3_.unsqueeze(2)
        o4 = pr2[k].rearrange("p (h d g) -> p h d g", h=16, d=8)
        n1, n2 = HD, 16 - HD
        tg = tk["p2g", k] = tt(pool, o4[:, n1:16, :, :], s4[:, n1:16, :, :].to_broadcast([128, n2, 8, 16]),
                               v4.to_broadcast([128, n2, 8, 16]), ALU.mult, t, tk.get(("r2", k)))
        t0 = red(ls, s3_, ALU.add, t)
        t0 = dve(lambda e: e.reciprocal(ls, ls), t0)
        td = tk["p2", k] = tt(dve, o4[:, 0:n1, :, :], s4[:, 0:n1, :, :].to_broadcast([128, n1, 8, 16]),
                              v4.to_broadcast([128, n1, 8, 16]), ALU.mult, t, tk.get(("r2", k)))
        yield
        yield
        p2 = pr2[k].rearrange("p (a g) -> p a g", g=16)
        t = red(ot2[k][:, 0:64], p2[:, 0:64, :], ALU.add, td, tg, tk.get(("trt", k)))
        yield
        t = tk["r2", k] = red(ot2[k][:, 64:128], p2[:, 64:128, :], ALU.add, tg, t)
        t = tt(dve, v3(ot2[k], 8), v3(ot2[k], 8), bc8(ls), ALU.mult, t, t0)
        yield
        b = take()
        tp = tk["trt", k] = tr(ps[:, b, 0:128], ot2[k], ident, t, *free[b])
        t = acp(oT2[c % 2][:, 128 * (i % 4):128 * (i % 4) + 128], ps[:, b, 0:128], tp, tk.get(("proj", c - 2)))
        free[b] = [t]
        tk["tile", i] = t
        yield

    def g_end2(c):
        yield from until(*[("tile", 4 * c + j) for j in range(4)], ("gT", 2, c))
        b = take()
        tp = tk["proj", c] = mm(ps[:, b, :], wA[:, 384:512], oT2[c % 2], tk["tile", 4 * c + 3],
                                tk["tile", 4 * c + 2], *free[b])
        a = acc_sb[:, 1024:1536]
        t = stt(a, ps[:, b, :], M("bp"), gT[:, CW * c:CW * c + CW], ALU.add, ALU.mult, tp, tk["gT", 2, c],
                tk.get(("tr", 2, c - 1)))
        free[b] = [t]
        yield
        yield from g_combine(2, c, a, None, t)

    qT3, kT3, v3_ = area(R, 1024), area(R + 1024, 1024), area(R + 2048, 1024)
    scb = [area(R + 3072 + 512 * i, 512) for i in range(4)]
    dt_sb = area(R + 5120, 1024)
    d_dt = Dma(queues, sem("d_dt"))
    d_out = Dma(queues, sem("d_out"))
    ov = out.rearrange("b (t p) d -> p (b t) d", p=128)
    ex = scn[:, 0:1]

    def g_l3start():
        yield from until(("x", 2, 3), ("x", 2, 2))
        w_ = [tk["x", 2, 3], tk["x", 2, 2], tk["tr", 1, 3]]
        tk["dt"] = d_dt(dt_sb, A["cf"][:, CF_KEPT + 1024:CF_N], *w_)
        t = ts(ex, M("th"), 0.0, None, ALU.mult, None, *w_)
        tk["ex"] = af(ex, ex, ACT.Exp, t)
        yield

    def g_att3(c):
        yield from until(("xn", 3, c), "ex")
        hf = c % 2
        x_ = xnT[:, CW * c:CW * c + CW]
        o_ = 512 * hf
        w_ = [tk["dt"], tk.get(("pv3", c - 1))] if hf == 0 else []
        for w3_, dst in ((M("wq"), qT3), (M("wk"), kT3)):
            b = take()
            tp = mm(ps[:, b, :], w3_, x_, tk["xn", 3, c], *free[b])
            t = ts(dst[:, o_:o_ + 512], ps[:, b, :], ex, None, ALU.mult, None, tp, tk["ex"], *w_)
            free[b] = [t]
            yield
        t_qk = t
        b = take()
        for j in range(4):
            i0 = CW * c + 128 * j
            tp = mm(ps[:, b, 128 * j:128 * j + 128], xnT[:, i0:i0 + 128], M("wv"), *free[b])
        t_v = acp(v3_[:, o_:o_ + 512], ps[:, b, :], tp, *w_)
        free[b] = [t_v]
        yield
        while tk.get("bank5"):
            yield "blocked"
        tk["bank5"] = True
        nb = 4 * (hf + 1)
        pend3 = []

        def pv3(jb, i0, t):
            tk["pv3", c] = tk["scb", jb % 4] = mm(
                ps[:, 5, i0:512], v3_[:, 128 * jb:128 * jb + 128], scb[jb % 4][:, i0:512], t, t_v,
                *(free[5] if jb == 0 else []), start=(jb == 0), stop=(jb == nb - 1))

        for jb in range(nb):
            i0 = max(0, 128 * jb - o_)
            b = take()
            tp = mm(ps[:, b, i0:512], kT3[:, 128 * jb:128 * jb + 128], qT3[:, o_ + i0:o_ + 512], t_qk, *free[b])
            d0 = o_ + i0 - 128 * jb
            t = tt(dve, scb[jb % 4][:, i0:512], ps[:, b, i0:512], dt_sb[:, d0:d0 + 512 - i0], ALU.mult, tp,
                   tk["dt"], tk.get(("scb", jb % 4)))
            free[b] = [t]
            pend3.append((jb, i0, t))
            if len(pend3) > 1:
                pv3(*pend3.pop(0))
            yield
        pv3(*pend3.pop(0))
        a = acc_sb[:, 1536:2048]
        while ("gT", 3, c) not in tk:
            yield "blocked"
        t = tt(dve, a, ps[:, 5, :], gT[:, CW * c:CW * c + CW], ALU.mult, tk["pv3", c], tk["gT", 3, c],
               tk.get(("tr", 3, c - 1)))
        free[5] = [t]
        tk["bank5"] = False
        yield
        yield from g_combine(3, c, a, None, t)
        tk["out"] = d_out(ov[:, 4 * c:4 * c + 4, :], xs[:, 4 * c:4 * c + 4, :], tk["x", 4, c])

    for c in range(NC):
        tk["x", 1, c] = t_x1[c]

    def lane(*gens):
        for g_ in gens:
            yield from g_

    lanes = [
        lane(*[x for c in range(NC) for x in (g_ln(1, c, lt[0]), g_gates(1, c))],
             *[x for c in range(NC) for x in (g_end1(c), g_ln(2, c, lt[0]), g_ffn2(c))]),
        lane(g_tables(), g_rec(0), g_rec(1), g_bias("b2", bp2, "b2"), g_bias("b3", bp3, "b3"), g_position(),
             g_rec(2), g_rec(3), g_l3start(), *[g_att3(c) for c in range(NC)]),
        lane(*[g_tile(i) for i in range(0, NT, 2)]),
        lane(*[g_tile(i) for i in range(1, NT, 2)]),
        lane(*[x for c in range(NC) for x in (g_end2(c), g_ln(3, c, lt[1]), g_gates(3, c))]),
    ]
    rr = [0]

    def steps(n):
        did = 0
        tried = 0
        while did < n and tried < len(lanes) and lanes:
            l = lanes[rr[0] % len(lanes)]
            try:
                r = next(l)
            except StopIteration:
                lanes.remove(l)
                continue
            rr[0] += 1
            if r == "blocked":
                tried += 1
            else:
                did += 1
                tried = 0
        return did > 0 or not lanes

    def need(*keys):
        while any(k not in tk for k in keys):
            assert steps(1), keys

    seq = [(1, c, e8) for c in range(NC) for e8 in range(NE)] + [(3, c, e8) for c in range(NC) for e8 in range(NE)]
    tg_tok, tg_free, s_free, h_free, pend = {}, {}, {}, {}, []

    def gate_of(i):
        layer, c, e8 = seq[i]
        b = take()
        buf = tg_buf[i % 2]
        x_ = xnT[:, CW * c:CW * c + CW]
        src = (gTT1 if layer == 1 else gTT3)[0:24, CW * c:CW * c + CW]
        t = mm(ps[:, b, :], cb[0:24, 128 + 128 * e8:256 + 128 * e8], src, tk["g", layer, c], *free[b])
        if layer == 1:
            t = tt(dve, buf, x_, ps[:, b, :], ALU.mult, t, tk["xn", 1, c], tg_free.get(i % 2))
        else:
            t = acp(buf, ps[:, b, :], t, tg_free.get(i % 2))
        free[b] = [t]
        tg_tok[i] = t

    def block(i, f, n):
        layer, c, e8 = seq[i]
        buf, h, s1 = tg_buf[i % 2], h_buf[n % 4], s_buf[n % 2]
        w_ = W[e8]
        if layer == 1:
            m = (128, 128, 96)[f]
            ba, bb2 = (0, 1) if n % 2 == 0 else (2, 3)
            ta = mm(ps[0:m, ba, :], w_[:, 128 * f:128 * f + m], buf, tg_tok[i], t_w1b if e8 == 7 else t_w1a[-1],
                    *free[ba])
            tb = mm(ps[0:m, bb2, :], w_[:, 352 + 128 * f:352 + 128 * f + m], buf, *free[bb2])
            tg_free[i % 2] = tb
            t = af(s1[0:m, :], ps[0:m, ba, :], ACT.Silu, ta, s_free.get(n % 2))
            free[ba] = [t]
            t = tt(dve, h[0:m, :], s1[0:m, :], ps[0:m, bb2, :], ALU.mult, t, tb, h_free.get(n % 4))
            free[bb2] = [t]
            s_free[n % 2] = t
            wd = w_[0:m, 704 + 128 * f:832 + 128 * f]
            nf = 3
        else:
            m = 128
            bk = n % 4
            ta = mm(ps[:, bk, :], w_[:, 128 * f:128 * f + 128], xnT[:, CW * c:CW * c + CW], tk["w3", e8],
                    tk["xn", 3, c], *free[bk])
            k = 4 * e8 + f
            t = af(s1, ps[:, bk, :], ACT.Silu, ta, s_free.get(n % 2), bias=M("b1c")[:, k:k + 1])
            free[bk] = [t]
            t = tt(dve, h, s1, buf, ALU.mult, t, tg_tok[i], h_free.get(n % 4))
            s_free[n % 2] = tg_free[i % 2] = t
            wd = w_[:, 512 + 128 * f:640 + 128 * f]
            nf = 4
        first, last = (e8 == 0 and f == 0), (e8 == NE - 1 and f == nf - 1)

        def down():
            t3 = mm(ps[:, 4, :], wd, h[0:m, :], t, *(free[4] if first else []),
                    start=first, stop=last and layer == 1)
            h_free[n % 4] = t3
            if layer == 1 and c == NC - 1 and f == nf - 1:
                tk["w3", e8] = d_w3[e8](W[e8][:, 0:1024], A["L3_w"][:, 1024 * e8:1024 * e8 + 1024], t3)
            if last:
                if layer == 3:
                    for q in range(3):
                        t3 = mm(ps[:, 4, :], bp3[q], gTT3[0:24, CW * c:CW * c + CW], tk["b3"],
                                start=False, stop=(q == 2))
                t4 = af(gT[:, CW * c:CW * c + CW], ps[:, 4, :], ACT.Silu, t3)
                free[4] = [t4]
                tk["gT", layer, c] = t4
        pend.append(down)

    n = 0
    for i, (layer, c, e8) in enumerate(seq):
        if i not in tg_tok:
            need(("g", layer, c))
            if layer == 3:
                need("b3")
            gate_of(i)
        for f in range(3 if layer == 1 else 4):
            block(i, f, n)
            n += 1
            steps(SPH)
            if len(pend) > 2:
                pend.pop(0)()
            if f == 1 and i + 1 < len(seq) and ("g",) + seq[i + 1][:2] in tk:
                gate_of(i + 1)
    while pend:
        pend.pop(0)()
    while lanes:
        assert steps(1)
    finish(tk["out"])


def constants():
    f = np.zeros((128, CF_N), np.float64)

    def put(name, a):
        o, _ = CF_COLS[name]
        f[:a.shape[0], o:o + a.shape[1]] = a

    put("ident", np.eye(128))
    n = np.arange(128)[:, None]
    k = np.arange(64)[None, :]
    w = 2 * np.pi * n * k / 128
    F = np.concatenate([np.cos(w), -np.sin(w)], 1)
    F[:, 64] = (-1.0) ** np.arange(128)
    J = np.zeros((128, 128))
    for i in range(1, 64):
        J[i, 64 + i] = 1
        J[64 + i, i] = -1
    Fi = np.concatenate([2 * np.cos(w), -2 * np.sin(w)], 1) / 128
    Fi[:, 0] = 1 / 128
    Fi[:, 64] = (-1.0) ** np.arange(128) / 128
    put("ft", F)
    put("jft", F @ J.T)
    put("fi", Fi)
    put("fij", -(Fi @ J))
    j = np.arange(1, 65)[:, None]
    s = -2 * np.sin(2 * np.pi * j * k / 128)
    s[63] = 0
    S = np.concatenate([s, s], 1)
    put("sm", S)
    pos = np.arange(1024, dtype=np.float32)[:, None]
    div = np.exp(np.arange(0, 32, 2, dtype=np.float32) * np.float32(-np.log(10000.0) / 32)).astype(np.float32)
    ang = (pos * div).astype(np.float32)
    pe = np.zeros((1024, 32), np.float32)
    pe[:, 0::2] = np.sin(ang)
    pe[:, 1::2] = np.cos(ang)
    put("pe", pe.T)
    i = np.arange(1024)[None, :] - np.arange(128)[:, None]
    put("dt", np.where(i >= 0, 0.96875 ** np.maximum(i, 0).astype(np.float64), 0.0))
    put("w8", np.tile(8.0 - np.arange(8), (128, 1)))
    one = 0x3F80
    b = np.zeros((128, CB_N), np.uint16)
    b[:, 0:128] = one * np.eye(128, dtype=np.uint16)
    for e in range(NE):
        for r in range(3):
            b[8 * r + e, 128 + 128 * e:256 + 128 * e] = one
    return f.astype(np.float32), b


def layouts(a):
    def blocks(w, k):
        return np.ascontiguousarray(w.reshape(-1, k, w.shape[-1]).transpose(1, 0, 2).reshape(k, -1))

    d = {"x": a["L0_attn_representations"]}
    Wc = a["L0_attn_Wc"]
    d["L0_WcT"] = Wc.T
    d["L0_WoT"] = blocks(a["L0_attn_Wo"].T, 128)
    d["L0_bqk"] = a["L0_attn_bc"][:256].reshape(2, 128).T
    d["L0_bv"] = a["L0_attn_bc"][256:]
    d["L0_bo"] = a["L0_attn_bo"][:, None]
    d["L0_Wg"] = a["L0_ffn_Wg"].T
    d["L0_w1"] = a["L0_ffn_W1"].reshape(2048, 128).T
    d["L0_w2"] = a["L0_ffn_W2"].reshape(2048, 128).T
    d["L0_w3"] = blocks(a["L0_ffn_W3"].transpose(0, 2, 1).reshape(2048, 128), 128)
    w2 = np.zeros((8, 384, 128), np.float32)
    w2[:, :352] = a["L1_ffn_w2"]
    d["L1_w"] = np.concatenate([np.concatenate([a["L1_ffn_w1"][e], a["L1_ffn_w3"][e], blocks(w2[e], 128)], 1)
                                for e in range(8)], 1)
    d["L3_w"] = np.concatenate([np.concatenate([a["L3_ffn_W1"][e], blocks(a["L3_ffn_W2"][e], 128)], 1)
                                for e in range(8)], 1)
    d["L2_W"] = a["L2_ffn_W"].transpose(2, 0, 1).reshape(128, -1)
    w = a["L2_attn_Wqkv"].reshape(16, 3, 8, 128).transpose(1, 0, 2, 3).reshape(384, 128)
    parts = {"wqkvp": np.concatenate([w.T, a["L2_attn_Wproj"].T], 1), "wq": a["L3_attn_weight_q"],
             "wk": a["L3_attn_weight_k"], "wv": a["L3_attn_weight_v"], "bw": a["L1_attn_B_w"],
             "cw": a["L1_attn_C_w"].T, "wg1": a["L1_ffn_gate_w"].T, "wg3": a["L3_ffn_Wg"],
             "b1c": a["L3_ffn_b1"].reshape(32, 128).T, "th": a["L3_attn_theta"][:, None],
             "asc": a["L1_attn_a_params"][:, None], "dcol": a["L1_attn_D"][:, None],
             "bp": a["L2_attn_bproj"][:, None], "eb": np.tile(a["L1_ffn_expert_bias"], (128, 1)),
             "bg": np.tile(a["L3_ffn_bg"], (128, 1)), "sig": a["L2_ffn_tile_sigs"].T,
             "b2": np.tile(a["L2_ffn_b"], (3, 1)), "b3": np.tile(a["L3_ffn_b2"], (3, 1))}
    misc = np.zeros((128, MISC_N), np.float32)
    for k, v in parts.items():
        misc[:v.shape[0], MISC_COLS[k][0]:MISC_COLS[k][0] + v.shape[1]] = v
    d["misc"] = misc
    return {k: np.ascontiguousarray(v) for k, v in d.items()}


def kernel(**inputs):
    import concourse.bacc as bacc
    from concourse.bass_utils import run_bass_kernel_spmd

    a = layouts({k: np.asarray(v) for k, v in inputs.items()})
    a["cf"], a["cb"] = constants()
    nc = bacc.Bacc("TRN2", target_bir_lowering=False, num_devices=1)
    arrays, aps = {}, {}
    for name, v in a.items():
        arrays["in_" + name] = v
        aps[name] = nc.dram_tensor("in_" + name, v.shape, mybir.dt.from_np(v.dtype), kind="ExternalInput").ap()
    out = nc.dram_tensor("out_0", (2, 1024, 128), F32, kind="ExternalOutput").ap()
    program(nc, aps, out)
    r = run_bass_kernel_spmd(nc, [arrays], core_ids=[0])
    return r.results[0]["out_0"]
```

```python
from contextlib import ExitStack

import numpy as np

import concourse.bass as bass
from concourse import mybir

ALU = mybir.AluOpType
ACT = mybir.ActivationFunctionType
AX = mybir.AxisListType
F32 = mybir.dt.float32
BF16 = mybir.dt.bfloat16

T = 2048
NT = T // 128
NC = 4
CW = 512
NE = 8
EPS = 1e-5
BIG = -3.0e38

CF_COLS = {}
_off = 0
for _name, _n in (("ident", 128), ("ft", 128), ("jft", 128), ("fi", 128), ("fij", 128), ("sm", 128),
                  ("w8", 8), ("pe", 1024), ("dt", 1024)):
    CF_COLS[_name] = (_off, _n)
    _off += _n
CF_N = _off
CF_KEPT = CF_COLS["pe"][0]
CB_N = 128 + NE * 128

MISC_COLS = {}
_off = 0
for _name, _n in (("wqkvp", 512), ("wq", 128), ("wk", 128), ("wv", 128), ("bw", 128), ("cw", 128), ("wg1", 8),
                  ("wg3", 8), ("b1c", 32), ("th", 1), ("asc", 1), ("dcol", 1), ("bp", 1), ("eb", 8), ("bg", 8),
                  ("sig", 8), ("b2", 128), ("b3", 128)):
    MISC_COLS[_name] = (_off, _n)
    _off += _n
MISC_N = _off
HD = 4
PAUSE = 2
B0, B1, B3 = 2.3, 2.0, 1.2


class Stream:

    def __init__(self, queues, key, sem):
        self.q, self.key, self.sem_of, self.n = queues[key], key, sem, 0
        self.sem = sem()

    def _put(self, f, after, inc):
        for t in after:
            if t is not None:
                self.q.append(("wait", t[0], t[1]))
        self.q.append(("do", f, inc))

    def __call__(self, f, *after):
        if self.n == 2000:
            self.sem, self.n = self.sem_of(), 0
        self.n += 1
        self._put(f, after, (self.sem, 1))
        return (self.sem, self.n)

    def quiet(self, f, *after):
        self._put(f, after, None)

    def last(self):
        return (self.sem, self.n) if self.n else None


class Dma:

    def __init__(self, queues, sem, key="sync"):
        self.q, self.sem, self.n = queues[key], sem, 0

    def __call__(self, out, in_, *after):
        for t in after:
            if t is not None:
                self.q.append(("wait", t[0], t[1]))
        self.n += 16
        self.q.append(("do", lambda e: e.dma_start(out, in_), (self.sem, 16)))
        return (self.sem, self.n)


def emit(eng, queue):
    seen = {}
    for item in queue:
        if item[0] == "wait":
            _, sem, value = item
            if seen.get(id(sem), 0) < value:
                eng.wait_ge(sem, value)
                seen[id(sem)] = value
        else:
            _, f, inc = item
            ins = f(eng)
            if inc is not None:
                ins.then_inc(*inc)


def program(nc, A, out):
    ctx = ExitStack()
    with ctx:
        _program(nc, A, out, ctx)


def _program(nc, A, out, ctx):
    queues = {k: [] for k in ("sync", "tensor", "vector", "scalar", "gpsimd")}

    def sem(name):
        return ctx.enter_context(nc.semaphore(name))

    def sb(name, shape, dt=F32):
        return ctx.enter_context(nc.sbuf_tensor(name, shape, dt))

    names = iter(range(1000))
    pe, dve, act, pool = (Stream(queues, k, lambda k=k: sem(f"{k}_{next(names)}"))
                          for k in ("tensor", "vector", "scalar", "gpsimd"))

    def ends():
        return [s.last() for s in (pe, dve, act, pool)]

    def finish(t_out):
        queues["sync"].append(("wait", *t_out))
        with nc.Block() as block:
            @block.sync
            def _(e):
                emit(e, queues["sync"])

            @block.tensor
            def _(e):
                emit(e, queues["tensor"])

            @block.vector
            def _(e):
                emit(e, queues["vector"])

            @block.scalar
            def _(e):
                emit(e, queues["scalar"])

            @block.gpsimd
            def _(e):
                emit(e, queues["gpsimd"])

    ps = ctx.enter_context(nc.psum_tensor("ps", [128, 8, CW], F32))
    cf = sb("cf", [128, CF_KEPT])
    cb = sb("cb", [128, CB_N], BF16)
    xs = sb("xs", [128, NT, 128])
    xnT = sb("xnT", [128, T])
    gT = sb("gT", [128, T])
    small = sb("small", [128, 1536])
    AR = 30720
    ar = sb("ar", [128, AR])

    def C(name):
        o, n = CF_COLS[name]
        return cf[:, o:o + n]

    ident = C("ident")
    identb = cb[:, 0:128]

    def area(off, n):
        assert off + n <= AR, (off, n)
        return ar[:, off:off + n]

    tk = {}
    free = {b: [] for b in range(8)}
    tb = [5, 6, 7]

    def take():
        tb.append(tb.pop(0))
        return tb[-1]

    def mm(o_, l, r, *w, start=True, stop=True):
        return pe(lambda e: e.matmul(o_, l, r, start=start, stop=stop), *w)

    def tr(o_, i_, idn, *w):
        return pe(lambda e: e.transpose(o_, i_, idn), *w)

    load_ = [0.0]

    def cost(eng, ap):
        if eng is dve:
            n_ = 1
            for x in ap.shape[1:]:
                n_ *= x
            load_[0] += 0.15 + n_ / 960.0

    def tt(eng, o_, a, b, op, *w):
        cost(eng, o_)
        return eng(lambda e: e.tensor_tensor(o_, a, b, op), *w)

    def ts(o_, a, s0, s1, op0, op1, *w):
        cost(dve, o_)
        if op1 is None:
            return dve(lambda e: e.tensor_scalar(o_, a, s0, None, op0), *w)
        return dve(lambda e: e.tensor_scalar(o_, a, s0, s1, op0, op1), *w)

    def stt(o_, a, s, b, op0, op1, *w):
        cost(dve, o_)
        return dve(lambda e: e.scalar_tensor_tensor(out=o_, in0=a, scalar=s, in1=b, op0=op0, op1=op1), *w)

    def red(o_, a, op, *w, negate=False):
        cost(dve, a)
        if negate:
            return dve(lambda e: e.tensor_reduce(o_, a, AX.X, op, negate=True), *w)
        return dve(lambda e: e.tensor_reduce(o_, a, AX.X, op), *w)

    def cp(eng, o_, a, *w):
        cost(eng, o_)
        return eng(lambda e: e.tensor_copy(o_, a), *w)

    def acp(o_, a, *w):
        return act(lambda e: e.copy(o_, a), *w)

    def af(o_, a, fn, *w, **kw):
        return act(lambda e: e.activation(o_, a, fn, **kw), *w)

    def v3(ap, k):
        return ap.rearrange("p (t k) -> p t k", k=k)

    def bc8(ap):
        return ap.unsqueeze(2).to_broadcast([128, ap.shape[1], 8])

    SM = [0]

    def sm(n):
        o = SM[0]
        SM[0] += n
        assert SM[0] <= 1536
        return small[:, o:o + n]

    mu, var, rstd = sm(16), sm(16), sm(16)
    gs, g1, g3, oh1, oh2, gate = (sm(128) for _ in range(6))
    r1, r2, r3, mn_, mt_ = sm(16), sm(16), sm(16), sm(32), sm(32)
    scn = sm(16)
    nm = sm(128)
    gsp = sm(192).bitcast(BF16)
    nsp = sm(96).bitcast(BF16)
    b8 = sm(32)

    NP = 5
    K2, K4, K8, LAG = 3, 5, 8, 2
    QOFF = 16384
    KOFF = QOFF + 3 * 2048
    POFF = KOFF + 3 * 1024
    assert POFF + NP * 1024 <= AR
    V0 = area(0, 16384)
    Qs = area(QOFF, 3 * 2048).bitcast(BF16).rearrange("p (s h t) -> p s h t", s=3, h=4)
    Ks = area(KOFF, 3 * 1024).bitcast(BF16).rearrange("p (s h t) -> p s h t", s=3, h=2)
    Ps = area(POFF, NP * 1024).rearrange("p (s t) -> p s t", s=NP)
    acc_sb = sb("acc_sb", [128, T])
    psum_sb = sb("psum_sb", [128, 2048])
    on_sb = sb("on_sb", [128, 1024])
    osb_ = sb("osb", [128, 1024])
    rec_sb = sb("rec_sb", [128, 1024])
    ps2_sb = sb("ps2_sb", [128, 1024])
    lrow = sb("lrow", [128, 512])
    lcol = sb("lcol", [128, 16])
    mT = sb("mT", [16, 2 * 1024], BF16)
    wA = sb("wA", [128, 1280 + 1024])
    onesf = sb("onesf", [128, 64])
    bias_qk = sb("bias_qk", [128, 2])
    bo = sb("bo", [128, 1])
    zero_b = sb("zero_b", [128, CW // 2], BF16)[:, :]
    bv = psum_sb[:, 0:1024]

    w0 = (area(QOFF + 2048, 2048), area(QOFF + 4096, 2048), area(KOFF + 1024, 2048))
    lt0 = area(15872, 512)
    parts = area(POFF, 4096)
    gTT0 = acc_sb[:, 0:1024].bitcast(BF16)
    s0b = [acc_sb[:, 1024:1536], acc_sb[:, 1536:2048]]
    u0b = [osb_[:, 0:512], osb_[:, 512:1024]]
    h0b = [rec_sb[:, 0:512], rec_sb[:, 512:1024], ps2_sb[:, 0:512], ps2_sb[:, 512:1024]]
    tg0 = [psum_sb[:, 1024:1536], psum_sb[:, 1536:2048]]

    d_c = Dma(queues, sem("d_const"))
    d_x = [Dma(queues, sem(f"d_x{c}")) for c in range(NC)]
    xv = A["x"].rearrange("b (t p) d -> p (b t) d", p=128)
    d_wg, d_w0 = Dma(queues, sem("d_wg0")), [Dma(queues, sem(f"d_w0_{i}")) for i in range(4)]
    d_wa, d_wb = Dma(queues, sem("d_wa0")), Dma(queues, sem("d_wb0"))
    wg0 = sm(8)
    t_w0 = []

    def load_x(c):
        tk["x", 0, c] = d_x[c](xs[:, 4 * c:4 * c + 4, :], xv[:, 4 * c:4 * c + 4, :])

    def load_w0(k):
        cols = slice(512 * k, 512 * k + 512)
        for i_, k_ in enumerate(("w1", "w2", "w3")):
            t = d_w0[k](w0[i_][:, cols], A["L0_" + k_][:, cols])
        t_w0.append(t)

    load_x(0)
    d_c(cf[:, :], A["cf"][:, 0:CF_KEPT])
    t_c = d_c(cb[:, :], A["cb"].bitcast(BF16))
    t_wg = d_wg(wg0, A["L0_Wg"])
    free[4], free[5], free[6], free[7] = [t_c], [t_c], [t_c], [t_c]
    load_w0(0)
    load_x(1)
    d_wa(bias_qk[:, :], A["L0_bqk"])
    d_wa(bv, A["L0_bv"].partition_broadcast(128))
    t_wa0 = d_wa(wA[:, 0:1280], A["L0_WcT"])
    load_w0(1)
    load_x(2)
    load_w0(2)
    load_x(3)
    load_w0(3)
    d_wb(bo[:, :], A["L0_bo"])
    t_wb = d_wb(wA[:, 1280:2304], A["L0_WoT"])
    t_zero = pool(lambda e: e.memset(zero_b, 0.0))
    pool(lambda e: e.memset(onesf[:, :], 1.0))

    def clear(s, *after):
        return [dve(lambda e: e.memset(Qs[:, s, :, :], 0.0), *after),
                pool(lambda e: e.memset(Ks[:, s, :, :], 1.0), *after)]

    t_clear = [clear(0), None, None]

    def until(*keys):
        while any(k not in tk for k in keys):
            yield "blocked"

    def g_ln(layer, c, buf):
        yield from until(("x", layer, c))
        x4 = xs[:, 4 * c:4 * c + 4, :]
        sl = slice(4 * c, 4 * c + 4)
        m4, v4, s4 = mu[:, sl], var[:, sl], rstd[:, sl]
        dst = xnT[:, CW * c:CW * c + CW]
        xc, sq = v3(buf, 128), v3(dst, 128)
        t = red(m4, x4, ALU.add, tk["x", layer, c])
        t = ts(m4, m4, -1.0 / 128, None, ALU.mult, None, t)
        t = tt(dve, xc, x4, m4.unsqueeze(2).to_broadcast([128, 4, 128]), ALU.add, t)
        yield
        t = af(sq, xc, ACT.Square, t)
        yield
        t = red(v4, sq, ALU.add, t)
        t = ts(v4, v4, 1.0 / 128, EPS, ALU.mult, ALU.add, t)
        yield
        t = af(s4, v4, ACT.Sqrt, t)
        yield
        t = dve(lambda e: e.reciprocal(s4, s4), t)
        t = tt(dve, xc, xc, s4.unsqueeze(2).to_broadcast([128, 4, 128]), ALU.mult, t)
        yield
        b = take()
        for j in range(4):
            t1 = tr(ps[:, b, 128 * j:128 * j + 128], xc[:, j, :], ident, t, *free[b])
        t = acp(dst, ps[:, b, :], t1)
        free[b] = [t]
        tk["xn", layer, c] = t
        yield

    def first_of(s, oh, m, g, q, t):
        n = s.shape[1]
        t = red(m, s, ALU.max, t)
        t = tt(dve, g, s, bc8(m), ALU.is_equal, t)
        t = tt(dve, g, g, C("w8").unsqueeze(1).to_broadcast([128, n, 8]), ALU.mult, t)
        t = red(q, g, ALU.max, t)
        return tt(dve, oh, g, bc8(q), ALU.is_equal, t)

    def g_split_T(src, n, gT_, c0, key, t):
        tmp = v3(g3, 8)[:, c0 // 128:c0 // 128 + n, :]
        g24 = v3(gsp, 24)[:, c0 // 128:c0 // 128 + n, :]
        t = cp(dve, g24[:, :, 0:8], src, t)
        t = tt(dve, tmp, src, g24[:, :, 0:8], ALU.subtract, t)
        t = cp(dve, g24[:, :, 8:16], tmp, t)
        t = tt(dve, tmp, tmp, g24[:, :, 8:16], ALU.subtract, t)
        t = cp(dve, g24[:, :, 16:24], tmp, t)
        yield
        b = take()
        pb = ps[:, b, :].bitcast(BF16)
        for j in range(n):
            tp = tr(pb[0:24, 128 * j:128 * j + 128], g24[:, j, :], identb, t, *free[b])
        t = cp(dve, gT_[0:24, c0:c0 + 128 * n], pb[0:24, 0:128 * n], tp)
        free[b] = [t]
        tk[key] = t
        yield

    def g_gates(layer, c):
        yield from until(("xn", layer, c))
        sl, wd = slice(32 * c, 32 * c + 32), slice(4 * c, 4 * c + 4)
        w_ = M("wg1" if layer == 1 else "wg3")
        s, a, g, o1, o2, gt = (v3(x[:, sl], 8) for x in (gs, g1, g3, oh1, oh2, gate))
        m, q = r1[:, wd], r2[:, wd]
        b = take()
        for j in range(4):
            i0 = CW * c + 128 * j
            tp = mm(ps[:, b, 8 * j:8 * j + 8], xnT[:, i0:i0 + 128], w_, tk["xn", layer, c], t_ml, *free[b])
        pv_ = v3(ps[:, b, 0:32], 8)
        if layer == 1:
            t = cp(dve, s, pv_, tp)
        else:
            t = tt(dve, s, pv_, M("bg").unsqueeze(1).to_broadcast([128, 4, 8]), ALU.add, tp)
        free[b] = [t]
        t = red(m, s, ALU.max, t, negate=True)
        t = tt(dve, s, s, bc8(m), ALU.add, t)
        yield
        t = af(s, s, ACT.Exp, t)
        yield
        t = red(m, s, ALU.add, t)
        t = dve(lambda e: e.reciprocal(m, m), t)
        t = tt(dve, s, s, bc8(m), ALU.mult, t)
        yield
        if layer == 1:
            t = tt(dve, a, s, M("eb").unsqueeze(1).to_broadcast([128, 4, 8]), ALU.add, t)
            t = first_of(a, o1, m, g, q, t)
            t = stt(a, o1, BIG, a, ALU.mult, ALU.add, t)
            yield
            t = first_of(a, o2, m, g, q, t)
            t = tt(dve, o1, o1, o2, ALU.add, t)
        else:
            t = first_of(s, o1, m, g, q, t)
        t = tt(dve, gt, o1, s, ALU.mult, t)
        yield
        yield from g_split_T(gt, 4, gTT1 if layer == 1 else gTT3, CW * c, ("g", layer, c), t)

    def g_bias(name, dst, key):
        yield from until("late")
        b_ = M(name)[0:24, :]
        tmp = wA[0:24, MISC_N:MISC_N + 128]
        t = cp(dve, dst[0], b_, tk["late"])
        t = tt(dve, tmp, b_, dst[0], ALU.subtract, t)
        t = cp(dve, dst[1], tmp, t)
        t = tt(dve, tmp, tmp, dst[1], ALU.subtract, t)
        tk[key] = cp(dve, dst[2], tmp, t)
        yield

    def g_combine(layer, c, a, t):
        b = take()
        for j in range(4):
            tp = tr(ps[:, b, 128 * j:128 * j + 128], a[:, 128 * j:128 * j + 128], ident, t, *free[b])
        x4 = xs[:, 4 * c:4 * c + 4, :]
        t = tt(dve, x4, x4, v3(ps[:, b, :], 128), ALU.add, tp)
        free[b] = [t]
        tk["tr", layer, c] = tp
        tk["x", layer + 1, c] = t
        yield

    def lane(*gens):
        for g_ in gens:
            yield from g_

    lanes = []
    hook, credit, rr = [0], [0.0], [0]
    again = {}

    def steps(budget):
        hook[0] += 1
        credit[0] = min(credit[0] + budget, 2.0 * budget)
        rr[0] += 1
        did = False
        order = lanes[rr[0] % len(lanes):] + lanes[:rr[0] % len(lanes)] if lanes else []
        for l in order:
            if credit[0] <= 0:
                break
            if again.get(id(l), 0) > hook[0]:
                did = True
                continue
            before = load_[0]
            try:
                r = next(l)
            except StopIteration:
                lanes.remove(l)
                did = True
                continue
            credit[0] -= load_[0] - before
            if r != "blocked":
                did = True
                if r:
                    again[id(l)] = hook[0] + r
        return did or not lanes or credit[0] <= 0

    def need(*keys):
        while any(k not in tk for k in keys):
            assert steps(4.0), keys

    scr = nc.dram_tensor("scr", [2, 7, 128, T], BF16).ap()
    lscr = nc.dram_tensor("lscr", [2, 2, 512], F32).ap()
    d_ld = [Dma(queues, sem(f"d_ld{i}")) for i in range(3)]
    d_mr, d_mr2 = Dma(queues, sem("d_mr")), Dma(queues, sem("d_mr2"), "scalar")
    d_lc = [Dma(queues, sem(f"d_lc{i}"), "sync" if i else "scalar") for i in range(4)]
    dd = [Dma(queues, sem(f"d_scr{i}")) for i in range(4)]
    QORD = (0, 0, 0, 1, 1, 2)
    KORD = (0, 1, 2, 0, 1, 0)
    NQ = 8
    ULAST = 28
    LK, LQ = (5,), (1, 4, 6)

    def g_gates0(c):
        yield from until(("xn", 0, c))
        sl, wd = slice(32 * c, 32 * c + 32), slice(4 * c, 4 * c + 4)
        s, a, g, o1, o2, gt = (v3(x[:, sl], 8) for x in (gs, g1, g3, oh1, oh2, gate))
        m1, m2, q = r1[:, wd], r2[:, wd], r3[:, wd]
        b = take()
        for j in range(4):
            i0 = CW * c + 128 * j
            tp = mm(ps[:, b, 8 * j:8 * j + 8], xnT[:, i0:i0 + 128], wg0, tk["xn", 0, c], t_wg, *free[b])
        t = cp(dve, s, v3(ps[:, b, 0:32], 8), tp, t_c)
        free[b] = [t]
        t = first_of(s, o1, m1, g, q, t)
        t = stt(a, o1, BIG, s, ALU.mult, ALU.add, t)
        yield
        t = first_of(a, o2, m2, g, q, t)
        t = tt(dve, q, m2, m1, ALU.subtract, t)
        t = af(q, q, ACT.Exp, t)
        yield
        t1 = ts(m1, q, 1.0, None, ALU.add, None, t)
        t1 = dve(lambda e: e.reciprocal(m1, m1), t1)
        t = tt(dve, m2, q, m1, ALU.mult, t1)
        t1 = tt(dve, o1, o1, bc8(m1), ALU.mult, t1)
        t = tt(dve, o2, o2, bc8(m2), ALU.mult, t)
        t = tt(dve, gt, o1, o2, ALU.add, t)
        yield
        yield from g_split_T(gt, 4, gTT0, CW * c, ("g", 0, c), t)

    def g_qk(c, ty):
        yield from until(("xn", 0, c))
        k = (2 * c + ty) % 4
        d, o_ = dd[k], 1024 + 768 * k
        f0, f1 = parts[:, 0:512], parts[:, 512:1024]
        pt = [parts[:, o_ + 256 * i:o_ + 256 * i + 256].bitcast(BF16) for i in range(3)]
        b = take()
        t = mm(ps[:, b, :], wA[:, 128 * ty:128 * ty + 128], xnT[:, CW * c:CW * c + CW], tk["xn", 0, c], t_wa0,
               *free[b])
        t = ts(f1, ps[:, b, :], bias_qk[:, ty:ty + 1], None, ALU.add, None, t, tk.get("parts"))
        free[b] = [t]
        t = stt(f0, f1, 0.01, f1, ALU.mult, ALU.max, t)
        t = acp(pt[0], f0, t, tk.get(("qk", k)))
        yield
        t = tt(dve, f1, f0, pt[0], ALU.subtract, t)
        t = acp(pt[1], f1, t)
        yield
        t = tt(dve, f1, f1, pt[1], ALU.subtract, t)
        t = tk["parts"] = acp(pt[2], f1, t)
        yield
        cols = slice(CW * c, CW * c + CW)
        for g, which in enumerate((QORD, KORD)[ty]):
            td = d(scr[ty, g, :, cols], pt[which], t)
        if ty == 0:
            for o_ in (CW * c, CW * c + CW // 2):
                td = d(scr[ty, 6, :, o_:o_ + CW // 2], zero_b, t_zero)
        tk["qk", k] = td
        tk["scr", ty, c] = td

    def g_v(i):
        yield from until(("xn", 0, max(i // 4, 3 if i == 15 else 0)))
        for hf in range(2):
            b = take()
            tmp = on_sb[:, 512 * hf:512 * hf + 512]
            t = mm(ps[:, b, :], xnT[:, 128 * i:128 * i + 128], wA[:, 256 + 512 * hf:768 + 512 * hf],
                   tk["xn", 0, i // 4], t_wa0, *free[b])
            t = tt(dve, tmp, ps[:, b, :], bv[:, 512 * hf:512 * hf + 512], ALU.add, t)
            free[b] = [t]
            tk["v"] = stt(V0[:, 1024 * i + 512 * hf:1024 * i + 512 * hf + 512], tmp, 0.01, tmp,
                          ALU.mult, ALU.max, t)
            yield

    slot_free = [[], [], []]
    ld_tok, mrow = {}, {}

    def load(g, heads=range(4)):
        b, q, s = g // 4, g % 4, g % 3
        d = d_ld[s]
        for h in heads:
            hh = 4 * q + h
            r0 = 64 * (h % 2)
            tok = d(Qs[r0:r0 + 56, s, h, :], scr[0, :, 8 * hh:8 * hh + 8, 1024 * b:1024 * b + 1024],
                    tk["scr", 0, 2 * b + 1], tk["scr", 1, 2 * b + 1], *slot_free[s], *t_clear[s])
            tok = d(Ks[r0:r0 + 48, s, h // 2, :], scr[1, 0:6, 8 * hh:8 * hh + 8, 1024 * b:1024 * b + 1024])
        ld_tok[g] = tok

    negm = [nm[:, 0:64], nm[:, 64:128]]
    negm_free = [None, None]
    mT_free = [None, None]

    def max_half(g, j, bank):
        s = g % 3
        h, qt, hf = j // 16, (j // 2) % 8, j % 2
        tp = mm(ps[:, bank, :], Qs[:, s, h, 128 * qt:128 * qt + 128], Ks[:, s, h // 2, 512 * hf:512 * hf + 512],
                ld_tok[g], *free[bank])
        t = red(negm[g % 2][:, j:j + 1], ps[:, bank, :], ALU.max, tp, negm_free[g % 2], negate=True)
        free[bank] = [t]
        return t

    def max_rows(g, t, bank):
        s, k = g % 3, g % 2
        t = red(mn_, negm[k].rearrange("p (a f) -> p a f", f=2), ALU.min, t)
        negm_free[k] = t
        sp = nsp[:, 96 * k:96 * k + 96].rearrange("p (q h r) -> p h q r", q=8, h=4)
        src = mn_.rearrange("p (h q) -> p h q", h=4)
        tmp = mt_.rearrange("p (h q) -> p h q", h=4)
        t = cp(dve, sp[:, :, :, 0], src, t)
        t = tt(dve, tmp, src, sp[:, :, :, 0], ALU.subtract, t)
        t = cp(dve, sp[:, :, :, 1], tmp, t)
        t = tt(dve, tmp, tmp, sp[:, :, :, 1], ALU.subtract, t)
        t = cp(dve, sp[:, :, :, 2], tmp, t)
        pb = ps[:, bank, :].bitcast(BF16)
        for qt in range(8):
            tp = tr(pb[0:12, 128 * qt:128 * qt + 128], nsp[:, 96 * k + 12 * qt:96 * k + 12 * qt + 12], identb,
                    t, *free[bank])
        t = cp(dve, mT[0:12, 1024 * k:1024 * k + 1024], pb[0:12, :], tp, *(mT_free[k] or []))
        free[bank] = [t]
        mrow[g] = []
        max_to_stack(g, (0, 1), d_mr, t)
        return t

    def max_to_stack(g, heads, d, t):
        s, k = g % 3, g % 2
        for h in heads:
            r0 = 64 * (h % 2) + 48
            tok = d(Qs[r0:r0 + 3, s, h, :], mT[3 * h:3 * h + 3, 1024 * k:1024 * k + 1024], t)
        mrow[g].append(tok)
        mT_free[k] = list(mrow[g])

    def g_max0():
        yield from until(("scr", 0, 1), ("scr", 1, 1))
        load(0)
        yield 5
        for j in range(0, 64, 2):
            max_half(0, j, take())
            t = max_half(0, j + 1, take())
            yield
        t = max_rows(0, t, take())
        yield
        max_to_stack(0, (2, 3), d_mr2, t)

    lanes[:] = [
        lane(*[x for c in range(NC) for x in (g_ln(0, c, lt0), g_gates0(c))]),
        lane(*[g_qk(c, ty) for c in range(NC) for ty in range(2)]),
        lane(*[g_v(i) for i in range(NT)]),
        lane(g_max0()),
    ]
    seq0 = [(c, e8) for c in range(NC) for e8 in range(NE)]
    tg_tok, tg_free, s_free, u_free, h_free, pend = {}, {}, {}, {}, {}, []

    def gate_of0(i):
        c, e8 = seq0[i]
        b = take()
        buf = tg0[i % 2]
        t = mm(ps[:, b, :], cb[0:24, 128 + 128 * e8:256 + 128 * e8], gTT0[0:24, CW * c:CW * c + CW],
               tk["g", 0, c], t_c, *free[b])
        t = acp(buf, ps[:, b, :], t, tg_free.get(i % 2))
        free[b] = [t]
        tg_tok[i] = t

    def block0(i, f, n):
        c, e8 = seq0[i]
        x_ = xnT[:, CW * c:CW * c + CW]
        ba, bb = (0, 1) if n % 2 == 0 else (2, 3)
        o1, k = 256 * e8 + 128 * f, 2 * e8 + f
        s1, u, h, buf = s0b[n % 2], u0b[n % 2], h0b[n % 4], tg0[i % 2]
        ta = mm(ps[:, ba, :], w0[0][:, o1:o1 + 128], x_, t_w0[e8 // 2], tk["xn", 0, c], *free[ba])
        tb_ = mm(ps[:, bb, :], w0[1][:, o1:o1 + 128], x_, *free[bb])
        t = af(s1, ps[:, ba, :], ACT.Silu, ta, s_free.get(n % 2))
        free[ba] = [t]
        t = tt(dve, u, s1, ps[:, bb, :], ALU.mult, t, tb_, u_free.get(n % 2))
        free[bb] = [t]
        s_free[n % 2] = t
        t = tt(pool, h, u, buf, ALU.mult, t, tg_tok[i], h_free.get(n % 4))
        u_free[n % 2] = tg_free[i % 2] = t
        first, last = k == 0, k == 2 * NE - 1

        def down():
            t3 = mm(ps[:, 4, :], w0[2][:, 128 * k:128 * k + 128], h, t, *(free[4] if first else []),
                    start=first, stop=last)
            h_free[n % 4] = t3
            if last:
                t4 = af(gT[:, CW * c:CW * c + CW], ps[:, 4, :], ACT.Silu, t3)
                free[4] = [t4]
                tk["gT", 0, c] = t4
        pend.append(down)

    n = 0
    for i, (c, e8) in enumerate(seq0):
        if i not in tg_tok:
            need(("g", 0, c))
            gate_of0(i)
        for f in range(2):
            block0(i, f, n)
            n += 1
            steps(B0)
            if len(pend) > 2:
                pend.pop(0)()
            if f == 0 and i + 1 < len(seq0) and ("g", 0, seq0[i + 1][0]) in tk:
                gate_of0(i + 1)
    while pend:
        pend.pop(0)()
    while lanes:
        assert steps(4.0)
    end0 = ends()

    scale = float(1.0 / np.sqrt(8.0))
    t_clear[1] = clear(1, *end0)
    t_clear[2] = clear(2)
    load(1)
    exp_tok, st_tok, pv_tok, add_tok = {}, {}, {}, {}
    tail = {}
    sched = [(g, hf, pr, kt) for g in range(NQ) for hf in range(2) for pr in range(2) for kt in range(8)]

    def pv(i):
        g, hf, pr, kt = sched[i]
        bank = 6 + (i // 8) % 2
        pbuf = Ps[:, i % NP, :]
        tile = 8 * (g // 4) + kt
        for a in range(2):
            h = 4 * (g % 4) + 2 * pr + a
            pv_tok[i] = mm(ps[64 * a:64 * a + 64, bank, :], V0[:, 1024 * tile + 64 * h:1024 * tile + 64 * h + 64],
                           pbuf[:, 512 * a:512 * a + 512], exp_tok[i], tk["v"], *(free[bank] if kt == 0 else []),
                           start=(kt == 0), stop=(kt == 7))

    def adds(i):
        u, k = i // 8, i % 8
        a_, b_ = psum_sb[:, 1024 * (u % 2):1024 * (u % 2) + 1024], ps2_sb[:, :]
        late = i >= 8 * ULAST
        np_ = 3 if late else 5
        if k == 1:
            add_tok[i] = add_tok[i - 1] = tt(pool, a_, Ps[:, (i - 1) % NP, :], Ps[:, i % NP, :], ALU.add,
                                             exp_tok[i], tail.get(("sum", u - 2)), *end0)
        elif 2 <= k <= np_:
            add_tok[i] = tt(pool, a_, a_, Ps[:, i % NP, :], ALU.add, exp_tok[i], add_tok[i - 1])
            if k == np_:
                tail["pool", u] = add_tok[i]
        if late and k == 5:
            add_tok[i] = add_tok[i - 1] = tt(dve, b_, Ps[:, (i - 1) % NP, :], Ps[:, i % NP, :], ALU.add,
                                             exp_tok[i], tail.get(("sum", u - 1)))
        elif late and k > 5:
            add_tok[i] = tail["dve", u] = tt(dve, b_, b_, Ps[:, i % NP, :], ALU.add, exp_tok[i], add_tok[i - 1])
        elif (k == 7 and not late) or (k == 0 and 0 < i <= 8 * ULAST):
            h = slice(0, 512) if k == 7 else slice(512, 1024)
            i1 = i if k == 7 else i - 1
            t = tt(dve, b_[:, h], Ps[:, (i1 - 1) % NP, h], Ps[:, i1 % NP, h], ALU.add, exp_tok[i1],
                   tail.get(("sum", i1 // 8 - 1)))
            if k == 0:
                add_tok[i1] = add_tok[i1 - 1] = tail["dve", i1 // 8] = t

    def unit_tail(u, k):
        if u < 0 or u >= 32:
            return
        g, hf, pr, _ = sched[8 * u]
        bank = 6 + u % 2
        c0 = 1024 * (g // 4) + 512 * hf
        m = u % 2
        on = on_sb[:, 512 * m:512 * m + 512]
        osb = osb_[:, 512 * m:512 * m + 512]
        rec = rec_sb[:, 512 * m:512 * m + 512]
        a_ = psum_sb[:, 1024 * m:1024 * m + 1024]
        if k == LAG:
            t = tail["osb", u] = acp(osb, ps[:, bank, :], pv_tok[8 * u + 7], tail.get(("on", u - 2)), *end0)
            free[bank] = [t]
        if k == K2:
            for q, src in enumerate((ps2_sb, a_)):
                for a in range(2):
                    r = 64 * q + 32 * a
                    t = mm(ps[r:r + 32, bank, :], onesf[:, 0:32], src[:, 512 * a:512 * a + 512],
                           tail["dve", u], tail["pool", u], *free[bank])
            tail["sum", u] = t
            t = acp(lrow[:, :], ps[:, bank, :], t, tail.get(("lc", u - 1)))
            free[bank] = [t]
            d_lc[0](lcol[:, 0:8], lrow[0:64:32, :], t, tail.get(("ld", u - 1)))
            tail["lc", u] = d_lc[0](lcol[:, 8:16], lrow[64:128:32, :])
        if k == K4:
            t = tt(dve, lcol[:, 0:8], lcol[:, 0:8], lcol[:, 8:16], ALU.add, tail["lc", u])
            t = dve(lambda e: e.reciprocal(lcol[:, 0:8], lcol[:, 0:8]), t)
            tail["ld", u] = d_lc[1](lscr[m], lcol[:, 0:8], t, tail.get(("rec", u - 2)))
            for a in range(2):
                tail["rec", u] = d_lc[2 + m](rec[64 * a:64 * a + 64, :], lscr[m, a].partition_broadcast(64),
                                             tail["ld", u], tail.get(("on", u - 2)))
        k8, pb = (12, 5) if u >= ULAST - 1 else (K8, bank)
        if k == k8:
            tail["on", u] = tt(dve, on, osb, rec, ALU.mult, tail["rec", u], tail["osb", u],
                               tail.get(("pr", u - 2)))
        if k == k8 + 1:
            pi = 2 * (g % 4) + pr
            t = tail["pr", u] = mm(ps[:, pb, :], wA[:, 1280 + 128 * pi:1408 + 128 * pi], on,
                                   tail["on", u], t_wb, *free[pb])
            dst = acc_sb[:, c0:c0 + CW]
            if pi == 0:
                t = cp(dve, dst, ps[:, pb, :], t)
            else:
                t = tt(dve, dst, dst, ps[:, pb, :], ALU.add, t, tail["acc", c0])
            tail["acc", c0] = t
            free[pb] = [t]
            if pi == 7:
                tk["acc", c0 // CW] = t

    def g_end0(c):
        yield from until(("acc", c))
        a, r = acc_sb[:, CW * c:CW * c + CW], slice(CW * c, CW * c + CW)
        t = ts(a, a, bo[:, 0:1], None, ALU.add, None, tk["acc", c])
        t = stt(a, a, 0.01, a, ALU.mult, ALU.max, t)
        yield
        t = tt(dve, a, a, xnT[:, r], ALU.add, t)
        t = tt(dve, a, a, gT[:, r], ALU.mult, t, tk["gT", 0, c])
        yield
        yield from g_combine(0, c, a, t)

    W = [area(1088 * e8, 1088) for e8 in range(NE)]
    R = 8704
    FB = 16304
    s_buf = [area(FB + 512 * i, 512) for i in range(2)]
    h_buf = [area(FB + 1024 + 512 * i, 512) for i in range(4)]
    tg_buf = [area(FB + 3072 + 512 * i, 512) for i in range(2)]
    pr1 = [area(20400 + 2048 * k, 2048) for k in range(2)]
    pr2 = [area(24496 + 2048 * k, 2048) for k in range(2)]
    pe_sb = pr1[0][0:32, 0:1024]
    lt1 = [acc_sb[:, CW * c:CW * c + CW] for c in range(NC)]
    qkv = [area(28592 + 384 * k, 384) for k in range(2)]
    sc2 = [area(29360 + 256 * k, 256) for k in range(2)]
    st2 = [area(29872 + 64 * k, 64) for k in range(2)]
    gTT1 = acc_sb[:, 0:1024].bitcast(BF16)
    gTT3 = psum_sb[:, 1024:2048].bitcast(BF16)
    gTT2 = osb_[:, 0:512].bitcast(BF16)
    ot2 = [osb_[:, 512 + 128 * k:640 + 128 * k] for k in range(2)]
    w2l = on_sb[:, :]
    lt = [rec_sb[:, 0:512], rec_sb[:, 512:1024]]
    oT2 = [ps2_sb[:, 0:512], ps2_sb[:, 512:1024]]

    def M(name):
        o_, n_ = MISC_COLS[name]
        return wA[:, o_:o_ + n_]

    MISC_E = MISC_COLS["b2"][0]
    d_ml = Dma(queues, sem("d_ml"))
    t_ml = d_ml(wA[:, 0:MISC_E], A["misc"][:, 0:MISC_E], *end0)
    d_w1a, t_w1a = Dma(queues, sem("d_w1a")), []
    d_w1b, d_w2 = Dma(queues, sem("d_w1b")), Dma(queues, sem("d_w2"))
    d_w3 = [Dma(queues, sem(f"d_w3_{e8}")) for e8 in range(NE)]

    load(2)
    MS = 27
    QUOTA = (2, 2, 2, 3, 3, 3, 3, 1)
    LOADS = (0, 1, 8, 9)
    for i, (g, hf, pr, kt) in enumerate(sched):
        s = g % 3
        loc = i % 32
        if loc in LOADS and 0 < g < NQ - 2:
            load(g + 2, [LOADS.index(loc)])
        if loc == 8 and g == NQ - 3:
            for e8 in range(NE - 1):
                t_w1a.append(d_w1a(W[e8], A["L1_w"][:, 1088 * e8:1088 * e8 + 1088], pv_tok[127]))
        if i == 144:
            tb[:] = [4]
            lanes[:] = [lane(*[x for c in range(2) for x in (g_end0(c), g_ln(1, c, lt1[c]), g_gates(1, c))])]
        b0 = 2 * (i % 2)
        for a in range(2):
            st_tok[i] = mm(ps[:, b0 + a, :], Ks[:, s, pr, 128 * kt:128 * kt + 128],
                           Qs[:, s, 2 * pr + a, 512 * hf:512 * hf + 512], *mrow[g], *free[b0], *free[b0 + 1],
                           *(end0 if i == 0 else []))
        ex_ = af(Ps[:, i % NP, :], ps[:, b0:b0 + 2, :].rearrange("p a t -> p (a t)"), ACT.Exp, st_tok[i],
                 pv_tok.get(i - NP), add_tok.get(i - NP), *[tk["qk", x] for x in range(4)], scale=scale)
        exp_tok[i] = ex_
        free[b0] = free[b0 + 1] = [ex_]
        lo = 5 if g == 0 else 0
        if loc == 0:
            nj = 0
        want = QUOTA[i % 8] if loc >= lo else 0
        if g == 0 and loc >= lo:
            want = max(want, 3)
        if loc == MS - 1:
            want = 64
        js = list(range(nj, min(64, nj + want))) if g + 1 < NQ and loc < MS else []
        nj += len(js)
        for j in js[:1]:
            tmx = max_half(g + 1, j, 4 + j % 2)
        unit_tail(i // 8 - 1, i % 8)
        unit_tail(i // 8 - 2, i % 8 + 8)
        if i >= LAG:
            pv(i - LAG)
        for j in js[1:]:
            tmx = max_half(g + 1, j, 4 + j % 2)
        adds(i)
        if g + 1 < NQ and loc == MS:
            tmx = max_rows(g + 1, tmx, 4)
        if g + 1 < NQ and loc == MS + 1:
            max_to_stack(g + 1, (2, 3), d_mr2, tmx)
        if i >= 144 and i % 8 in (LQ if g == NQ - 1 else LK):
            steps(2.0)
        if loc == 31:
            slot_free[s] = [st_tok[i]]
    for x in range(LAG - 1, -1, -1):
        pv(255 - x)
    tk["w1b"] = d_w1b(W[7], A["L1_w"][:, 7 * 1088:8 * 1088], pv_tok[255])

    def g_tail0():
        for x in range(256 + K2 + 1, 256 + 16):
            unit_tail(x // 8 - 1, x % 8)
            unit_tail(x // 8 - 2, x % 8 + 8)
            if x in (256 + K4, 256 + 12, 256 + 13):
                yield
        tb[:] = [6, 7]
        w_ = ends()
        d_w2(pe_sb, A["cf"][0:32, CF_KEPT:CF_KEPT + 1024], *w_)
        d_w2(wA[:, MISC_E:MISC_N], A["misc"][:, MISC_E:MISC_N])
        tk["late"] = d_w2(w2l, A["L2_W"])

    for x in range(256, 256 + K2 + 1):
        unit_tail(x // 8 - 1, x % 8)
        unit_tail(x // 8 - 2, x % 8 + 8)
    tb[:] = [6, 5]

    bp2 = [wA[0:24, MISC_N + 128 + 64 * i:MISC_N + 192 + 64 * i].bitcast(BF16) for i in range(3)]
    bp3 = [wA[0:24, MISC_N + 320 + 64 * i:MISC_N + 384 + 64 * i].bitcast(BF16) for i in range(3)]

    def g_position():
        yield from until(("g", 1, 0), ("g", 1, 1), "late")
        sg = M("sig")[0:32, :]
        t = ts(b8[0:32, 0:8], sg, 0.0, None, ALU.is_gt, None, t_ml)
        t = ts(b8[0:32, 8:16], sg, 0.0, None, ALU.is_lt, None, t)
        t = tt(dve, b8[0:32, 0:8], b8[0:32, 0:8], b8[0:32, 8:16], ALU.subtract, t)
        yield
        b = take()
        for j in range(8):
            tp = mm(ps[:, b, 8 * j:8 * j + 8], pe_sb[:, 128 * j:128 * j + 128], b8[0:32, 0:8], t, tk["late"], *free[b])
        s, g, q = v3(gs[:, 0:64], 8), v3(oh2[:, 0:64], 8), v3(oh1[:, 0:64], 8)
        t = cp(dve, s, v3(ps[:, b, 0:64], 8), tp)
        free[b] = [t]
        tk["pe_read"] = tp
        t = first_of(s, q, r1[:, 0:8], g, r2[:, 0:8], t)
        yield
        yield from g_split_T(q, 8, gTT2, 0, "pos", t)

    wt, wjt, gt_, gjt = (area(R + 128 * i, 128) for i in range(4))
    tabc, tabs, tmpt = area(R + 512, 1024), area(R + 1536, 1024), area(R + 2560, 512)
    bb_ = [area(R + 3072 + 512 * i, 512) for i in range(2)]
    bj_ = [area(R + 4096 + 512 * i, 512) for i in range(2)]
    zz = area(R + 5120, 2048)

    def g_tables():
        tm_ = None
        for dst, l, r in ((wt, M("bw"), C("ft")), (wjt, M("bw"), C("jft")), (gt_, C("fi"), M("cw")),
                          (gjt, C("fij"), M("cw"))):
            b = take()
            tp = mm(ps[:, b, 0:128], l, r, t_ml, *free[b])
            tm_ = cp(dve, dst, ps[:, b, 0:128], tp)
            free[b] = [tm_]
            yield
        tk["mats"] = tm_
        b = take()
        tp = mm(ps[:, b, 0:1], C("sm")[0:64, :], M("asc")[0:64, :], t_ml, *free[b])
        om, w2_, dn, rd, cr, ci, u1, u2 = (scn[:, i:i + 1] for i in range(8))
        t = cp(dve, om, ps[:, b, 0:1], tp)
        free[b] = [t]
        t = tt(dve, w2_, om, om, ALU.mult, t)
        t = ts(dn, w2_, 1.0, None, ALU.add, None, t)
        t = dve(lambda e: e.reciprocal(rd, dn), t)
        t = ts(cr, w2_, -1.0, 1.0, ALU.mult, ALU.add, t)
        t = tt(dve, cr, cr, rd, ALU.mult, t)
        t = ts(ci, om, -2.0, None, ALU.mult, None, t)
        t = tt(dve, ci, ci, rd, ALU.mult, t)
        dve.quiet(lambda e: e.memset(tabs[:, 0:1], 0.0))
        t = dve(lambda e: e.memset(tabc[:, 0:1], 1.0), t)
        m = 1
        while m < 1024:
            t = ts(tmpt[:, 0:m], tabs[:, 0:m], ci, None, ALU.mult, None, t)
            t = stt(tabc[:, m:2 * m], tabc[:, 0:m], cr, tmpt[:, 0:m], ALU.mult, ALU.subtract, t)
            t = ts(tmpt[:, 0:m], tabc[:, 0:m], ci, None, ALU.mult, None, t)
            t = stt(tabs[:, m:2 * m], tabs[:, 0:m], cr, tmpt[:, 0:m], ALU.mult, ALU.add, t)
            m *= 2
            if m < 1024:
                t = tt(dve, u1, ci, ci, ALU.mult, t)
                t = tt(dve, u2, cr, ci, ALU.mult, t)
                t = stt(cr, cr, cr, u1, ALU.mult, ALU.subtract, t)
                t = ts(ci, u2, 2.0, None, ALU.mult, None, t)
            yield
        tk["tab"] = t

    def g_rec(c):
        yield from until(("xn", 1, c), "tab", "mats", *([("recout", c - 2)] if c > 1 else []))
        x_ = xnT[:, CW * c:CW * c + CW]
        k0 = 512 * (c % 2)
        tc_, tn_ = tabc[:, k0:k0 + 512], tabs[:, k0:k0 + 512]
        bb, bj, z = bb_[c % 2], bj_[c % 2], zz[:, CW * c:CW * c + CW]
        b = take()
        tp = mm(ps[:, b, :], wt, x_, tk["mats"], tk["xn", 1, c], *free[b])
        t1 = tt(dve, bb, tc_, ps[:, b, :], ALU.mult, tp, tk["tab"], tk.get(("recout", c - 2)))
        free[b] = [t1]
        yield
        b = take()
        tp = mm(ps[:, b, :], wjt, x_, *free[b])
        t1 = tt(dve, bj, tn_, ps[:, b, :], ALU.mult, tp)
        free[b] = [t1]
        yield
        t = tt(dve, bb, bb, bj, ALU.add, t1)
        init = 0.0 if c % 2 == 0 else zz[:, CW * c - 1:CW * c]
        t = dve(lambda e: e.tensor_tensor_scan(z, bb, bb, init, ALU.add, ALU.bypass), t)
        yield
        t = tt(dve, bb, tc_, z, ALU.mult, t)
        t = tt(dve, bj, tn_, z, ALU.mult, t)
        yield
        b = take()
        mm(ps[:, b, :], gt_, bb, t, *free[b], stop=False)
        tp = mm(ps[:, b, :], gjt, bj, start=False)
        t = stt(bb, x_, M("dcol"), ps[:, b, :], ALU.mult, ALU.add, tp)
        free[b] = [t]
        tk["s", 1, c] = t
        yield

    def g_end1(c):
        yield from until(("s", 1, c), ("gT", 1, c))
        bb = bb_[c % 2]
        t = tt(dve, bb, bb, gT[:, CW * c:CW * c + CW], ALU.mult, tk["s", 1, c], tk["gT", 1, c])
        yield
        yield from g_combine(1, c, bb, t)
        tk["recout", c] = tk["tr", 1, c]

    def g_ffn2(c):
        yield from until(("xn", 2, c), "pos", "b2")
        while tk.get("bank5"):
            yield "blocked"
        tk["bank5"] = True
        x_ = xnT[:, CW * c:CW * c + CW]
        c0 = CW * (c % 2)
        for e8 in range(NE):
            b = take()
            sp = mm(ps[:, b, :], cb[0:24, 128 + 128 * e8:256 + 128 * e8], gTT2[0:24, c0:c0 + CW],
                    tk["pos"], *free[b])
            xb = psum_sb[:, 512 * (e8 % 2):512 * (e8 % 2) + 512]
            t = tt(dve, xb, x_, ps[:, b, :], ALU.mult, sp, tk["xn", 2, c], tk.get(("xb", e8 % 2)))
            free[b] = [t]
            yield
            tk["xb", e8 % 2] = mm(ps[:, 5, :], w2l[:, 128 * e8:128 * e8 + 128], xb, t, tk["late"],
                                  *(free[5] if e8 == 0 else []), start=(e8 == 0), stop=False)
        for i in range(3):
            tp = mm(ps[:, 5, :], bp2[i], gTT2[0:24, c0:c0 + CW], tk["b2"], start=False, stop=(i == 2))
        t = af(gT[:, CW * c:CW * c + CW], ps[:, 5, :], ACT.Silu, tp)
        free[5] = [t]
        tk["bank5"] = False
        tk["gT", 2, c] = t
        yield

    def g_tile(i):
        k, c = i % 2, i // 4
        yield from until(("xn", 2, c), "pos")
        q_, s, ls = qkv[k], sc2[k], st2[k][:, 16:32]
        mx = st2[k][:, 0:16]
        s3_ = s.rearrange("p (h g) -> p h g", g=16)
        b = take()
        tp = mm(ps[:, b, 0:384], xnT[:, 128 * i:128 * i + 128], wA[:, 0:384], tk["xn", 2, c], t_ml, *free[b])
        t = acp(q_, ps[:, b, 0:384], tp, tk.get(("p2", k)), tk.get(("p2g", k)))
        free[b] = [t]
        q4 = q_[:, 0:128].rearrange("p (h d) -> p h d", d=8).unsqueeze(2).to_broadcast([128, 16, 16, 8])
        k4 = q_[:, 128:256].rearrange("p (g d) -> p g d", d=8).unsqueeze(1).to_broadcast([128, 16, 16, 8])
        t = tt(pool, pr1[k].rearrange("p (h g d) -> p h g d", h=16, g=16), q4, k4, ALU.mult, t,
               tk.get(("r1", k)), tk["pe_read"])
        yield PAUSE
        p1 = pr1[k].rearrange("p (a d) -> p a d", d=8)
        t1 = red(s[:, 0:128], p1[:, 0:128, :], ALU.add, t)
        yield
        t = red(s[:, 128:256], p1[:, 128:256, :], ALU.add, t1)
        tk["r1", k] = t
        t = red(mx, s3_, ALU.max, t, negate=True)
        t = tt(dve, s3_, s3_, mx.unsqueeze(2).to_broadcast([128, 16, 16]), ALU.add, t)
        yield
        t = af(s, s, ACT.Exp, t, scale=0.125)
        yield
        v4 = q_[:, 256:384].rearrange("p (g d) -> p d g", d=8).unsqueeze(1)
        s4 = s3_.unsqueeze(2)
        o4 = pr2[k].rearrange("p (h d g) -> p h d g", h=16, d=8)
        n1, n2 = HD, 16 - HD
        tg = tk["p2g", k] = tt(pool, o4[:, n1:16, :, :], s4[:, n1:16, :, :].to_broadcast([128, n2, 8, 16]),
                               v4.to_broadcast([128, n2, 8, 16]), ALU.mult, t, tk.get(("r2", k)))
        t0 = red(ls, s3_, ALU.add, t)
        t0 = dve(lambda e: e.reciprocal(ls, ls), t0)
        yield
        td = tk["p2", k] = tt(dve, o4[:, 0:n1, :, :], s4[:, 0:n1, :, :].to_broadcast([128, n1, 8, 16]),
                              v4.to_broadcast([128, n1, 8, 16]), ALU.mult, t, tk.get(("r2", k)))
        yield PAUSE
        p2 = pr2[k].rearrange("p (a g) -> p a g", g=16)
        t = red(ot2[k][:, 0:64], p2[:, 0:64, :], ALU.add, td, tg, tk.get(("trt", k)))
        yield
        t = tk["r2", k] = red(ot2[k][:, 64:128], p2[:, 64:128, :], ALU.add, tg, t)
        t = tt(dve, v3(ot2[k], 8), v3(ot2[k], 8), bc8(ls), ALU.mult, t, t0)
        yield
        b = take()
        tp = tk["trt", k] = tr(ps[:, b, 0:128], ot2[k], ident, t, *free[b])
        t = acp(oT2[c % 2][:, 128 * (i % 4):128 * (i % 4) + 128], ps[:, b, 0:128], tp, tk.get(("proj", c - 2)))
        free[b] = [t]
        tk["tile", i] = t
        yield

    def g_end2(c):
        yield from until(*[("tile", 4 * c + j) for j in range(4)], ("gT", 2, c))
        b = take()
        tp = tk["proj", c] = mm(ps[:, b, :], wA[:, 384:512], oT2[c % 2], tk["tile", 4 * c + 3],
                                tk["tile", 4 * c + 2], *free[b])
        a = acc_sb[:, 1024:1536]
        t = stt(a, ps[:, b, :], M("bp"), gT[:, CW * c:CW * c + CW], ALU.add, ALU.mult, tp, tk["gT", 2, c],
                tk.get(("tr", 2, c - 1)))
        free[b] = [t]
        yield
        yield from g_combine(2, c, a, t)

    qT3, kT3, v3_ = area(R, 1024), area(R + 1024, 1024), area(R + 2048, 1024)
    scb = [area(R + 3072 + 512 * i, 512) for i in range(4)]
    dt_sb = area(R + 5120, 1024)
    d_dt = Dma(queues, sem("d_dt"))
    d_out = Dma(queues, sem("d_out"))
    ov = out.rearrange("b (t p) d -> p (b t) d", p=128)
    ex = scn[:, 0:1]

    def g_l3start():
        yield from until(("x", 2, 3), ("x", 2, 2))
        w_ = [tk["x", 2, 3], tk["x", 2, 2], tk["tr", 1, 3]]
        tk["dt"] = d_dt(dt_sb, A["cf"][:, CF_KEPT + 1024:CF_N], *w_)
        t = ts(ex, M("th"), 0.0, None, ALU.mult, None, *w_)
        tk["ex"] = af(ex, ex, ACT.Exp, t)
        yield

    def g_att3(c):
        yield from until(("xn", 3, c), "ex")
        hf = c % 2
        x_ = xnT[:, CW * c:CW * c + CW]
        o_ = 512 * hf
        w_ = [tk["dt"], tk.get(("pv3", c - 1))] if hf == 0 else []
        for w3_, dst in ((M("wq"), qT3), (M("wk"), kT3)):
            b = take()
            tp = mm(ps[:, b, :], w3_, x_, tk["xn", 3, c], *free[b])
            t = ts(dst[:, o_:o_ + 512], ps[:, b, :], ex, None, ALU.mult, None, tp, tk["ex"], *w_)
            free[b] = [t]
            yield
        t_qk = t
        b = take()
        for j in range(4):
            i0 = CW * c + 128 * j
            tp = mm(ps[:, b, 128 * j:128 * j + 128], xnT[:, i0:i0 + 128], M("wv"), *free[b])
        t_v = acp(v3_[:, o_:o_ + 512], ps[:, b, :], tp, *w_)
        free[b] = [t_v]
        yield
        while tk.get("bank5"):
            yield "blocked"
        tk["bank5"] = True
        nb = 4 * (hf + 1)
        pend3 = []

        def pv3(jb, i0, t):
            tk["pv3", c] = tk["scb", jb % 4] = mm(
                ps[:, 5, i0:512], v3_[:, 128 * jb:128 * jb + 128], scb[jb % 4][:, i0:512], t, t_v,
                *(free[5] if jb == 0 else []), start=(jb == 0), stop=(jb == nb - 1))

        for jb in range(nb):
            i0 = max(0, 128 * jb - o_)
            b = take()
            tp = mm(ps[:, b, i0:512], kT3[:, 128 * jb:128 * jb + 128], qT3[:, o_ + i0:o_ + 512], t_qk, *free[b])
            d0 = o_ + i0 - 128 * jb
            t = tt(dve, scb[jb % 4][:, i0:512], ps[:, b, i0:512], dt_sb[:, d0:d0 + 512 - i0], ALU.mult, tp,
                   tk["dt"], tk.get(("scb", jb % 4)))
            free[b] = [t]
            pend3.append((jb, i0, t))
            if len(pend3) > 1:
                pv3(*pend3.pop(0))
            yield
        pv3(*pend3.pop(0))
        a = acc_sb[:, 1536:2048]
        while ("gT", 3, c) not in tk:
            yield "blocked"
        t = tt(dve, a, ps[:, 5, :], gT[:, CW * c:CW * c + CW], ALU.mult, tk["pv3", c], tk["gT", 3, c],
               tk.get(("tr", 3, c - 1)))
        free[5] = [t]
        tk["bank5"] = False
        yield
        yield from g_combine(3, c, a, t)
        tk["out"] = d_out(ov[:, 4 * c:4 * c + 4, :], xs[:, 4 * c:4 * c + 4, :], tk["x", 4, c])

    lanes += [
        lane(g_tail0(), *[x for c in range(2, NC) for x in (g_end0(c), g_ln(1, c, lt1[c]), g_gates(1, c))],
             *[x for c in range(NC) for x in (g_end1(c), g_ln(2, c, lt[0]), g_ffn2(c))]),
        lane(g_tables(), g_rec(0), g_rec(1), g_bias("b2", bp2, "b2"), g_bias("b3", bp3, "b3"), g_position(),
             g_rec(2), g_rec(3), g_l3start(), *[g_att3(c) for c in range(NC)]),
        lane(*[g_tile(i) for i in range(0, NT, 2)]),
        lane(*[g_tile(i) for i in range(1, NT, 2)]),
        lane(*[x for c in range(NC) for x in (g_end2(c), g_ln(3, c, lt[1]), g_gates(3, c))]),
    ]
    seq = [(1, c, e8) for c in range(NC) for e8 in range(NE)] + [(3, c, e8) for c in range(NC) for e8 in range(NE)]
    tg_tok, tg_free, s_free, h_free, pend = {}, {}, {}, {}, []

    def gate_of(i):
        layer, c, e8 = seq[i]
        b = take()
        buf = tg_buf[i % 2]
        x_ = xnT[:, CW * c:CW * c + CW]
        src = (gTT1 if layer == 1 else gTT3)[0:24, CW * c:CW * c + CW]
        t = mm(ps[:, b, :], cb[0:24, 128 + 128 * e8:256 + 128 * e8], src, tk["g", layer, c], *free[b])
        if layer == 1:
            t = tt(dve, buf, x_, ps[:, b, :], ALU.mult, t, tk["xn", 1, c], tg_free.get(i % 2))
        else:
            t = acp(buf, ps[:, b, :], t, tg_free.get(i % 2))
        free[b] = [t]
        tg_tok[i] = t

    def block(i, f, n):
        layer, c, e8 = seq[i]
        buf, h, s1 = tg_buf[i % 2], h_buf[n % 4], s_buf[n % 2]
        w_ = W[e8]
        if layer == 1:
            m = (128, 128, 96)[f]
            ba, bb2 = (0, 1) if n % 2 == 0 else (2, 3)
            ta = mm(ps[0:m, ba, :], w_[:, 128 * f:128 * f + m], buf, tg_tok[i], tk["w1b"] if e8 == 7 else t_w1a[-1],
                    *free[ba])
            tb = mm(ps[0:m, bb2, :], w_[:, 352 + 128 * f:352 + 128 * f + m], buf, *free[bb2])
            tg_free[i % 2] = tb
            t = af(s1[0:m, :], ps[0:m, ba, :], ACT.Silu, ta, s_free.get(n % 2))
            free[ba] = [t]
            t = tt(dve, h[0:m, :], s1[0:m, :], ps[0:m, bb2, :], ALU.mult, t, tb, h_free.get(n % 4))
            free[bb2] = [t]
            s_free[n % 2] = t
            wd = w_[0:m, 704 + 128 * f:832 + 128 * f]
            nf = 3
        else:
            m = 128
            bk = n % 4
            ta = mm(ps[:, bk, :], w_[:, 128 * f:128 * f + 128], xnT[:, CW * c:CW * c + CW], tk["w3", e8],
                    tk["xn", 3, c], *free[bk])
            k = 4 * e8 + f
            t = af(s1, ps[:, bk, :], ACT.Silu, ta, s_free.get(n % 2), bias=M("b1c")[:, k:k + 1])
            free[bk] = [t]
            t = tt(dve, h, s1, buf, ALU.mult, t, tg_tok[i], h_free.get(n % 4))
            s_free[n % 2] = tg_free[i % 2] = t
            wd = w_[:, 512 + 128 * f:640 + 128 * f]
            nf = 4
        first, last = (e8 == 0 and f == 0), (e8 == NE - 1 and f == nf - 1)

        def down():
            t3 = mm(ps[:, 4, :], wd, h[0:m, :], t, *(free[4] if first else []),
                    start=first, stop=last and layer == 1)
            h_free[n % 4] = t3
            if layer == 1 and c == NC - 1 and f == nf - 1:
                tk["w3", e8] = d_w3[e8](W[e8][:, 0:1024], A["L3_w"][:, 1024 * e8:1024 * e8 + 1024], t3)
            if last:
                if layer == 3:
                    for q in range(3):
                        t3 = mm(ps[:, 4, :], bp3[q], gTT3[0:24, CW * c:CW * c + CW], tk["b3"],
                                start=False, stop=(q == 2))
                t4 = af(gT[:, CW * c:CW * c + CW], ps[:, 4, :], ACT.Silu, t3)
                free[4] = [t4]
                tk["gT", layer, c] = t4
        pend.append(down)

    n = 0
    for i, (layer, c, e8) in enumerate(seq):
        if i not in tg_tok:
            need(("g", layer, c))
            if layer == 3:
                need("b3")
            gate_of(i)
        for f in range(3 if layer == 1 else 4):
            block(i, f, n)
            n += 1
            steps(B1 if layer == 1 else B3)
            if len(pend) > 2:
                pend.pop(0)()
            if f == 1 and i + 1 < len(seq) and ("g",) + seq[i + 1][:2] in tk:
                gate_of(i + 1)
    while pend:
        pend.pop(0)()
    while lanes:
        assert steps(4.0)
    finish(tk["out"])


def constants():
    f = np.zeros((128, CF_N), np.float64)

    def put(name, a):
        o, _ = CF_COLS[name]
        f[:a.shape[0], o:o + a.shape[1]] = a

    put("ident", np.eye(128))
    n = np.arange(128)[:, None]
    k = np.arange(64)[None, :]
    w = 2 * np.pi * n * k / 128
    F = np.concatenate([np.cos(w), -np.sin(w)], 1)
    F[:, 64] = (-1.0) ** np.arange(128)
    J = np.zeros((128, 128))
    for i in range(1, 64):
        J[i, 64 + i] = 1
        J[64 + i, i] = -1
    Fi = np.concatenate([2 * np.cos(w), -2 * np.sin(w)], 1) / 128
    Fi[:, 0] = 1 / 128
    Fi[:, 64] = (-1.0) ** np.arange(128) / 128
    put("ft", F)
    put("jft", F @ J.T)
    put("fi", Fi)
    put("fij", -(Fi @ J))
    j = np.arange(1, 65)[:, None]
    s = -2 * np.sin(2 * np.pi * j * k / 128)
    s[63] = 0
    S = np.concatenate([s, s], 1)
    put("sm", S)
    pos = np.arange(1024, dtype=np.float32)[:, None]
    div = np.exp(np.arange(0, 32, 2, dtype=np.float32) * np.float32(-np.log(10000.0) / 32)).astype(np.float32)
    ang = (pos * div).astype(np.float32)
    pe = np.zeros((1024, 32), np.float32)
    pe[:, 0::2] = np.sin(ang)
    pe[:, 1::2] = np.cos(ang)
    put("pe", pe.T)
    i = np.arange(1024)[None, :] - np.arange(128)[:, None]
    put("dt", np.where(i >= 0, 0.96875 ** np.maximum(i, 0).astype(np.float64), 0.0))
    put("w8", np.tile(8.0 - np.arange(8), (128, 1)))
    one = 0x3F80
    b = np.zeros((128, CB_N), np.uint16)
    b[:, 0:128] = one * np.eye(128, dtype=np.uint16)
    for e in range(NE):
        for r in range(3):
            b[8 * r + e, 128 + 128 * e:256 + 128 * e] = one
    return f.astype(np.float32), b


def layouts(a):
    def blocks(w, k):
        return np.ascontiguousarray(w.reshape(-1, k, w.shape[-1]).transpose(1, 0, 2).reshape(k, -1))

    d = {"x": a["L0_attn_representations"]}
    Wc = a["L0_attn_Wc"]
    d["L0_WcT"] = Wc.T
    d["L0_WoT"] = blocks(a["L0_attn_Wo"].T, 128)
    d["L0_bqk"] = a["L0_attn_bc"][:256].reshape(2, 128).T
    d["L0_bv"] = a["L0_attn_bc"][256:]
    d["L0_bo"] = a["L0_attn_bo"][:, None]
    d["L0_Wg"] = a["L0_ffn_Wg"].T
    d["L0_w1"] = a["L0_ffn_W1"].reshape(2048, 128).T
    d["L0_w2"] = a["L0_ffn_W2"].reshape(2048, 128).T
    d["L0_w3"] = blocks(a["L0_ffn_W3"].transpose(0, 2, 1).reshape(2048, 128), 128)
    w2 = np.zeros((8, 384, 128), np.float32)
    w2[:, :352] = a["L1_ffn_w2"]
    d["L1_w"] = np.concatenate([np.concatenate([a["L1_ffn_w1"][e], a["L1_ffn_w3"][e], blocks(w2[e], 128)], 1)
                                for e in range(8)], 1)
    d["L3_w"] = np.concatenate([np.concatenate([a["L3_ffn_W1"][e], blocks(a["L3_ffn_W2"][e], 128)], 1)
                                for e in range(8)], 1)
    d["L2_W"] = a["L2_ffn_W"].transpose(2, 0, 1).reshape(128, -1)
    w = a["L2_attn_Wqkv"].reshape(16, 3, 8, 128).transpose(1, 0, 2, 3).reshape(384, 128)
    parts = {"wqkvp": np.concatenate([w.T, a["L2_attn_Wproj"].T], 1), "wq": a["L3_attn_weight_q"],
             "wk": a["L3_attn_weight_k"], "wv": a["L3_attn_weight_v"], "bw": a["L1_attn_B_w"],
             "cw": a["L1_attn_C_w"].T, "wg1": a["L1_ffn_gate_w"].T, "wg3": a["L3_ffn_Wg"],
             "b1c": a["L3_ffn_b1"].reshape(32, 128).T, "th": a["L3_attn_theta"][:, None],
             "asc": a["L1_attn_a_params"][:, None], "dcol": a["L1_attn_D"][:, None],
             "bp": a["L2_attn_bproj"][:, None], "eb": np.tile(a["L1_ffn_expert_bias"], (128, 1)),
             "bg": np.tile(a["L3_ffn_bg"], (128, 1)), "sig": a["L2_ffn_tile_sigs"].T,
             "b2": np.tile(a["L2_ffn_b"], (3, 1)), "b3": np.tile(a["L3_ffn_b2"], (3, 1))}
    misc = np.zeros((128, MISC_N), np.float32)
    for k, v in parts.items():
        misc[:v.shape[0], MISC_COLS[k][0]:MISC_COLS[k][0] + v.shape[1]] = v
    d["misc"] = misc
    return {k: np.ascontiguousarray(v) for k, v in d.items()}


def kernel(**inputs):
    import concourse.bacc as bacc
    from concourse.bass_utils import run_bass_kernel_spmd

    a = layouts({k: np.asarray(v) for k, v in inputs.items()})
    a["cf"], a["cb"] = constants()
    nc = bacc.Bacc("TRN2", target_bir_lowering=False, num_devices=1)
    arrays, aps = {}, {}
    for name, v in a.items():
        arrays["in_" + name] = v
        aps[name] = nc.dram_tensor("in_" + name, v.shape, mybir.dt.from_np(v.dtype), kind="ExternalInput").ap()
    out = nc.dram_tensor("out_0", (2, 1024, 128), F32, kind="ExternalOutput").ap()
    program(nc, aps, out)
    r = run_bass_kernel_spmd(nc, [arrays], core_ids=[0])
    return r.results[0]["out_0"]
```
